# Optimizing a Trainium2 kernel written in Bass

```python
import numpy as np
import jax
import jax.numpy as jnp

def _softmax(x, axis=-1):
    return jax.nn.softmax(x, axis=axis)

def _gelu(x):
    return jax.nn.gelu(x, approximate=True)

def _silu(x):
    return jax.nn.silu(x)

def _sigmoid(x):
    return jax.nn.sigmoid(x)

def _layernorm(x, axis=-1, eps=1e-05):
    m = jnp.mean(x, axis=axis, keepdims=True)
    v = jnp.var(x, axis=axis, keepdims=True)
    return (x - m) / jnp.sqrt(v + eps)

def _scatter_add(tgt, idx, src, axis=0):
    return tgt.at[idx].add(src)

def _segment_sum(src, seg, n):
    return jax.ops.segment_sum(src, seg, n)
kernel_name = 'mk_hybrid_d1_jaxref_r8_b96e72'

def setup_inputs(seed: int=0):
    np.random.seed(seed)
    _w = jnp.asarray

    def _L0_attn_a_setup():
        import jax, jax.numpy as jnp
        import numpy as np
        D_MODEL = 128
        SCALE = float(np.sqrt(D_MODEL))
        key = jax.random.key(seed)
        k1, k2, k3 = jax.random.split(key, 3)
        input_data = jax.random.normal(k1, (4, 256, D_MODEL), dtype=jnp.float32)
        qk = jax.random.normal(k2, (D_MODEL, D_MODEL), dtype=jnp.float32) / SCALE
        ov = jax.random.normal(k3, (D_MODEL, D_MODEL), dtype=jnp.float32) / SCALE
        return {'input_data': input_data, 'qk': qk, 'ov': ov}
    _L0_attn_a_in = _L0_attn_a_setup()

    def _L0_attn_b_setup():
        import jax, jax.numpy as jnp
        import numpy as np
        EPS = 1e-05

        def layernorm(x, g, b):
            m = x.mean(-1, keepdims=True)
            v = x.var(-1, keepdims=True)
            return (x - m) / jnp.sqrt(v + EPS) * g + b

        def mamba(x, w_in, w_conv, b_conv, w_xproj, w_dt, b_dt, A_log, Dp, w_out):
            B, L, _ = x.shape
            d_inner, d_conv = w_conv.shape
            dt_rank = w_dt.shape[0]
            N = A_log.shape[1]
            xz = x @ w_in
            xm, z = jnp.split(xz, 2, axis=-1)
            xc = xm.transpose(0, 2, 1)
            xc = jax.lax.conv_general_dilated(xc, w_conv[:, None, :], window_strides=(1,), padding=[(d_conv - 1, 0)], feature_group_count=d_inner, dimension_numbers=('NCH', 'OIH', 'NCH'))
            xc = xc + b_conv[None, :, None]
            xm = jax.nn.silu(xc.transpose(0, 2, 1))
            proj = xm @ w_xproj
            dt = proj[..., :dt_rank]
            Bc = proj[..., dt_rank:dt_rank + N]
            Cc = proj[..., dt_rank + N:]
            delta = jax.nn.softplus(dt @ w_dt + b_dt)
            A = -jnp.exp(A_log)
            deltaA = jnp.exp(delta[..., None] * A)
            deltaBu = delta[..., None] * Bc[:, :, None, :] * xm[..., None]

            def step(h, inp):
                a, b, c = inp
                h = a * h + b
                y = (h * c[:, None, :]).sum(-1)
                return (h, y)
            h0 = jnp.zeros((B, d_inner, N), x.dtype)
            _, ys = jax.lax.scan(step, h0, (deltaA.transpose(1, 0, 2, 3), deltaBu.transpose(1, 0, 2, 3), Cc.transpose(1, 0, 2)))
            y = ys.transpose(1, 0, 2) + xm * Dp
            y = y * jax.nn.silu(z)
            return y @ w_out
        key = jax.random.key(seed)
        ks = jax.random.split(key, 8)
        d_model, d_inner, N, d_conv, dt_rank, d_ff = (128, 256, 16, 4, 64, 512)
        B, L = (2, 128)
        s = lambda d: 1.0 / np.sqrt(d)
        return {'x': jax.random.normal(ks[0], (B, L, d_model), jnp.float32), 'ln1_g': jnp.ones((d_model,), jnp.float32), 'ln1_b': jnp.zeros((d_model,), jnp.float32), 'w_in': jax.random.normal(ks[1], (d_model, 2 * d_inner), jnp.float32) * s(d_model), 'w_conv': jax.random.normal(ks[2], (d_inner, d_conv), jnp.float32) * s(d_conv), 'b_conv': jnp.zeros((d_inner,), jnp.float32), 'w_xproj': jax.random.normal(ks[3], (d_inner, dt_rank + 2 * N), jnp.float32) * s(d_inner), 'w_dt': jax.random.normal(ks[4], (dt_rank, d_inner), jnp.float32) * s(dt_rank), 'b_dt': jnp.zeros((d_inner,), jnp.float32), 'A_log': jnp.tile(jnp.log(jnp.arange(1, N + 1, dtype=jnp.float32)), (d_inner, 1)), 'Dp': jnp.ones((d_inner,), jnp.float32), 'w_out': jax.random.normal(ks[5], (d_inner, d_model), jnp.float32) * s(d_inner), 'ln2_g': jnp.ones((d_model,), jnp.float32), 'ln2_b': jnp.zeros((d_model,), jnp.float32), 'w_ff1': jax.random.normal(ks[6], (d_model, d_ff), jnp.float32) * s(d_model), 'b_ff1': jnp.zeros((d_ff,), jnp.float32), 'w_ff2': jax.random.normal(ks[7], (d_ff, d_model), jnp.float32) * s(d_ff), 'b_ff2': jnp.zeros((d_model,), jnp.float32)}
    _L0_attn_b_in = _L0_attn_b_setup()

    def _L0_ffn_setup():
        import jax, jax.numpy as jnp
        import numpy as np
        key = jax.random.key(seed)
        k0, k1, k2, k3 = jax.random.split(key, 4)
        B, S, D, F, E = (8, 256, 128, 256, 8)
        x = jax.random.normal(k0, (B, S, D), dtype=jnp.float32)
        Wg = jax.random.normal(k1, (D, E), dtype=jnp.float32) * 0.02
        W1 = jax.random.normal(k2, (E, D, F), dtype=jnp.float32) * 0.02
        W2 = jax.random.normal(k3, (E, F, D), dtype=jnp.float32) * 0.02
        return {'x': x, 'Wg': Wg, 'W1': W1, 'W2': W2}
    _L0_ffn_in = _L0_ffn_setup()
    _d = {'L0_attn_a_input_data': _L0_attn_a_in['input_data'], 'L0_attn_a_qk': _L0_attn_a_in['qk'], 'L0_attn_a_ov': _L0_attn_a_in['ov'], 'L0_attn_b_ln1_g': _L0_attn_b_in['ln1_g'], 'L0_attn_b_ln1_b': _L0_attn_b_in['ln1_b'], 'L0_attn_b_w_in': _L0_attn_b_in['w_in'], 'L0_attn_b_w_conv': _L0_attn_b_in['w_conv'], 'L0_attn_b_b_conv': _L0_attn_b_in['b_conv'], 'L0_attn_b_w_xproj': _L0_attn_b_in['w_xproj'], 'L0_attn_b_w_dt': _L0_attn_b_in['w_dt'], 'L0_attn_b_b_dt': _L0_attn_b_in['b_dt'], 'L0_attn_b_A_log': _L0_attn_b_in['A_log'], 'L0_attn_b_Dp': _L0_attn_b_in['Dp'], 'L0_attn_b_w_out': _L0_attn_b_in['w_out'], 'L0_attn_b_ln2_g': _L0_attn_b_in['ln2_g'], 'L0_attn_b_ln2_b': _L0_attn_b_in['ln2_b'], 'L0_attn_b_w_ff1': _L0_attn_b_in['w_ff1'], 'L0_attn_b_b_ff1': _L0_attn_b_in['b_ff1'], 'L0_attn_b_w_ff2': _L0_attn_b_in['w_ff2'], 'L0_attn_b_b_ff2': _L0_attn_b_in['b_ff2'], 'L0_ffn_Wg': _L0_ffn_in['Wg'], 'L0_ffn_W1': _L0_ffn_in['W1'], 'L0_ffn_W2': _L0_ffn_in['W2']}
    _x0 = _d['L0_attn_a_input_data']
    _d['L0_attn_a_input_data'] = jax.random.normal(jax.random.fold_in(jax.random.key(seed), 1), (16, 256, 128), dtype=_x0.dtype)
    del _x0
    return _d

def reference(L0_attn_a_input_data, L0_attn_a_qk, L0_attn_a_ov, L0_attn_b_ln1_g, L0_attn_b_ln1_b, L0_attn_b_w_in, L0_attn_b_w_conv, L0_attn_b_b_conv, L0_attn_b_w_xproj, L0_attn_b_w_dt, L0_attn_b_b_dt, L0_attn_b_A_log, L0_attn_b_Dp, L0_attn_b_w_out, L0_attn_b_ln2_g, L0_attn_b_ln2_b, L0_attn_b_w_ff1, L0_attn_b_b_ff1, L0_attn_b_w_ff2, L0_attn_b_b_ff2, L0_ffn_Wg, L0_ffn_W1, L0_ffn_W2):

    def _L0_attn_a_ref(input_data, qk, ov):
        import jax, jax.numpy as jnp
        import numpy as np
        D_MODEL = 128
        SCALE = float(np.sqrt(D_MODEL))
        S = input_data.shape[1]
        scores = jnp.einsum('bsd,de,bte->bst', input_data, qk, input_data) / SCALE
        causal = jnp.tril(jnp.ones((S, S), dtype=bool))
        scores = jnp.where(causal, scores, -jnp.inf)
        attn = jax.nn.softmax(scores, axis=-1)
        return jnp.einsum('bst,btd,de->bse', attn, input_data, ov)

    def _L0_attn_b_ref(x, ln1_g, ln1_b, w_in, w_conv, b_conv, w_xproj, w_dt, b_dt, A_log, Dp, w_out, ln2_g, ln2_b, w_ff1, b_ff1, w_ff2, b_ff2):
        import jax, jax.numpy as jnp
        import numpy as np
        EPS = 1e-05

        def layernorm(x, g, b):
            m = x.mean(-1, keepdims=True)
            v = x.var(-1, keepdims=True)
            return (x - m) / jnp.sqrt(v + EPS) * g + b

        def mamba(x, w_in, w_conv, b_conv, w_xproj, w_dt, b_dt, A_log, Dp, w_out):
            B, L, _ = x.shape
            d_inner, d_conv = w_conv.shape
            dt_rank = w_dt.shape[0]
            N = A_log.shape[1]
            xz = x @ w_in
            xm, z = jnp.split(xz, 2, axis=-1)
            xc = xm.transpose(0, 2, 1)
            xc = jax.lax.conv_general_dilated(xc, w_conv[:, None, :], window_strides=(1,), padding=[(d_conv - 1, 0)], feature_group_count=d_inner, dimension_numbers=('NCH', 'OIH', 'NCH'))
            xc = xc + b_conv[None, :, None]
            xm = jax.nn.silu(xc.transpose(0, 2, 1))
            proj = xm @ w_xproj
            dt = proj[..., :dt_rank]
            Bc = proj[..., dt_rank:dt_rank + N]
            Cc = proj[..., dt_rank + N:]
            delta = jax.nn.softplus(dt @ w_dt + b_dt)
            A = -jnp.exp(A_log)
            deltaA = jnp.exp(delta[..., None] * A)
            deltaBu = delta[..., None] * Bc[:, :, None, :] * xm[..., None]

            def step(h, inp):
                a, b, c = inp
                h = a * h + b
                y = (h * c[:, None, :]).sum(-1)
                return (h, y)
            h0 = jnp.zeros((B, d_inner, N), x.dtype)
            _, ys = jax.lax.scan(step, h0, (deltaA.transpose(1, 0, 2, 3), deltaBu.transpose(1, 0, 2, 3), Cc.transpose(1, 0, 2)))
            y = ys.transpose(1, 0, 2) + xm * Dp
            y = y * jax.nn.silu(z)
            return y @ w_out
        x = x + mamba(layernorm(x, ln1_g, ln1_b), w_in, w_conv, b_conv, w_xproj, w_dt, b_dt, A_log, Dp, w_out)
        h = layernorm(x, ln2_g, ln2_b)
        h = jax.nn.gelu(h @ w_ff1 + b_ff1) @ w_ff2 + b_ff2
        return x + h

    def _L0_ffn_ref(x, Wg, W1, W2):
        import jax, jax.numpy as jnp
        import numpy as np
        B, S, D = x.shape
        E = Wg.shape[1]
        T = B * S
        cap = max(1, T // E)
        xt = x.reshape(T, D)
        logits = xt @ Wg
        probs = jax.nn.softmax(logits, axis=-1)
        pT = probs.T
        _, top_idx = jax.lax.top_k(pT, cap)
        sel = jnp.zeros((E, T), dtype=bool).at[jnp.arange(E)[:, None], top_idx].set(True)
        masked = jnp.where(sel, pT, -jnp.inf)
        assigned = sel.any(axis=0)
        tok2exp = jnp.where(assigned, jnp.argmax(masked, axis=0), jnp.argmax(pT, axis=0))
        weights = jnp.take_along_axis(probs, tok2exp[:, None], axis=1)[:, 0]
        out = jnp.zeros_like(xt)
        for e in range(E):
            gate = jnp.where(tok2exp == e, weights, 0.0)
            h = jax.nn.gelu(xt @ W1[e], approximate=False) @ W2[e]
            out = out + gate[:, None] * h
        return out.reshape(B, S, D)
    x = L0_attn_a_input_data
    x = x + _L0_attn_a_ref(_layernorm(x, axis=-1), L0_attn_a_qk, L0_attn_a_ov)
    x = x + _L0_ffn_ref(_layernorm(x, axis=-1), L0_ffn_Wg, L0_ffn_W1, L0_ffn_W2)
    x = x + _L0_attn_b_ref(_layernorm(x, axis=-1), L0_attn_b_ln1_g, L0_attn_b_ln1_b, L0_attn_b_w_in, L0_attn_b_w_conv, L0_attn_b_b_conv, L0_attn_b_w_xproj, L0_attn_b_w_dt, L0_attn_b_b_dt, L0_attn_b_A_log, L0_attn_b_Dp, L0_attn_b_w_out, L0_attn_b_ln2_g, L0_attn_b_ln2_b, L0_attn_b_w_ff1, L0_attn_b_b_ff1, L0_attn_b_w_ff2, L0_attn_b_b_ff2)
    x = x + _L0_ffn_ref(_layernorm(x, axis=-1), L0_ffn_Wg, L0_ffn_W1, L0_ffn_W2)
    return x

_drawn_inputs = setup_inputs


def setup_inputs(seed=0):
    import zlib

    import numpy as np

    out = dict(_drawn_inputs(seed))
    spreads = {'L0_attn_b_ln1_g': (1.0, 0.2),
     'L0_attn_b_ln1_b': (0.0, 0.1),
     'L0_attn_b_b_conv': (0.0, 0.1),
     'L0_attn_b_b_dt': (0.0, 0.517),
     'L0_attn_b_Dp': (1.0, 0.2),
     'L0_attn_b_ln2_g': (1.0, 0.2),
     'L0_attn_b_ln2_b': (0.0, 0.1),
     'L0_attn_b_b_ff1': (0.0, 0.292),
     'L0_attn_b_b_ff2': (0.0, 0.1)}
    factors = {'L0_ffn_Wg': 6.723, 'L0_ffn_W1': 6.362, 'L0_ffn_W2': 6.316}
    for name, (base, spread) in spreads.items():
        noise = np.random.default_rng([zlib.crc32(name.encode()), seed]).standard_normal(out[name].shape)
        drawn = base * np.exp(spread * noise) if base else spread * noise
        out[name] = jnp.asarray(drawn.astype(out[name].dtype))
    for name, factor in factors.items():
        out[name] = (out[name] * factor).astype(out[name].dtype)
    return out
```

```python
from contextlib import ExitStack

import concourse.bass as bass
from concourse import mybir

P = 128
ALU = mybir.AluOpType
ACT = mybir.ActivationFunctionType
AX = mybir.AxisListType.X
F32 = mybir.dt.float32
BF16 = mybir.dt.bfloat16
I32 = mybir.dt.int32
EPS = 1e-5
MASKED = -1e30
TOP_BIT = 29


class Chain:

    def __init__(self, eng, sem):
        self.eng, self.sem = eng, sem
        self.base, self.i, self.per, self.trips, self.k = 0, None, 0, 0, 0

    def loop(self, i, per, trips):
        self.base += self.k
        self.i, self.per, self.trips, self.k = i, per, trips, 0

    def end(self):
        assert self.k == self.per, (self.k, self.per)
        self.base += self.per * self.trips
        self.i, self.k = None, 0

    def step(self, ins):
        ins.then_inc(self.sem, 1)
        self.k += 1

    def wait(self):
        at = self.base + self.k
        self.eng.wait_ge(self.sem, at if self.i is None else self.i * self.per + at)

    def link(self, ins):
        self.step(ins)
        self.wait()


def hybrid_kernel(nc, x_in, qk, ov, ln1_g, ln1_b, w_in, w_conv, b_conv, w_xproj, w_dt, b_dt, A_log, Dp, w_out,
                  ln2_g, ln2_b, w_ff1, b_ff1, w_ff2, b_ff2, Wg, W1, W2, out, routed_in, routed_out):
    B, S, D = x_in.shape
    T = B * S
    NT = T // P
    E = Wg.shape[1]
    F = W1.shape[2]
    FC = F // P
    CAP = max(1, T // E)
    RT = (T + E * (P - 1)) // P
    DI, TAPS = w_conv.shape
    NB = DI // P
    N = A_log.shape[1]
    R = w_dt.shape[0]
    FF = w_ff1.shape[1]
    FFC = FF // P
    G = 512
    NG = T // G
    GT = G // P
    GB = G // S
    PAD = TAPS - 1
    SP_ = S + PAD
    BC3 = 3 * 2 * N
    assert NT * E == 256 and RT % 3 == 0 and BC3 == 96 and S == 2 * P

    with ExitStack() as ctx:
        def sb(name, shape, dt=F32):
            return ctx.enter_context(nc.sbuf_tensor(name, shape, dt))

        def sem(name):
            return ctx.enter_context(nc.semaphore(name))

        bank = [ctx.enter_context(nc.psum_tensor(f"bank{k}", [P, 512], F32)) for k in range(4)]
        decay_ps = ctx.enter_context(nc.psum_tensor("decay_ps", [P, 2, NB, G], F32))
        bank += [decay_ps[:, s, b, :] for s in range(2) for b in range(NB)]
        bank = [b[:, :] for b in bank]

        X = sb("X", [P, NT, D])

        r_delta = sb("r_delta", [P, NB, T])
        r_du = sb("r_du", [P, NB, T])
        r_xm = sb("r_xm", [P, NB, T])
        r_zs = sb("r_zs", [P, NB, T])
        delta, du, xm, zs = r_delta, r_du, r_xm, r_zs
        W1s = r_du[:, 0, 0:E * F].rearrange("p (e f) -> p e f", e=E)
        W2s = r_du[:, 0, E * F:2 * E * F].rearrange("p (e c d) -> p e c d", e=E, c=FC)
        XN = r_zs[:, 0, :].rearrange("p (j d) -> p j d", j=NT)
        Y = r_zs[:, 1, :].rearrange("p (j d) -> p j d", j=NT)
        XA = r_delta[:, 0, :].rearrange("p (j d) -> p j d", j=NT)

        early = r_delta[:, 1, :]
        mask, qk_s, ov_s = early[:, 0:S], early[:, S:S + D], early[:, S + D:S + 2 * D]
        wconv_row = early[0:1, 512:512 + TAPS * DI].rearrange("p (k c) -> p k c", k=TAPS)
        kcmp = early[:, 1536:1536 + RT * E].rearrange("p (k e) -> p k e", e=E)
        ktab, pos_f = early[:, 1856:1856 + RT], early[:, 1920:1920 + NT]
        e8 = early[:, 1984:2048].rearrange("p (k e) -> p k e", e=E)

        work = sb("work", [P, max(6144, 2048 + B * SP_)])

        def carve(at, *shape):
            n = 1
            for k in shape:
                n *= k
            names = " ".join("abcd"[:len(shape)])
            v = work[:, at:at + n]
            if len(shape) > 1:
                v = v.rearrange(f"p ({names}) -> p {names}", **dict(zip("abcd", shape)))
            return v

        xn_a = carve(0, 2, 2, P)
        xT_a = carve(512, 2, S)
        uv_a = carve(1024, 2, 512)
        sc_a = carve(2048, 2, 384)
        pr_a = carve(2816, 2, 384)
        pT_a = carve(3584, 2, 384)
        xs = carve(0, 2, GT, P)
        xsT = carve(1024, 2, G)
        pe = carve(2048, E, NT)
        prob = carve(2304, E, NT)
        fA = carve(2560, E, NT)
        fB = carve(2816, E, NT)
        fC = carve(3072, E, NT)
        incl = carve(3328, E, NT)
        sel = carve(3584, E, NT)
        tl = carve(3840, NT)
        xin = carve(4096, 3, P)
        rxT = carve(4480, 3, P)
        rh = carve(0, 3, F)
        rhT = carve(768, 3, F)
        ry = carve(1536, 3, P)
        dtT = carve(0, 2, G)
        bcr = carve(1024, 2, G)
        sx = carve(2048, NB, G)
        ab = carve(3072, NB, G)
        ex = carve(4096, NB, G)
        bc_hi = carve(5120, G // 2).bitcast(BF16)[0:BC3]
        xaT = carve(2048, B, SP_)
        dBu = carve(0, NB, G)
        h = carve(1024, 2, NB, G)
        hC = carve(3072, 2, NB, G)
        C_bc = carve(5120, 2, G)
        hT = carve(2048, FFC, G)
        ygs = carve(2048, 2, NB, G)

        ident = sb("ident", [P, P])
        ones_b = sb("ones_b", [P, P], BF16)
        below_b = sb("below_b", [P, P], BF16)
        flag_b = sb("flag_b", [P, E, NT], BF16)
        cnt_b = sb("cnt_b", [P, E], BF16)
        resets = sb("resets", [P, E, NT])
        em8 = sb("em8", [P, E, NT])
        kk = sb("kk", [P, RT, E])
        etab = sb("etab", [P, RT], I32)
        cand = sb("cand", [P, E], I32)
        cand_next = sb("cand_next", [P, E], I32)
        miss = sb("miss", [P, E], I32)
        e8i = sb("e8i", [P, E], I32)
        gate = sb("gate", [P, NT])
        pos = sb("pos", [P, NT], I32)
        one_c = sb("one_c", [P, 1])
        stats = sb("stats", [P, NT, 6])
        mean2 = sb("mean2", [P, NT])
        var4 = sb("var4", [P, NT])
        vv = sb("vv", [P, NT])
        guess = sb("guess", [P, NT], I32)
        t32 = sb("t32", [P, NT])
        rs = sb("rs", [P, NT])
        nmr = sb("nmr", [P, NT])
        rs2 = sb("rs2", [P, NT])
        nmr2 = sb("nmr2", [P, NT])
        nmax = sb("nmax", [P, 2, 2])
        psum_e = sb("psum_e", [P, 2, 2])
        rinv = sb("rinv", [P, 2, 2])

        Wg_s = sb("Wg_s", [P, E])
        g1, b1 = sb("g1", [P, 1]), sb("b1", [P, 1])
        g2, b2 = sb("g2", [P, 1]), sb("b2", [P, 1])
        win_s = sb("win_s", [P, 2 * DI])
        wfold = sb("wfold", [P, TAPS, DI])
        bconv_s = sb("bconv_s", [P, NB])
        wx_s = sb("wx_s", [P, NB, R + 2 * N])
        wbc3 = sb("wbc3", [P, NB, BC3])
        wdt_s = sb("wdt_s", [R, DI])
        bdt_s = sb("bdt_s", [P, NB])
        Aneg = sb("Aneg", [P, NB, N])
        Dp_s = sb("Dp_s", [P, NB])
        diagD = sb("diagD", [P, NB, P])
        wout_s = sb("wout_s", [P, NB, D])
        wff1_s = sb("wff1_s", [P, FF])
        bff1_s = sb("bff1_s", [P, FFC])
        wff2_s = sb("wff2_s", [P, FFC, D])
        bff2_s = sb("bff2_s", [1, D])
        ones_row = sb("ones_row", [1, P])
        pick = sb("pick", [BC3, 2 * N, P], BF16)
        bc_parts = sb("bc_parts", [BC3, T], BF16)

        s_const = sem("s_const")
        s_passed = sem("s_passed")
        s_zeros = sem("s_zeros")
        s_x = sem("s_x")
        s_attn_w = sem("s_attn_w")
        s_weights = sem("s_weights")
        s_experts = [sem(f"s_experts{n}") for n in range(2)]
        s_routed_clear = sem("s_routed_clear")
        v_chain, a_chain, g_chain = sem("v_chain"), sem("a_chain"), sem("g_chain")
        a_xn = sem("a_xn")
        a_xT_ps = sem("a_xT_ps")
        a_xT = sem("a_xT")
        a_uv_ps = sem("a_uv_ps")
        a_uv = sem("a_uv")
        a_sc_ps = sem("a_sc_ps")
        a_max = sem("a_max")
        a_exp = sem("a_exp")
        a_pT_ps = sem("a_pT_ps")
        a_pT = sem("a_pT")
        a_out_ps = sem("a_out_ps")
        s_weights_prep = sem("s_weights_prep")
        s_conv_ps = sem("s_conv_ps")

        class Turn:
            def __init__(self, tag):
                self.xs = sem(f"{tag}_xs")
                self.ps = sem(f"{tag}_ps")
                self.xT = sem(f"{tag}_xT")

        class Ffn:
            def __init__(self, l):
                self.turn = Turn(f"f{l}")
                self.copied = sem(f"f{l}_copied")
                self.logits = sem(f"f{l}_logits")
                self.shifted = sem(f"f{l}_shifted")
                self.exps = sem(f"f{l}_exps")
                self.flags = sem(f"f{l}_flags")
                self.counts = sem(f"f{l}_counts")
                self.routed = sem(f"f{l}_routed")
                self.scattered = sem(f"f{l}_scattered")
                self.loaded = [sem(f"f{l}_loaded{s}") for s in range(3)]
                self.x_ps = sem(f"f{l}_x_ps")
                self.x = sem(f"f{l}_x")
                self.h_ps = sem(f"f{l}_h_ps")
                self.h = sem(f"f{l}_h")
                self.hT_ps = sem(f"f{l}_hT_ps")
                self.hT = sem(f"f{l}_hT")
                self.y_ps = sem(f"f{l}_y_ps")
                self.y = sem(f"f{l}_y")
                self.stored = [sem(f"f{l}_stored{s}") for s in range(3)]
                self.gathered = [sem(f"f{l}_gathered{q}") for q in range(4)]
                self.added = sem(f"f{l}_added")

        ffn = [Ffn(0), Ffn(1)]
        m_turn = Turn("m")
        m_xc_ps = sem("m_xc_ps")
        m_silu = sem("m_silu")
        m_dt_ps = sem("m_dt_ps")
        m_dt = sem("m_dt")
        m_bc_ps = sem("m_bc_ps")
        m_bc = sem("m_bc")
        m_raw_ps = sem("m_raw_ps")
        m_raw = sem("m_raw")
        m_soft = sem("m_soft")
        m_delta = sem("m_delta")
        m_du = sem("m_du")
        c_B = sem("c_B")
        c_C = sem("c_C")
        c_dBu = sem("c_dBu")
        c_decay = sem("c_decay")
        c_h = sem("c_h")
        c_C_sb = sem("c_C_sb")
        c_hC = sem("c_hC")
        c_y = sem("c_y")
        c_gated = sem("c_gated")
        p_yg = sem("p_yg")
        p_out_ps = sem("p_out_ps")
        p_xa = sem("p_xa")
        d_turn = Turn("d")
        d_h_ps = sem("d_h_ps")
        d_h = sem("d_h")
        d_y_ps = sem("d_y_ps")
        d_x = sem("d_x")
        s_out = sem("s_out")

        x_tiles = x_in.rearrange("b (h p) d -> p (b h) d", p=P)
        out_tiles = out.rearrange("b (h p) d -> p (b h) d", p=P)

        def col(v, axis=1):
            return v.unsqueeze(axis)

        def over_tiles(v):
            return col(v, 2).broadcast_to([P, E, NT])

        def over_experts(v):
            return col(v, 1).broadcast_to([P, E, NT])

        def by_tile(v):
            return v.rearrange("p e j -> p j e")

        def apart(eng, semaphore, value):
            eng.wait_ge(semaphore, value)
            eng.sem_inc(s_passed, 1)

        block = ctx.enter_context(nc.Block())

        N_WEIGHTS = 19

        @block.sync
        def _(sp):
            for q in range(4):
                a, b = q * NT // 4, (q + 1) * NT // 4
                sp.dma_start(X[:, a:b, :], x_tiles[:, a:b, :]).then_inc(s_x, 16)
            sp.dma_start(qk_s[:, :], qk).then_inc(s_attn_w, 16)
            sp.dma_start(ov_s[:, :], ov).then_inc(s_attn_w, 16)

            def experts(n):
                sp.dma_start(W1s, W1.rearrange("e d f -> d e f")).then_inc(s_experts[n], 16)
                for c in range(FC):
                    sp.dma_start(W2s[:, :, c, :], W2[:, c * P:(c + 1) * P, :].rearrange("e p d -> p e d")).then_inc(
                        s_experts[n], 16)

            experts(0)

            def ld(dst, src):
                sp.dma_start(dst, src).then_inc(s_weights, 16)

            with nc.allow_non_contiguous_dma(reason="small weights"):
                ld(Wg_s[:, :], Wg)
                for v, w in ((g1, ln1_g), (b1, ln1_b), (g2, ln2_g), (b2, ln2_b)):
                    ld(v[:, :], w.rearrange("(p a) -> p a", a=1))
                ld(win_s[:, :], w_in)
                ld(wconv_row[0:1, :, :], w_conv.rearrange("(a c) k -> a k c", a=1))
                ld(bconv_s[:, :], b_conv.rearrange("(b p) -> p b", p=P))
                ld(wx_s[:, :, :], w_xproj.rearrange("(b p) r -> p b r", p=P))
                ld(wdt_s[:, :], w_dt)
                ld(bdt_s[:, :], b_dt.rearrange("(b p) -> p b", p=P))
                ld(Aneg[:, :, :], A_log.rearrange("(b p) n -> p b n", p=P))
                ld(Dp_s[:, :], Dp.rearrange("(b p) -> p b", p=P))
                ld(wout_s[:, :, :], w_out.rearrange("(b p) d -> p b d", p=P))
                ld(wff1_s[:, :], w_ff1)
                ld(bff1_s[:, :], b_ff1.rearrange("(c p) -> p c", p=P))
                ld(wff2_s[:, :, :], w_ff2.rearrange("(c p) d -> p c d", p=P))
                ld(bff2_s[0:1, :], b_ff2.rearrange("(a d) -> a d", a=1))
            sp.wait_ge(s_zeros, 1)
            sp.dma_start(routed_in.rearrange("(k p) d -> p k d", p=P),
                         col(Y[:, 0, :]).broadcast_to([P, RT, D])).then_inc(s_routed_clear, 16)

            def routed_tiles(f):
                def load(i, s):
                    sp.wait_ge(f.x_ps, i * 3 + (s + 1))
                    sp.dma_start(xin[:, s, :], routed_in[bass.ds(i * (3 * P) + s * P, P), :]).then_inc(
                        f.loaded[s], 16)

                def store(i, s):
                    sp.wait_ge(f.y, i * 3 + (s + 1))
                    sp.dma_start(routed_out[bass.ds(i * (3 * P) + s * P, P), :], ry[:, s, :]).then_inc(
                        f.stored[s], 16)

                sp.wait_ge(f.scattered, 16 * NT)
                for s in range(3):
                    sp.sem_inc(f.stored[s], 16)
                    load(0, s)
                with sp.Fori(0, RT // 3 - 1) as i:
                    for s in range(3):
                        load(i + 1, s)
                    for s in range(3):
                        store(i, s)
                for s in range(3):
                    store(RT // 3 - 1, s)

            routed_tiles(ffn[0])
            sp.wait_ge(c_gated, NG + 1)
            experts(1)
            routed_tiles(ffn[1])
            for q in range(4):
                a, b = q * NT // 4, (q + 1) * NT // 4
                sp.wait_ge(ffn[1].added, q + 1)
                sp.dma_start(out_tiles[:, a:b, :], X[:, a:b, :]).then_inc(s_out, 16)
            sp.wait_ge(s_out, 64)

        @block.gpsimd
        def _(pool):
            ch = Chain(pool, g_chain)
            pool.memset(Y[:, 0, :], 0.0).then_inc(s_zeros, 1)
            ch.step(pool.memset(ident[:, :], 0.0))
            ch.step(pool.memset(below_b[:, :], 1.0))
            ch.step(pool.memset(mask[:, :], 0.0))
            ch.step(pool.memset(resets[:, :, :], 1.0))
            ch.step(pool.memset(pick[:, :, :], 0.0))
            ch.step(pool.memset(ones_b[:, :], 1.0))
            ch.step(pool.memset(ones_row[:, :], 1.0))
            ch.step(pool.memset(one_c[:, :], 1.0))
            ch.step(pool.iota(em8[:, :, :], [[1, E], [0, NT]], base=-E, channel_multiplier=0,
                              allow_small_or_imprecise_dtypes=True))
            ch.link(pool.iota(kk[:, :, :], [[1, RT], [0, E]], base=0, channel_multiplier=0,
                              allow_small_or_imprecise_dtypes=True))
            ch.step(pool.affine_select(out=ident[:, :], in_=ident[:, :], compare_op=ALU.not_equal, fill=1.0, base=0,
                                       pattern=[[-1, P]], channel_multiplier=1))
            ch.step(pool.affine_select(out=below_b[:, :], in_=below_b[:, :], compare_op=ALU.is_gt, fill=0.0, base=0,
                                       pattern=[[1, P]], channel_multiplier=-1))
            ch.step(pool.affine_select(out=mask[:, P:S], in_=mask[:, P:S], compare_op=ALU.is_ge, fill=MASKED, base=0,
                                       pattern=[[-1, P]], channel_multiplier=1))
            ch.step(pool.memset(resets[:, :, 0:1], 0.0))
            for part in range(3):
                ch.link(pool.affine_select(out=pick[:, :, :], in_=pick[:, :, :], compare_op=ALU.not_equal, fill=1.0,
                                           base=-2 * N * part, pattern=[[-1, 2 * N], [0, P]], channel_multiplier=1))
            pool.sem_inc(s_const, 1)
            pool.sem_inc(c_hC, 2)

            def routed(f):
                pool.wait_ge(f.routed, 1)
                pool.wait_ge(s_routed_clear, 16)
                pool.wait_ge(f.copied, NG + 2)
                for j in range(NT):
                    pool.indirect_dma_start(out=routed_in, out_offset=bass.IndirectOffsetOnAxis(
                        ap=pos[:, j:j + 1], axis=0), in_=XN[:, j, :], in_offset=None,
                        bounds_check=RT * P - 1).then_inc(f.scattered, 16)
                for s in range(3):
                    pool.wait_ge(f.stored[s], 16 * (RT // 3 + 1))
                for j in range(NT):
                    pool.indirect_dma_start(out=Y[:, j, :], out_offset=None, in_=routed_out,
                                            in_offset=bass.IndirectOffsetOnAxis(ap=pos[:, j:j + 1], axis=0),
                                            bounds_check=RT * P - 1).then_inc(f.gathered[j * 4 // NT], 16)

            routed(ffn[0])

            with pool.Fori(0, NG) as g:
                pool.wait_ge(m_delta, g + 1)
                pool.tensor_tensor(du[:, :, bass.ds(g * G, G)], delta[:, :, bass.ds(g * G, G)],
                                   xm[:, :, bass.ds(g * G, G)], ALU.mult).then_inc(m_du, 1)

            with pool.Fori(0, NG) as g:
                for n in range(N):
                    s = n % 2
                    pool.wait_ge(c_h, g * N + (n + 3))
                    pool.wait_ge(c_C_sb, g * N + (n + 1))
                    pool.wait_ge(c_y, g * N + (n + 1))
                    pool.tensor_tensor(hC[:, s], h[:, s], col(C_bc[:, s]).broadcast_to([P, NB, G]),
                                       ALU.mult).then_inc(c_hC, 1)

            routed(ffn[1])

        @block.scalar
        def _(act):
            ch = Chain(act, a_chain)
            A = nc.scalar.activation
            act.wait_ge(s_const, 1)
            act.preload_act_table(ACT.Exp)
            with act.Fori(0, B // 2) as i:
                for s in range(2):
                    act.wait_ge(a_uv_ps, i * 2 + (s + 1))
                    A(uv_a[:, s], bank[2 + s], ACT.Copy).then_inc(a_uv, 1)
                for s in range(2):
                    act.wait_ge(a_max, i * 4 + (2 * s + 2))
                    A(pr_a[:, s, 0:P], sc_a[:, s, 0:P], ACT.Exp, scale=-1.0, bias=nmax[:, s, 0:1],
                      accum_out=psum_e[:, s, 0:1])
                    A(pr_a[:, s, P:P + S], sc_a[:, s, P:P + S], ACT.Exp, scale=-1.0, bias=nmax[:, s, 1:2],
                      accum_out=psum_e[:, s, 1:2]).then_inc(a_exp, 1)

            def route_ffn(f):
                act.sem_inc(f.copied, 2)
                with act.Fori(0, NG // 2) as i:
                    for s in range(2):
                        apart(act, f.turn.xs, i * 2 + (s + 1))
                        A(XN[:, bass.ds(i * (2 * GT) + s * GT, GT), :], xs[:, s], ACT.Copy).then_inc(f.copied, 1)
                act.wait_ge(f.shifted, 1)
                A(pe, pe, ACT.Exp).then_inc(f.exps, 1)
                act.preload_act_table(ACT.Gelu)
                with act.Fori(0, RT // 3) as i:
                    for s in range(3):
                        act.wait_ge(f.h_ps, i * 3 + (s + 1))
                        A(rh[:, s], bank[3 + s][:, 0:F], ACT.Gelu).then_inc(f.h, 1)

            route_ffn(ffn[0])

            act.wait_ge(s_weights, 16 * (N_WEIGHTS - 1))
            ch.link(A(Aneg[:, :, :], Aneg[:, :, :], ACT.Exp))
            ch.link(A(Aneg[:, :, :], Aneg[:, :, :], ACT.Copy, scale=-1.0))
            act.preload_act_table(ACT.Silu)
            with act.Fori(0, NG // 2) as i:
                for s in range(2):
                    at = bass.ds(i * (2 * G) + s * G, G)
                    apart(act, m_xc_ps, i * 2 + (s + 1))
                    for b in range(NB):
                        A(xm[:, b, at], bank[2 + b], ACT.Silu, bias=bconv_s[:, b:b + 1])
                    for b in range(NB):
                        last = A(zs[:, b, at], bank[4 + b], ACT.Silu)
                    last.then_inc(m_silu, 1)
            act.preload_act_table_set("natural_log_exp_and_others")
            with act.Fori(0, NG) as g:
                ch.loop(g, 2, NG)
                act.wait_ge(m_raw, g + 1)
                ch.link(A(ab, sx, ACT.Abs))
                ch.link(A(ex, ab, ACT.Exp, scale=-1.0))
                A(ab, ex, ACT.Ln, bias=one_c[:, 0:1]).then_inc(m_soft, 1)
            ch.end()

            act.wait_ge(m_du, NG)
            with act.Fori(0, NG) as g:
                for n in range(N):
                    s = n % 2
                    apart(act, c_h, g * N + (n + 1))
                    for b in range(NB):
                        d = delta[:, b, bass.ds(g * G, G)].rearrange("p (q t) -> p q t", q=GB)[:, :, 1:S]
                        o = decay_ps[:, s, b, :].rearrange("p (q t) -> p q t", q=GB)[:, :, 1:S]
                        last = A(o, d, ACT.Exp, scale=Aneg[:, b, n:n + 1])
                    last.then_inc(c_decay, 1)
                    act.wait_ge(c_C, g * N + (n + 1))
                    act.wait_ge(c_hC, g * N + (n + 1))
                    A(C_bc[:, s], bank[3], ACT.Copy).then_inc(c_C_sb, 1)

            with act.Fori(0, NG // 2) as i:
                for s in range(2):
                    if s == 0:
                        act.wait_ge(c_gated, NG + 1)
                    apart(act, p_xa, i * 2 + (s + 1))
                    A(ygs[:, s], xm[:, :, bass.ds(i * (2 * G) + s * G, G)], ACT.Copy).then_inc(p_yg, 1)
            act.preload_act_table(ACT.Gelu_apprx_tanh)
            with act.Fori(0, NG) as g:
                for c in range(FFC):
                    act.wait_ge(d_h_ps, g * FFC + (c + 1))
                    A(hT[:, c], bank[2 + c], ACT.Gelu_apprx_tanh, bias=bff1_s[:, c:c + 1]).then_inc(d_h, 1)
            route_ffn(ffn[1])

        @block.vector
        def _(dve):
            V = nc.vector
            ch = Chain(dve, v_chain)
            def rsqrt(w, r):
                ch.link(V.tensor_scalar(guess[:, :], w[:, :].bitcast(I32), 1, None, ALU.logical_shift_right))
                ch.link(V.tensor_scalar(r[:, :].bitcast(I32), guess[:, :], -1.0, float(0x5f3759df), ALU.mult,
                                        ALU.add))
                for _ in range(4):
                    ch.link(V.scalar_tensor_tensor(out=t32[:, :], in0=r[:, :], scalar=-0.5, in1=r[:, :],
                                                   op0=ALU.mult, op1=ALU.mult))
                    ch.link(V.tensor_tensor(t32[:, :], t32[:, :], w[:, :], ALU.mult))
                    ch.link(V.scalar_tensor_tensor(out=r[:, :], in0=t32[:, :], scalar=1.5, in1=r[:, :],
                                                   op0=ALU.add, op1=ALU.mult))

            def norm_factors():
                ch.step(V.tensor_tensor(mean2[:, :], stats[:, :, 1], stats[:, :, 4], ALU.add))
                ch.step(V.tensor_tensor(var4[:, :], stats[:, :, 1], stats[:, :, 4], ALU.subtract))
                ch.link(V.tensor_tensor(t32[:, :], stats[:, :, 2], stats[:, :, 5], ALU.add))
                ch.link(V.tensor_tensor(var4[:, :], var4[:, :], var4[:, :], ALU.mult))
                ch.link(V.scalar_tensor_tensor(out=var4[:, :], in0=t32[:, :], scalar=4.0 / D, in1=var4[:, :],
                                               op0=ALU.mult, op1=ALU.add))
                ch.link(V.tensor_scalar(vv[:, :], var4[:, :], 0.25, EPS, ALU.mult, ALU.add))
                rsqrt(vv, rs)
                ch.link(V.scalar_tensor_tensor(out=nmr[:, :], in0=mean2[:, :], scalar=-0.5, in1=rs[:, :],
                                               op0=ALU.mult, op1=ALU.mult))

            def all_stats(tile):
                with dve.Fori(0, NT // 8) as i:
                    ch.loop(i, 8, NT // 8)
                    for q in range(8):
                        ch.step(V.bn_stats(stats[:, bass.ds(i * 8 + q, 1), :].rearrange("p a k -> p (a k)"),
                                           tile[:, bass.ds(i * 8 + q, 1), :].rearrange("p a d -> p (a d)")))
                ch.end()
                ch.wait()

            def normed(dst, src, j, r, m):
                return V.tensor_scalar(dst, src[:, bass.ds(j, 1), :].rearrange("p a d -> p (a d)"),
                                       r[:, bass.ds(j, 1)], m[:, bass.ds(j, 1)], ALU.mult, ALU.add)

            dve.wait_ge(s_x, 64)
            all_stats(X)
            norm_factors()
            dve.wait_ge(s_const, 1)
            with dve.Fori(0, B // 2) as i:
                for s in range(2):
                    for k in range(2):
                        last = normed(xn_a[:, s, k, :], X, i * 4 + (2 * s + k), rs, nmr)
                    last.then_inc(a_xn, 1)
                for s in range(2):
                    dve.wait_ge(a_xT_ps, i * 2 + (s + 1))
                    V.tensor_copy(xT_a[:, s], bank[s][:, 0:S]).then_inc(a_xT, 1)
                for s in range(2):
                    apart(dve, a_sc_ps, i * 2 + (s + 1))
                    V.tensor_tensor_reduce(sc_a[:, s, 0:P], bank[4 + s][:, 0:P], mask[:, P:S], -1.0 / D ** 0.5,
                                           3e38, ALU.add, ALU.min, nmax[:, s, 0:1]).then_inc(a_max, 1)
                    V.tensor_tensor_reduce(sc_a[:, s, P:P + S], bank[4 + s][:, P:P + S], mask[:, :], -1.0 / D ** 0.5,
                                           3e38, ALU.add, ALU.min, nmax[:, s, 1:2]).then_inc(a_max, 1)
                for s in range(2):
                    dve.wait_ge(a_pT_ps, i * 2 + (s + 1))
                    V.tensor_copy(pT_a[:, s], bank[s][:, 0:384]).then_inc(a_pT, 1)
                ch.loop(i, 6, B // 2)
                for s in range(2):
                    dve.wait_ge(a_exp, i * 2 + (s + 1))
                    ch.link(V.reciprocal(rinv[:, s], psum_e[:, s]))
                    dve.wait_ge(a_out_ps, i * 2 + (s + 1))
                    for k in range(2):
                        xt = X[:, bass.ds(i * 4 + (2 * s + k), 1), :].rearrange("p a d -> p (a d)")
                        ch.step(V.scalar_tensor_tensor(out=xt, in0=bank[2 + s][:, k * P:(k + 1) * P],
                                                       scalar=rinv[:, s, k:k + 1], in1=xt, op0=ALU.mult,
                                                       op1=ALU.add))
            ch.end()
            ch.wait()

            def turned(turn, src, r, m, done, copied=None):
                with dve.Fori(0, NG // 2) as i:
                    for s in range(2):
                        if copied is not None:
                            dve.wait_ge(copied, i * 2 + (s + 1))
                        for q in range(GT):
                            last = normed(xs[:, s, q, :], src, i * (2 * GT) + (s * GT + q), r, m)
                        last.then_inc(turn.xs, 1)
                    for s in range(2):
                        dve.wait_ge(turn.ps, i * 2 + (s + 1))
                        done(i, s).then_inc(turn.xT, 1)

            def route_ffn(f, last_layer):
                all_stats(X)
                norm_factors()
                turned(f.turn, X, rs, nmr, lambda i, s: V.tensor_copy(xsT[:, s], bank[s]), f.copied)
                logits = bank[2][:, 0:E * NT].rearrange("p (e j) -> p e j", e=E)
                dve.wait_ge(f.logits, 2 * (NG // 2))
                ch.link(V.tensor_reduce(tl, by_tile(logits), AX, ALU.max))
                V.tensor_tensor(pe, logits, over_experts(tl), ALU.subtract).then_inc(f.shifted, 1)
                dve.wait_ge(f.exps, 1)
                ch.link(V.tensor_reduce(tl, by_tile(pe), AX, ALU.add))
                ch.link(V.reciprocal(tl, tl))
                ch.step(V.memset(cand[:, :], 1 << TOP_BIT))
                ch.link(V.tensor_tensor(prob, pe, over_experts(tl), ALU.mult))
                for k in range(TOP_BIT, -1, -1):
                    ch.link(V.tensor_tensor(flag_b[:, :, :], prob, over_tiles(cand[:, :].bitcast(F32)), ALU.is_ge))
                    with nc.allow_low_precision(reason="counts up to 32 are exact"):
                        V.tensor_reduce(cnt_b[:, :], flag_b[:, :, :], AX, ALU.add).then_inc(f.flags, 1)
                    ch.step(V.tensor_scalar(cand_next[:, :], cand[:, :], (1 << k) >> 1, None, ALU.bitwise_xor))
                    dve.wait_ge(f.counts, TOP_BIT - k + 1)
                    ch.link(V.tensor_scalar(miss[:, :], bank[3][:, 0:E], CAP - 0.5, -1.0, ALU.is_lt, ALU.mult))
                    ch.link(V.scalar_tensor_tensor(out=cand[:, :], in0=miss[:, :], scalar=1 << k,
                                                   in1=cand_next[:, :], op0=ALU.bitwise_and, op1=ALU.bitwise_xor))
                thr = over_tiles(cand[:, :].bitcast(F32))
                above, least, need = fA, fB, e8[:, 0]
                ch.link(V.tensor_tensor(above, prob, thr, ALU.is_gt))
                with nc.allow_low_precision(reason="counts up to 32 are exact"):
                    V.tensor_reduce(cnt_b[:, :], above, AX, ALU.add).then_inc(f.flags, 1)
                ch.step(V.tensor_tensor(least, prob, thr, ALU.is_equal))
                dve.wait_ge(f.counts, 31)
                ch.link(V.tensor_scalar(need, bank[3][:, 0:E], -1.0, float(CAP), ALU.mult, ALU.add))
                V.tensor_copy(flag_b[:, :, :], least).then_inc(f.flags, 1)

                def before(n, dst):
                    within = bank[0][:, 0:E * NT].rearrange("p (e j) -> p e j", e=E)
                    totals = bank[1][:, 0:E * NT]
                    dve.wait_ge(f.counts, n)
                    flat = incl.rearrange("p e j -> p (e j)")
                    ch.link(V.tensor_tensor_scan(flat, resets[:, :, :].rearrange("p e j -> p (e j)"), totals, 0.0,
                                                 ALU.mult, ALU.add))
                    ch.link(V.tensor_tensor(dst, incl, totals.rearrange("p (e j) -> p e j", e=E), ALU.subtract))
                    ch.link(V.tensor_tensor(dst, dst, within, ALU.add))

                before(32, fC)
                ch.link(V.tensor_tensor(fC, fC, over_tiles(need), ALU.is_lt))
                ch.link(V.tensor_tensor(fC, fC, least, ALU.mult))
                ch.link(V.tensor_tensor(sel, fC, above, ALU.add))
                ch.link(V.tensor_reduce(tl, by_tile(sel), AX, ALU.max))
                ch.link(V.tensor_scalar(tl, tl, -1.0, 1.0, ALU.mult, ALU.add))
                ch.link(V.tensor_tensor(sel, sel, over_experts(tl), ALU.max))
                ch.link(V.tensor_tensor(fA, prob, sel, ALU.mult))
                ch.link(V.scalar_tensor_tensor(out=fA.rearrange("p e j -> p (e j)"),
                                               in0=sel.rearrange("p e j -> p (e j)"), scalar=-1.0,
                                               in1=fA.rearrange("p e j -> p (e j)"), op0=ALU.add, op1=ALU.add))
                ch.link(V.tensor_reduce(gate[:, :], by_tile(fA), AX, ALU.max))
                ch.link(V.tensor_tensor(fB, fA, over_experts(gate[:, :]), ALU.is_equal))
                ch.link(V.tensor_tensor(fB, fB, em8[:, :, :], ALU.mult))
                ch.link(V.tensor_reduce(tl, by_tile(fB), AX, ALU.min))
                ch.link(V.tensor_tensor(fA, em8[:, :, :], over_experts(tl), ALU.is_equal))
                V.tensor_copy(flag_b[:, :, :], fA).then_inc(f.flags, 1)
                before(33, fC)
                ch.link(V.tensor_scalar(e8i[:, :], incl[:, :, NT - 1], float(P - 1), None, ALU.add))
                ch.link(V.tensor_scalar(e8i[:, :], e8i[:, :], P.bit_length() - 1, None, ALU.logical_shift_right))
                ch.step(V.memset(e8[:, 2], 1.0))
                ch.link(V.tensor_copy(e8[:, 1], e8i[:, :]))
                ch.link(V.tensor_tensor_scan(e8[:, 3], e8[:, 2], e8[:, 1], 0.0, ALU.mult, ALU.add))
                ch.link(V.tensor_tensor(e8[:, 4], e8[:, 3], e8[:, 1], ALU.subtract))
                ch.link(V.tensor_scalar(e8[:, 5], e8[:, 4], float(P), None, ALU.mult))
                ch.link(V.tensor_tensor(fC, fC, over_tiles(e8[:, 5]), ALU.add))
                ch.link(V.tensor_tensor(fC, fC, fA, ALU.mult))
                ch.link(V.tensor_reduce(pos_f[:, :], by_tile(fC), AX, ALU.add))
                ch.link(V.tensor_tensor(kcmp[:, :, :], col(e8[:, 3]).broadcast_to([P, RT, E]), kk[:, :, :], ALU.is_le))
                ch.link(V.tensor_reduce(ktab[:, :], kcmp[:, :, :], AX, ALU.add))
                ch.link(V.tensor_scalar(etab[:, :], ktab[:, :], float(E - 1), None, ALU.min))
                V.tensor_copy(pos[:, :], pos_f[:, :]).then_inc(f.routed, 1)

                with dve.Fori(0, RT // 3) as i:
                    for s in range(3):
                        dve.wait_ge(f.x_ps, i * 3 + (s + 4))
                        V.tensor_copy(rxT[:, s], bank[s][:, 0:P]).then_inc(f.x, 1)
                    for s in range(3):
                        dve.wait_ge(f.hT_ps, i * 3 + (s + 1))
                        V.tensor_copy(rhT[:, s], bank[s][:, 0:F]).then_inc(f.hT, 1)
                    for s in range(3):
                        dve.wait_ge(f.y_ps, i * 3 + (s + 1))
                        dve.wait_ge(f.stored[s], i * 16 + 16)
                        V.tensor_copy(ry[:, s], bank[3 + s][:, 0:P]).then_inc(f.y, 1)
                for q in range(4):
                    dve.wait_ge(f.gathered[q], 16 * NT // 4)
                    with dve.Fori(q * NT // 4, (q + 1) * NT // 4) as j:
                        xt = X[:, bass.ds(j, 1), :].rearrange("p a d -> p (a d)")
                        last = V.scalar_tensor_tensor(out=xt, in0=Y[:, bass.ds(j, 1), :].rearrange("p a d -> p (a d)"),
                                                      scalar=gate[:, bass.ds(j, 1)], in1=xt, op0=ALU.mult,
                                                      op1=ALU.add)
                        ch.loop(j - q * (NT // 4), 1, NT // 4)
                        ch.step(last)
                    ch.end()
                    ch.wait()
                    V.memset(t32[:, 0:1], 0.0).then_inc(f.added, 1)

            route_ffn(ffn[0], False)

            all_stats(X)
            norm_factors()
            ch.link(V.tensor_scalar(var4[:, :], var4[:, :], 0.25, None, ALU.mult))
            ch.link(V.tensor_tensor(var4[:, :], var4[:, :], rs[:, :], ALU.mult))
            ch.link(V.tensor_tensor(var4[:, :], var4[:, :], rs[:, :], ALU.mult))
            ch.link(V.tensor_scalar(vv[:, :], var4[:, :], 1.0, EPS, ALU.mult, ALU.add))
            rsqrt(vv, rs2)
            ch.link(V.tensor_tensor(rs2[:, :], rs2[:, :], rs[:, :], ALU.mult))
            ch.link(V.scalar_tensor_tensor(out=nmr2[:, :], in0=mean2[:, :], scalar=-0.5, in1=rs2[:, :],
                                           op0=ALU.mult, op1=ALU.mult))

            dve.wait_ge(s_weights, 16 * (N_WEIGHTS - 1))
            for k in range(TAPS):
                if k % 2 == 0:
                    dve.wait_ge(s_conv_ps, k // 2 + 1)
                V.tensor_tensor(wfold[:, k, :], win_s[:, 0:DI], bank[6 + k // 2][:, (k % 2) * DI:(k % 2 + 1) * DI],
                                ALU.mult).then_inc(s_weights_prep, 1)
            for b in range(NB):
                for c in range(3):
                    V.tensor_copy(wbc3[:, b, c * 2 * N:(c + 1) * 2 * N], wx_s[:, b, R:R + 2 * N]).then_inc(
                        s_weights_prep, 1)
                V.tensor_scalar(diagD[:, b, :], ident[:, :], Dp_s[:, b:b + 1], None, ALU.mult).then_inc(
                    s_weights_prep, 1)
            ch.link(V.memset(xaT[:, :, 0:PAD], 0.0))

            def into_xaT(i, s):
                return V.tensor_scalar(xaT[:, bass.ds(i * (2 * GB) + s * GB, GB), PAD:SP_],
                                       bank[s].rearrange("p (q t) -> p q t", q=GB), g1[:, 0:1], b1[:, 0:1],
                                       ALU.mult, ALU.add)

            turned(m_turn, X, rs2, nmr2, into_xaT)

            with dve.Fori(0, NG) as g:
                dve.wait_ge(m_dt_ps, g + 1)
                V.tensor_copy(dtT[0:R, 0], bank[0][0:R, :]).then_inc(m_dt, 1)
                dve.wait_ge(m_bc_ps, g + 1)
                at = bass.ds(g * G, G)
                ch.loop(g, 6, NG)
                ch.link(V.tensor_copy(bc_hi[:, :], bank[1][0:BC3, :]))
                ch.step(V.tensor_copy(bc_parts[0:2 * N, at], bc_hi[0:2 * N, :]))
                ch.link(V.tensor_tensor(bcr[0:BC3, 0], bank[1][0:BC3, :], bc_hi[:, :], ALU.subtract))
                ch.link(V.tensor_copy(bc_hi[:, :], bcr[0:BC3, 0]))
                ch.step(V.tensor_copy(bc_parts[2 * N:4 * N, at], bc_hi[2 * N:4 * N, :]))
                ch.link(V.tensor_tensor(bcr[0:BC3, 1], bcr[0:BC3, 0], bc_hi[:, :], ALU.subtract))
                V.tensor_copy(bc_parts[4 * N:6 * N, at], bcr[4 * N:6 * N, 1]).then_inc(m_bc, 1)
                dve.wait_ge(m_raw_ps, g + 1)
                for b in range(NB):
                    last = V.tensor_scalar(sx[:, b], bank[2 + b], bdt_s[:, b:b + 1], None, ALU.add)
                last.then_inc(m_raw, 1)
                dve.wait_ge(m_soft, g + 1)
                V.scalar_tensor_tensor(out=delta[:, :, at], in0=sx, scalar=0.0, in1=ab, op0=ALU.max,
                                       op1=ALU.add).then_inc(m_delta, 1)
            ch.end()

            dve.wait_ge(m_soft, NG)
            V.memset(decay_ps[:, :, :, 0:G:S], 0.0).then_inc(c_h, 1)
            dve.wait_ge(c_h, 1)
            dve.sem_inc(c_h, 1)
            dve.sem_inc(c_dBu, 1)
            dve.sem_inc(c_gated, 1)
            dve.wait_ge(m_du, NG)
            with dve.Fori(0, NG) as g:
                at = bass.ds(g * G, G)
                for n in range(N):
                    s = n % 2
                    dve.wait_ge(c_h, g * N + (n + 2))
                    dve.wait_ge(c_B, g * N + (n + 1))
                    V.tensor_tensor(dBu, du[:, :, at], col(bank[2]).broadcast_to([P, NB, G]),
                                    ALU.mult).then_inc(c_dBu, 1)
                    dve.wait_ge(c_dBu, g * N + (n + 2))
                    dve.wait_ge(c_decay, g * N + (n + 1))
                    dve.wait_ge(c_hC, g * N + (n + 1))
                    V.tensor_tensor_scan(h[:, s].rearrange("p b t -> p (b t)"),
                                         decay_ps[:, s].rearrange("p b t -> p (b t)"),
                                         dBu.rearrange("p b t -> p (b t)"), 0.0, ALU.mult,
                                         ALU.add).then_inc(c_h, 1)
                dve.wait_ge(c_y, g * N + (N + 2))
                for b in range(NB):
                    last = V.tensor_tensor(xm[:, b, at], bank[b], zs[:, b, at], ALU.mult)
                last.then_inc(c_gated, 1)

            with dve.Fori(0, NG // 2) as i:
                ch.loop(i, 2 * GT, NG // 2)
                for s in range(2):
                    for q in range(GT):
                        j = i * (2 * GT) + (s * GT + q)
                        ch.step(normed(XA[:, bass.ds(j, 1), :].rearrange("p a d -> p (a d)"), X, j, rs, nmr))
                    ch.wait()
                    dve.wait_ge(p_out_ps, i * 2 + (s + 1))
                    xa = XA[:, bass.ds(i * (2 * GT) + s * GT, GT), :]
                    V.tensor_tensor(xa, xa, bank[s].rearrange("p (q d) -> p q d", q=GT), ALU.add).then_inc(p_xa, 1)
            ch.end()
            dve.wait_ge(p_xa, NG + 2)
            all_stats(XA)
            norm_factors()
            with dve.Fori(0, NG) as g:
                ch.loop(g, 1, NG)
                for q in range(GT):
                    last = normed(xs[:, 0, q, :], XA, g * GT + q, rs, nmr)
                last.then_inc(d_turn.xs, 1)
                dve.wait_ge(d_turn.ps, g + 1)
                V.tensor_scalar(xsT[:, 0], bank[0], g2[:, 0:1], b2[:, 0:1], ALU.mult, ALU.add).then_inc(
                    d_turn.xT, 1)
                xt, xa = X[:, bass.ds(g * GT, GT), :], XA[:, bass.ds(g * GT, GT), :]
                ch.link(V.tensor_tensor(xt, xt, xa, ALU.add))
                dve.wait_ge(d_y_ps, g + 1)
                V.tensor_tensor(xt, xt, bank[1].rearrange("p (q d) -> p q d", q=GT), ALU.add).then_inc(d_x, 1)
            ch.end()
            dve.wait_ge(d_x, NG)
            route_ffn(ffn[1], True)

        @block.tensor
        def _(pe_):
            mm, tr = nc.tensor.matmul, nc.tensor.transpose
            pe_.wait_ge(s_const, 1)
            pe_.wait_ge(s_attn_w, 32)
            with pe_.Fori(0, B // 2) as i:
                for s in range(2):
                    pe_.wait_ge(a_xn, i * 2 + (s + 1))
                    for k in range(2):
                        last = tr(bank[s][:, k * P:(k + 1) * P], xn_a[:, s, k, :], ident[:, :])
                    last.then_inc(a_xT_ps, 1)
                for s in range(2):
                    pe_.wait_ge(a_xT, i * 2 + (s + 1))
                    mm(bank[2 + s][:, 0:S], qk_s[:, :], xT_a[:, s], start=True, stop=True)
                    for k in range(2):
                        last = mm(bank[2 + s][:, S + k * P:S + (k + 1) * P], xT_a[:, s, k * P:(k + 1) * P],
                                  ov_s[:, :], start=True, stop=True)
                    last.then_inc(a_uv_ps, 1)
                for s in range(2):
                    pe_.wait_ge(a_uv, i * 2 + (s + 1))
                    mm(bank[4 + s][:, 0:P], uv_a[:, s, 0:P], xT_a[:, s, 0:P], start=True, stop=True)
                    mm(bank[4 + s][:, P:P + S], uv_a[:, s, P:S], xT_a[:, s, :], start=True,
                       stop=True).then_inc(a_sc_ps, 1)
                for s in range(2):
                    pe_.wait_ge(a_exp, i * 2 + (s + 1))
                    for k in range(3):
                        last = tr(bank[s][:, k * P:(k + 1) * P], pr_a[:, s, k * P:(k + 1) * P], ident[:, :])
                    last.then_inc(a_pT_ps, 1)
                for s in range(2):
                    pe_.wait_ge(a_pT, i * 2 + (s + 1))
                    v = [uv_a[:, s, S + k * P:S + (k + 1) * P] for k in range(2)]
                    mm(bank[2 + s][:, 0:P], pT_a[:, s, 0:P], v[0], start=True, stop=True)
                    mm(bank[2 + s][:, P:S], pT_a[:, s, P:2 * P], v[0], start=True, stop=False)
                    mm(bank[2 + s][:, P:S], pT_a[:, s, 2 * P:3 * P], v[1], start=False,
                       stop=True).then_inc(a_out_ps, 1)

            pe_.wait_ge(s_weights, 16 * (N_WEIGHTS - 1))

            def turned(turn, then):
                with pe_.Fori(0, NG // 2) as i:
                    for s in range(2):
                        pe_.wait_ge(turn.xs, i * 2 + (s + 1))
                        for q in range(GT):
                            last = tr(bank[s][:, q * P:(q + 1) * P], xs[:, s, q, :], ident[:, :])
                        last.then_inc(turn.ps, 1)
                    for s in range(2):
                        pe_.wait_ge(turn.xT, i * 2 + (s + 1))
                        then(i, s)

            def route_ffn(f, n):
                def logits(i, s):
                    for q in range(GT):
                        j = i * (2 * GT) + (s * GT + q)
                        o = bank[2][:, 0:E * NT].rearrange("p (e j) -> p e j", e=E)[:, :, bass.ds(j, 1)]
                        last = mm(o.rearrange("p e a -> p (e a)"), xsT[:, s, q * P:(q + 1) * P], Wg_s[:, :],
                                  start=True, stop=True)
                    last.then_inc(f.logits, 1)

                turned(f.turn, logits)

                def count():
                    return mm(bank[3][:, 0:E], ones_b[:, :], cnt_b[:, :], start=True, stop=True)

                for k in range(TOP_BIT + 2):
                    pe_.wait_ge(f.flags, k + 1)
                    count().then_inc(f.counts, 1)
                flags = flag_b[:, :, :].rearrange("p e j -> p (e j)")
                for n_flags in (32, 33):
                    pe_.wait_ge(f.flags, n_flags)
                    mm(bank[0][:, 0:E * NT], below_b[:, :], flags, start=True, stop=True)
                    mm(bank[1][:, 0:E * NT], ones_b[:, :], flags, start=True, stop=True).then_inc(f.counts, 1)
                pe_.wait_ge(f.routed, 1)
                pe_.wait_ge(s_experts[n], 16 * (1 + FC))
                pe_.sem_inc(f.x_ps, 3)
                with pe_.Fori(0, RT // 3) as i:
                    for s in range(3):
                        pe_.wait_ge(f.loaded[s], i * 16 + 16)
                        tr(bank[s][:, 0:P], xin[:, s, :], ident[:, :]).then_inc(f.x_ps, 1)
                    who = [pe_.value_load(etab[0:1, bass.ds(i * 3 + s, 1)], min_val=0, max_val=E - 1)
                           for s in range(3)]
                    for s in range(3):
                        pe_.wait_ge(f.x, i * 3 + (s + 1))
                        mm(bank[3 + s][:, 0:F], rxT[:, s], W1s[:, bass.ds(who[s], 1), :].rearrange("p a f -> p (a f)"),
                           start=True, stop=True).then_inc(f.h_ps, 1)
                    for s in range(3):
                        pe_.wait_ge(f.h, i * 3 + (s + 1))
                        for c in range(FC):
                            last = tr(bank[s][:, c * P:(c + 1) * P], rh[:, s, c * P:(c + 1) * P], ident[:, :])
                        last.then_inc(f.hT_ps, 1)
                    for s in range(3):
                        pe_.wait_ge(f.hT, i * 3 + (s + 1))
                        for c in range(FC):
                            last = mm(bank[3 + s][:, 0:P], rhT[:, s, c * P:(c + 1) * P],
                                      W2s[:, bass.ds(who[s], 1), c, :].rearrange("p a d -> p (a d)"),
                                      start=(c == 0), stop=(c == FC - 1))
                        last.then_inc(f.y_ps, 1)

            route_ffn(ffn[0], 0)

            for k in range(TAPS):
                last = mm(bank[6 + k // 2][:, (k % 2) * DI:(k % 2 + 1) * DI], ones_row[0:1, :], wconv_row[0:1, k, :],
                          start=True, stop=True)
                if k % 2:
                    last.then_inc(s_conv_ps, 1)
            pe_.wait_ge(s_weights_prep, TAPS + NB * 4)

            def in_proj(i, s):
                seqs = bass.ds(i * (2 * GB) + s * GB, GB)
                for b in range(NB):
                    for k in range(TAPS):
                        mm(bank[2 + b], wfold[:, k, b * P:(b + 1) * P], xaT[:, seqs, k:k + S],
                           start=(k == 0), stop=(k == TAPS - 1))
                if s == 0:
                    pass
                for b in range(NB):
                    last = mm(bank[4 + b], win_s[:, DI + b * P:DI + (b + 1) * P], xaT[:, seqs, PAD:SP_],
                              start=True, stop=True)
                last.then_inc(m_xc_ps, 1)
                pe_.wait_ge(m_silu, i * 2 + (s + 1))

            turned(m_turn, in_proj)

            with pe_.Fori(0, NG) as g:
                at = bass.ds(g * G, G)
                for b in range(NB):
                    last = mm(bank[0][0:R, :], wx_s[:, b, 0:R], xm[:, b, at], start=(b == 0), stop=(b == NB - 1))
                last.then_inc(m_dt_ps, 1)
                for b in range(NB):
                    last = mm(bank[1][0:BC3, :], wbc3[:, b, :], xm[:, b, at], start=(b == 0), stop=(b == NB - 1))
                last.then_inc(m_bc_ps, 1)
                pe_.wait_ge(m_dt, g + 1)
                for b in range(NB):
                    last = mm(bank[2 + b], wdt_s[:, b * P:(b + 1) * P], dtT[0:R, 0], start=True, stop=True)
                last.then_inc(m_raw_ps, 1)
                pe_.wait_ge(m_bc, g + 1)
                pe_.wait_ge(m_raw, g + 1)

            pe_.sem_inc(c_y, 2)
            def pick_B(g, n):
                pe_.wait_ge(c_dBu, g * N + (n + 1))
                mm(bank[2], pick[:, n, :], bc_parts[:, bass.ds(g * G, G)], start=True, stop=True).then_inc(c_B, 1)

            def pick_C(g, n):
                mm(bank[3], pick[:, N + n, :], bc_parts[:, bass.ds(g * G, G)], start=True, stop=True).then_inc(c_C, 1)

            with pe_.Fori(0, NG) as g:
                at = bass.ds(g * G, G)
                pick_B(g, 0)
                pick_C(g, 0)
                pe_.wait_ge(c_gated, g + 1)
                for b in range(NB):
                    mm(bank[b], diagD[:, b, :], xm[:, b, at], start=True, stop=False)
                for n in range(N + 1):
                    if n + 1 < N:
                        pick_B(g, n + 1)
                        pe_.wait_ge(c_C_sb, g * N + (n + 1))
                        pick_C(g, n + 1)
                    if n > 0:
                        pe_.wait_ge(c_hC, g * N + (n + 2))
                        for b in range(NB):
                            last = mm(bank[b], ident[:, :], hC[:, (n - 1) % 2, b, :], start=False, stop=(n == N))
                        last.then_inc(c_y, 1)

            for s in range(2):
                pe_.sem_inc(p_xa, 1)
            with pe_.Fori(0, NG // 2) as i:
                for s in range(2):
                    pe_.wait_ge(p_yg, i * 2 + (s + 1))
                    for q in range(GT):
                        for b in range(NB):
                            last = mm(bank[s][:, q * P:(q + 1) * P], ygs[:, s, b, q * P:(q + 1) * P], wout_s[:, b, :],
                                      start=(b == 0), stop=(b == NB - 1))
                    last.then_inc(p_out_ps, 1)

            with pe_.Fori(0, NG) as g:
                pe_.wait_ge(d_turn.xs, g + 1)
                for q in range(GT):
                    last = tr(bank[0][:, q * P:(q + 1) * P], xs[:, 0, q, :], ident[:, :])
                last.then_inc(d_turn.ps, 1)
                pe_.wait_ge(d_turn.xT, g + 1)
                for c in range(FFC):
                    mm(bank[2 + c], wff1_s[:, c * P:(c + 1) * P], xsT[:, 0], start=True,
                       stop=True).then_inc(d_h_ps, 1)
                pe_.wait_ge(d_h, g * FFC + FFC)
                for q in range(GT):
                    mm(bank[1][:, q * P:(q + 1) * P], ones_row[0:1, :], bff2_s[0:1, :], start=True, stop=False)
                    for c in range(FFC):
                        last = mm(bank[1][:, q * P:(q + 1) * P], hT[:, c, q * P:(q + 1) * P], wff2_s[:, c, :],
                                  start=False, stop=(c == FFC - 1))
                last.then_inc(d_y_ps, 1)
            route_ffn(ffn[1], 1)


_INS = ["L0_attn_a_input_data", "L0_attn_a_qk", "L0_attn_a_ov", "L0_attn_b_ln1_g", "L0_attn_b_ln1_b",
        "L0_attn_b_w_in", "L0_attn_b_w_conv", "L0_attn_b_b_conv", "L0_attn_b_w_xproj", "L0_attn_b_w_dt",
        "L0_attn_b_b_dt", "L0_attn_b_A_log", "L0_attn_b_Dp", "L0_attn_b_w_out", "L0_attn_b_ln2_g",
        "L0_attn_b_ln2_b", "L0_attn_b_w_ff1", "L0_attn_b_b_ff1", "L0_attn_b_w_ff2", "L0_attn_b_b_ff2",
        "L0_ffn_Wg", "L0_ffn_W1", "L0_ffn_W2"]


def kernel(**inputs):
    import numpy as _np
    import concourse.bacc as _bacc
    from concourse import mybir as _mybir
    from concourse.bass_utils import run_bass_kernel_spmd as _run

    nc = _bacc.Bacc("TRN2", target_bir_lowering=False, num_devices=1)
    arrays, args = {}, []
    for name in _INS:
        a = _np.ascontiguousarray(inputs[name])
        arrays[f"in_{name}"] = a
        args.append(nc.dram_tensor(f"in_{name}", a.shape, _mybir.dt.from_np(a.dtype), kind="ExternalInput").ap())
    shape = inputs["L0_attn_a_input_data"].shape
    tokens, experts = shape[0] * shape[1], inputs["L0_ffn_Wg"].shape[1]
    rows = (tokens + experts * (P - 1)) // P * P
    args.append(nc.dram_tensor("out_0", shape, _mybir.dt.float32, kind="ExternalOutput").ap())
    for name in ("routed_in", "routed_out"):
        args.append(nc.dram_tensor(name, (rows, shape[2]), _mybir.dt.float32, kind="Internal").ap())
    hybrid_kernel(nc, *args)
    r = _run(nc, [arrays], core_ids=[0])
    return r.results[0]["out_0"]
```

```python
from contextlib import ExitStack

import concourse.bass as bass
from concourse import mybir

P = 128
ALU = mybir.AluOpType
ACT = mybir.ActivationFunctionType
AX = mybir.AxisListType.X
F32 = mybir.dt.float32
BF16 = mybir.dt.bfloat16
I32 = mybir.dt.int32
EPS = 1e-5
MASKED = -1e30
DIGITS = 15


class Chain:

    def __init__(self, eng, sem):
        self.eng, self.sem = eng, sem
        self.base, self.i, self.per, self.trips, self.k = 0, None, 0, 0, 0

    def loop(self, i, per, trips):
        self.base += self.k
        self.i, self.per, self.trips, self.k = i, per, trips, 0

    def end(self):
        assert self.k == self.per, (self.k, self.per)
        self.base += self.per * self.trips
        self.i, self.k = None, 0

    def step(self, ins):
        ins.then_inc(self.sem, 1)
        self.k += 1

    def wait(self):
        at = self.base + self.k
        self.eng.wait_ge(self.sem, at if self.i is None else self.i * self.per + at)

    def link(self, ins):
        self.step(ins)
        self.wait()


def hybrid_kernel(nc, x_in, qk, ov, ln1_g, ln1_b, w_in, w_conv, b_conv, w_xproj, w_dt, b_dt, A_log, Dp, w_out,
                  ln2_g, ln2_b, w_ff1, b_ff1, w_ff2, b_ff2, Wg, W1, W2, out, routed_in, routed_out):
    B, S, D = x_in.shape
    T = B * S
    NT = T // P
    E = Wg.shape[1]
    F = W1.shape[2]
    FC = F // P
    CAP = max(1, T // E)
    RT = (T + E * (P - 1)) // P
    DI, TAPS = w_conv.shape
    NB = DI // P
    N = A_log.shape[1]
    R = w_dt.shape[0]
    FF = w_ff1.shape[1]
    FFC = FF // P
    G = 512
    NG = T // G
    GT = G // P
    GB = G // S
    PAD = TAPS - 1
    SP_ = S + PAD
    BC3 = 3 * 2 * N
    assert NT * E == 256 and RT % 3 == 0 and BC3 == 96 and S == 2 * P

    with ExitStack() as ctx:
        def sb(name, shape, dt=F32):
            return ctx.enter_context(nc.sbuf_tensor(name, shape, dt))

        def sem(name):
            return ctx.enter_context(nc.semaphore(name))

        bank = [ctx.enter_context(nc.psum_tensor(f"bank{k}", [P, 512], F32)) for k in range(4)]
        decay_ps = ctx.enter_context(nc.psum_tensor("decay_ps", [P, 2, NB, G], F32))
        bank += [decay_ps[:, s, b, :] for s in range(2) for b in range(NB)]
        bank = [b[:, :] for b in bank]

        X = sb("X", [P, NT, D])

        r_delta = sb("r_delta", [P, NB, T])
        r_du = sb("r_du", [P, NB, T])
        r_xm = sb("r_xm", [P, NB, T])
        r_zs = sb("r_zs", [P, NB, T])
        delta, du, xm, zs = r_delta, r_du, r_xm, r_zs
        W1s = r_du[:, 0, 0:E * F].rearrange("p (e f) -> p e f", e=E)
        W2s = r_du[:, 0, E * F:2 * E * F].rearrange("p (e c d) -> p e c d", e=E, c=FC)
        XN = r_zs[:, 0, :].rearrange("p (j d) -> p j d", j=NT)
        Y = r_zs[:, 1, :].rearrange("p (j d) -> p j d", j=NT)
        XA = r_delta[:, 0, :].rearrange("p (j d) -> p j d", j=NT)

        early = r_delta[:, 1, :]
        mask, qk_s, ov_s = early[:, 0:S], early[:, S:S + D], early[:, S + D:S + 2 * D]
        wconv_row = early[0:1, 512:512 + TAPS * DI].rearrange("p (k c) -> p k c", k=TAPS)
        kcmp = early[:, 1536:1536 + RT * E].rearrange("p (k e) -> p k e", e=E)
        ktab, pos_f = early[:, 1856:1856 + RT], early[:, 1920:1920 + NT]
        e8 = early[:, 1984:2048].rearrange("p (k e) -> p k e", e=E)

        work = sb("work", [P, max(6144, 2048 + B * SP_)])

        def carve(at, *shape):
            n = 1
            for k in shape:
                n *= k
            names = " ".join("abcd"[:len(shape)])
            v = work[:, at:at + n]
            if len(shape) > 1:
                v = v.rearrange(f"p ({names}) -> p {names}", **dict(zip("abcd", shape)))
            return v

        xn_a = carve(0, 2, 2, P)
        xT_a = carve(512, 2, S)
        uv_a = carve(1024, 2, 512)
        sc_a = carve(2048, 2, 384)
        pr_a = carve(2816, 2, 384)
        pT_a = carve(3584, 2, 384)
        xs = carve(0, 2, GT, P)
        xsT = carve(1024, 2, G)
        pe = carve(2048, E, NT)
        prob = carve(2304, E, NT)
        fA = carve(2560, E, NT)
        fB = carve(2816, E, NT)
        fC = carve(3072, E, NT)
        incl = carve(3328, E, NT)
        sel = carve(3584, E, NT)
        tl = carve(3840, NT)
        probT = carve(4096, 2, P)
        thr_row = carve(4352, 2, P)
        reached = carve(4608, 2, 3, P)
        xin = carve(4096, 3, P)
        rxT = carve(4480, 3, P)
        rh = carve(0, 3, F)
        rhT = carve(768, 3, F)
        ry = carve(1536, 3, P)
        dtT = carve(0, 2, G)
        bcr = carve(1024, 1, G)
        bc_hi = carve(1536, G // 2).bitcast(BF16)[0:BC3]
        pos_part = carve(1792, 2, NB, G)
        ln_part = carve(3840, 2, NB, G)
        xaT = carve(2048, B, SP_)
        h = carve(0, 4, NB, G)
        dBu0 = carve(4096, NB, G)
        C_bc = carve(5120, 2, G)
        hT = carve(2048, FFC, G)
        ygs = carve(2048, 2, NB, G)

        ident = sb("ident", [P, P])
        ones_b = sb("ones_b", [P, P], BF16)
        below_b = sb("below_b", [P, P], BF16)
        flag_b = sb("flag_b", [P, E, NT], BF16)
        cnt_b = sb("cnt_b", [P, E], BF16)
        resets = sb("resets", [P, E, NT])
        em8 = sb("em8", [P, E, NT])
        kk = sb("kk", [P, RT, E])
        etab = sb("etab", [P, RT // 3], I32)
        same_expert = sb("same_expert", [P, P], BF16)
        digits = sb("digits", [P, 2, 3], I32)
        least_bits = sb("least_bits", [P, 2], I32)
        cand = sb("cand", [P, 2, 3], I32)
        n_reached = sb("n_reached", [P, 2, 3], BF16)
        enough = sb("enough", [P, 2, 3])
        digit = sb("digit", [P, 2], I32)
        e8i = sb("e8i", [P, E], I32)
        gate = sb("gate", [P, NT])
        pos = sb("pos", [P, NT], I32)
        one_c = sb("one_c", [P, 1])
        stats = sb("stats", [P, NT, 6])
        mean2 = sb("mean2", [P, NT])
        var4 = sb("var4", [P, NT])
        vv = sb("vv", [P, 2, NT])
        t32 = sb("t32", [P, 2, NT])
        factor = sb("factor", [P, 2, NT])
        offset = sb("offset", [P, 2, NT])
        rs, nmr, rs2, nmr2 = factor[:, 0], offset[:, 0], factor[:, 1], offset[:, 1]
        nmax = sb("nmax", [P, 2, 2])
        psum_e = sb("psum_e", [P, 2, 2])
        rinv = sb("rinv", [P, 2, 2])

        Wg_s = sb("Wg_s", [P, E])
        g1, b1 = sb("g1", [P, 1]), sb("b1", [P, 1])
        g2, b2 = sb("g2", [P, 1]), sb("b2", [P, 1])
        win_s = sb("win_s", [P, 2 * DI])
        wfold = sb("wfold", [P, TAPS, DI])
        dBu = [dBu0, wfold[:, :, :].rearrange("p k c -> p (k c)").rearrange("p (b t) -> p b t", b=NB)]
        bconv_s = sb("bconv_s", [P, NB])
        wx_s = sb("wx_s", [P, NB, R + 2 * N])
        wbc3 = sb("wbc3", [P, NB, BC3])
        wdt_s = sb("wdt_s", [R, DI])
        bdt_s = sb("bdt_s", [P, NB])
        Aneg = sb("Aneg", [P, NB, N])
        Dp_s = sb("Dp_s", [P, NB])
        diagD = sb("diagD", [P, NB, P])
        wout_s = sb("wout_s", [P, NB, D])
        wff1_s = sb("wff1_s", [P, FF])
        bff1_s = sb("bff1_s", [P, FFC])
        wff2_s = sb("wff2_s", [P, FFC, D])
        bff2_s = sb("bff2_s", [1, D])
        ones_row = sb("ones_row", [1, P])
        pick = sb("pick", [BC3, 2 * N, P], BF16)
        bc_parts = sb("bc_parts", [BC3, T], BF16)

        s_first_const = sem("s_first_const")
        s_const = sem("s_const")
        s_passed = sem("s_passed")
        s_zeros = sem("s_zeros")
        s_x = [sem(f"s_x{q}") for q in range(4)]
        s_attn_w = sem("s_attn_w")
        s_weights = sem("s_weights")
        s_experts = [sem(f"s_experts{n}") for n in range(2)]
        s_routed_clear = sem("s_routed_clear")
        v_chain, a_chain, g_chain = sem("v_chain"), sem("a_chain"), sem("g_chain")
        a_xn = sem("a_xn")
        a_xT_ps = sem("a_xT_ps")
        a_xT = sem("a_xT")
        a_uv_ps = sem("a_uv_ps")
        a_uv = sem("a_uv")
        a_sc_ps = sem("a_sc_ps")
        a_max = sem("a_max")
        a_exp = sem("a_exp")
        a_pT_ps = sem("a_pT_ps")
        a_pT = sem("a_pT")
        a_out_ps = sem("a_out_ps")
        a_fin = sem("a_fin")
        s_weights_prep = sem("s_weights_prep")
        s_conv_ps = sem("s_conv_ps")

        class Turn:
            def __init__(self, tag):
                self.xs = sem(f"{tag}_xs")
                self.ps = sem(f"{tag}_ps")
                self.xT = sem(f"{tag}_xT")

        class Ffn:
            def __init__(self, l):
                self.turn = Turn(f"f{l}")
                self.copied = sem(f"f{l}_copied")
                self.logits = sem(f"f{l}_logits")
                self.shifted = sem(f"f{l}_shifted")
                self.exps = sem(f"f{l}_exps")
                self.to_turn = sem(f"f{l}_to_turn")
                self.turned = sem(f"f{l}_turned")
                self.flags = sem(f"f{l}_flags")
                self.counts = sem(f"f{l}_counts")
                self.routed = sem(f"f{l}_routed")
                self.scattered = sem(f"f{l}_scattered")
                self.loaded = sem(f"f{l}_loaded")
                self.x_ps = sem(f"f{l}_x_ps")
                self.x = sem(f"f{l}_x")
                self.h_ps = sem(f"f{l}_h_ps")
                self.h = sem(f"f{l}_h")
                self.hT_ps = sem(f"f{l}_hT_ps")
                self.hT = sem(f"f{l}_hT")
                self.y_ps = sem(f"f{l}_y_ps")
                self.y = sem(f"f{l}_y")
                self.stored = sem(f"f{l}_stored")
                self.gathered = [sem(f"f{l}_gathered{q}") for q in range(4)]
                self.added = sem(f"f{l}_added")

        ffn = [Ffn(0), Ffn(1)]
        m_turn = Turn("m")
        m_xc_ps = sem("m_xc_ps")
        m_xc = sem("m_xc")
        m_z_ps = sem("m_z_ps")
        m_z = sem("m_z")
        m_dt_ps = sem("m_dt_ps")
        m_dt = sem("m_dt")
        m_bc_ps = sem("m_bc_ps")
        m_bc = sem("m_bc")
        m_raw_ps = sem("m_raw_ps")
        m_raw = sem("m_raw")
        m_soft = sem("m_soft")
        m_delta = sem("m_delta")
        m_du = sem("m_du")
        c_B = sem("c_B")
        c_C = sem("c_C")
        c_dBu = sem("c_dBu")
        c_decay = sem("c_decay")
        c_h = sem("c_h")
        c_C_sb = sem("c_C_sb")
        c_hC = sem("c_hC")
        c_y = sem("c_y")
        c_gated = sem("c_gated")
        p_yg = sem("p_yg")
        p_xl = sem("p_xl")
        p_out_ps = sem("p_out_ps")
        p_xa = sem("p_xa")
        d_turn = Turn("d")
        d_h_ps = sem("d_h_ps")
        d_h = sem("d_h")
        d_y_ps = sem("d_y_ps")
        d_x = sem("d_x")
        s_out = sem("s_out")

        x_tiles = x_in.rearrange("b (h p) d -> p (b h) d", p=P)
        out_tiles = out.rearrange("b (h p) d -> p (b h) d", p=P)

        def col(v, axis=1):
            return v.unsqueeze(axis)

        def over_tiles(v):
            return col(v, 2).broadcast_to([P, E, NT])

        def over_experts(v):
            return col(v, 1).broadcast_to([P, E, NT])

        def by_tile(v):
            return v.rearrange("p e j -> p j e")

        def tokens_of(g, n):
            return bass.ds(g * G + n // N * G, G)

        def rows(routed, i):
            return routed[bass.ds(i * (3 * P), 3 * P), :].rearrange("(k p) d -> p k d", p=P)

        def apart(eng, semaphore, value):
            eng.wait_ge(semaphore, value)
            eng.sem_inc(s_passed, 1)

        block = ctx.enter_context(nc.Block())

        N_WEIGHTS = 19
        FIRST = 1
        ATT_LOOP = (B - 4) // 2

        @block.sync
        def _(sp):
            for q in range(4):
                a, b = q * NT // 4, (q + 1) * NT // 4
                sp.dma_start(X[:, a:b, :], x_tiles[:, a:b, :]).then_inc(s_x[q], 16)
            sp.dma_start(qk_s[:, :], qk).then_inc(s_attn_w, 16)
            sp.dma_start(ov_s[:, :], ov).then_inc(s_attn_w, 16)

            def experts(n):
                sp.dma_start(W1s, W1.rearrange("e d f -> d e f")).then_inc(s_experts[n], 16)
                for c in range(FC):
                    sp.dma_start(W2s[:, :, c, :], W2[:, c * P:(c + 1) * P, :].rearrange("e p d -> p e d")).then_inc(
                        s_experts[n], 16)

            experts(0)

            def ld(dst, src):
                sp.dma_start(dst, src).then_inc(s_weights, 16)

            with nc.allow_non_contiguous_dma(reason="small weights"):
                ld(Wg_s[:, :], Wg)
                for v, w in ((g1, ln1_g), (b1, ln1_b), (g2, ln2_g), (b2, ln2_b)):
                    ld(v[:, :], w.rearrange("(p a) -> p a", a=1))
                ld(win_s[:, :], w_in)
                ld(wconv_row[0:1, :, :], w_conv.rearrange("(a c) k -> a k c", a=1))
                ld(bconv_s[:, :], b_conv.rearrange("(b p) -> p b", p=P))
                ld(wx_s[:, :, :], w_xproj.rearrange("(b p) r -> p b r", p=P))
                ld(wdt_s[:, :], w_dt)
                ld(bdt_s[:, :], b_dt.rearrange("(b p) -> p b", p=P))
                ld(Aneg[:, :, :], A_log.rearrange("(b p) n -> p b n", p=P))
                ld(Dp_s[:, :], Dp.rearrange("(b p) -> p b", p=P))
                ld(wout_s[:, :, :], w_out.rearrange("(b p) d -> p b d", p=P))
                ld(wff1_s[:, :], w_ff1)
                ld(bff1_s[:, :], b_ff1.rearrange("(c p) -> p c", p=P))
                ld(wff2_s[:, :, :], w_ff2.rearrange("(c p) d -> p c d", p=P))
                ld(bff2_s[0:1, :], b_ff2.rearrange("(a d) -> a d", a=1))
            sp.wait_ge(s_zeros, 1)
            sp.dma_start(routed_in.rearrange("(k p) d -> p k d", p=P),
                         col(Y[:, 0, :]).broadcast_to([P, RT, D])).then_inc(s_routed_clear, 16)

            def routed_tiles(f):
                def store(i):
                    sp.wait_ge(f.y, i + 2)
                    sp.dma_start(rows(routed_out, i), ry).then_inc(f.stored, 16)

                sp.sem_inc(f.stored, 16)
                with sp.Fori(0, RT // 3) as i:
                    store(i)

            routed_tiles(ffn[0])
            sp.wait_ge(c_gated, NG + 1)
            experts(1)
            routed_tiles(ffn[1])
            for q in range(4):
                a, b = q * NT // 4, (q + 1) * NT // 4
                sp.wait_ge(ffn[1].added, q + 1)
                sp.dma_start(out_tiles[:, a:b, :], X[:, a:b, :]).then_inc(s_out, 16)
            sp.wait_ge(s_out, 64)

        @block.gpsimd
        def _(pool):
            ch = Chain(pool, g_chain)
            pool.memset(Y[:, 0, :], 0.0).then_inc(s_zeros, 1)
            ch.step(pool.memset(ident[:, :], 0.0))
            ch.link(pool.memset(mask[:, :], 0.0))
            ch.step(pool.affine_select(out=ident[:, :], in_=ident[:, :], compare_op=ALU.not_equal, fill=1.0, base=0,
                                       pattern=[[-1, P]], channel_multiplier=1))
            ch.link(pool.affine_select(out=mask[:, P:S], in_=mask[:, P:S], compare_op=ALU.is_ge, fill=MASKED, base=0,
                                       pattern=[[-1, P]], channel_multiplier=1))
            pool.sem_inc(s_first_const, 1)
            ch.step(pool.memset(below_b[:, :], 1.0))
            ch.step(pool.memset(resets[:, :, :], 1.0))
            ch.step(pool.memset(pick[:, :, :], 0.0))
            ch.step(pool.memset(ones_b[:, :], 1.0))
            ch.step(pool.memset(ones_row[:, :], 1.0))
            ch.step(pool.memset(one_c[:, :], 1.0))
            ch.step(pool.iota(em8[:, :, :], [[1, E], [0, NT]], base=-E, channel_multiplier=0,
                              allow_small_or_imprecise_dtypes=True))
            ch.step(pool.memset(same_expert[:, :], 1.0))
            ch.step(pool.iota(digits[:, :, :], [[0, 2], [1, 3]], base=1, channel_multiplier=0))
            ch.link(pool.iota(kk[:, :, :], [[1, RT], [0, E]], base=0, channel_multiplier=0,
                              allow_small_or_imprecise_dtypes=True))
            ch.step(pool.affine_select(out=below_b[:, :], in_=below_b[:, :], compare_op=ALU.is_gt, fill=0.0, base=0,
                                       pattern=[[1, P]], channel_multiplier=-1))
            ch.step(pool.memset(resets[:, :, 0:1], 0.0))
            blocks = same_expert[:, :].rearrange("p (e j) -> p e j", j=NT)
            ch.step(pool.affine_select(out=blocks, in_=blocks, compare_op=ALU.is_ge, fill=0.0, base=0,
                                       pattern=[[-NT, P // NT], [0, NT]], channel_multiplier=1))
            ch.wait()
            ch.step(pool.affine_select(out=blocks, in_=blocks, compare_op=ALU.is_ge, fill=0.0, base=NT - 1,
                                       pattern=[[NT, P // NT], [0, NT]], channel_multiplier=-1))
            for part in range(3):
                ch.link(pool.affine_select(out=pick[:, :, :], in_=pick[:, :, :], compare_op=ALU.not_equal, fill=1.0,
                                           base=-2 * N * part, pattern=[[-1, 2 * N], [0, P]], channel_multiplier=1))
            pool.sem_inc(s_const, 1)
            pool.sem_inc(c_hC, 2)

            def routed(f):
                pool.wait_ge(f.routed, 1)
                pool.wait_ge(s_routed_clear, 16)
                pool.wait_ge(f.copied, NG + 2)
                for j in range(NT):
                    pool.indirect_dma_start(out=routed_in, out_offset=bass.IndirectOffsetOnAxis(
                        ap=pos[:, j:j + 1], axis=0), in_=XN[:, j, :], in_offset=None,
                        bounds_check=RT * P - 1).then_inc(f.scattered, 16)
                pool.wait_ge(f.stored, 16 * (RT // 3 + 1))
                for j in range(NT):
                    pool.indirect_dma_start(out=Y[:, j, :], out_offset=None, in_=routed_out,
                                            in_offset=bass.IndirectOffsetOnAxis(ap=pos[:, j:j + 1], axis=0),
                                            bounds_check=RT * P - 1).then_inc(f.gathered[j * 4 // NT], 16)

            routed(ffn[0])

            with pool.Fori(0, NG // 2) as i:
                for s in range(2):
                    at = bass.ds(i * (2 * G) + s * G, G)
                    pool.wait_ge(m_soft, i * 2 + (s + 1))
                    pool.tensor_tensor(delta[:, :, at], pos_part[:, s], ln_part[:, s], ALU.add).then_inc(m_delta, 1)
                    pool.wait_ge(m_delta, i * 2 + (s + 3))
                    pool.tensor_tensor(du[:, :, at], delta[:, :, at], xm[:, :, at], ALU.mult).then_inc(m_du, 1)
            with pool.Fori(0, NG) as g:
                for n in range(N):
                    s = n % 2
                    pool.wait_ge(c_h, g * N + (n + 3))
                    pool.wait_ge(c_C_sb, g * N + (n + 1))
                    pool.tensor_tensor(h[:, n % 4], h[:, n % 4], col(C_bc[:, s]).broadcast_to([P, NB, G]),
                                       ALU.mult).then_inc(c_hC, 1)

            routed(ffn[1])

        @block.scalar
        def _(act):
            ch = Chain(act, a_chain)
            A = nc.scalar.activation
            act.preload_act_table(ACT.Exp)

            def attend(n, c=0):
                s = (n + c) % 2 if isinstance(n, int) else c % 2

                def has(k):
                    return not isinstance(n, int) or 0 <= n + c + k < B

                if has(0):
                    act.wait_ge(a_max, (n * 2) + (2 * c + 2))
                    A(pr_a[:, s, 0:P], sc_a[:, s, 0:P], ACT.Exp, scale=-1.0, bias=nmax[:, s, 0:1],
                      accum_out=psum_e[:, s, 0:1])
                    A(pr_a[:, s, P:P + S], sc_a[:, s, P:P + S], ACT.Exp, scale=-1.0, bias=nmax[:, s, 1:2],
                      accum_out=psum_e[:, s, 1:2]).then_inc(a_exp, 1)
                if has(1):
                    act.wait_ge(a_uv_ps, n + (c + 2))
                    A(uv_a[:, 1 - s], bank[3 - s], ACT.Copy).then_inc(a_uv, 1)

            for n in range(-1, FIRST):
                attend(n)
            with act.Fori(0, ATT_LOOP) as i:
                for c in range(2):
                    attend(i * 2, FIRST + c)
            for n in range(FIRST + 2 * ATT_LOOP, B):
                attend(n)

            def route_ffn(f):
                act.sem_inc(f.copied, 2)
                act.sem_inc(f.logits, 2)
                with act.Fori(0, NG // 2) as i:
                    for s in range(2):
                        apart(act, f.turn.xs, i * 2 + (s + 1))
                        A(XN[:, bass.ds(i * (2 * GT) + s * GT, GT), :], xs[:, s], ACT.Copy).then_inc(f.copied, 1)
                    for s in range(2):
                        act.wait_ge(f.logits, i * 2 + (s + 1))
                        act.wait_ge(f.turn.ps, i * 2 + (s + 3))
                        A(xsT[:, s], bank[s], ACT.Copy).then_inc(f.turn.xT, 1)
                act.wait_ge(f.shifted, 1)
                A(pe, pe, ACT.Exp).then_inc(f.exps, 1)
                act.preload_act_table(ACT.Gelu)

                def load(i):
                    act.dma_start(xin, rows(routed_in, i)).then_inc(f.loaded, 16)

                def tiles(i):
                    for s in range(3):
                        act.wait_ge(f.h_ps, i * 3 + (s + 1))
                        A(rh[:, s], bank[s][:, 0:F], ACT.Gelu).then_inc(f.h, 1)

                act.wait_ge(f.scattered, 16 * NT)
                load(0)
                with act.Fori(0, RT // 3 - 1) as i:
                    act.wait_ge(f.x_ps, i + 1)
                    load(i + 1)
                    tiles(i)
                tiles(RT // 3 - 1)

            route_ffn(ffn[0])

            act.wait_ge(s_weights, 16 * (N_WEIGHTS - 1))
            ch.link(A(Aneg[:, :, :], Aneg[:, :, :], ACT.Exp))
            ch.link(A(Aneg[:, :, :], Aneg[:, :, :], ACT.Copy, scale=-1.0))
            act.preload_act_table(ACT.Silu)
            with act.Fori(0, NG) as g:
                at = bass.ds(g * G, G)
                apart(act, m_xc_ps, g + 1)
                for b in range(NB):
                    last = A(xm[:, b, at], bank[2 + b], ACT.Silu, bias=bconv_s[:, b:b + 1])
                last.then_inc(m_xc, 1)
                apart(act, m_z_ps, g + 1)
                for b in range(NB):
                    last = A(zs[:, b, at], bank[4 + b], ACT.Silu)
                last.then_inc(m_z, 1)
            act.preload_act_table_set("natural_log_exp_and_others")
            act.sem_inc(m_delta, 2)
            with act.Fori(0, NG // 2) as i:
                ch.loop(i, 2 * (NB + 1), NG // 2)
                for s in range(2):
                    apart(act, m_delta, i * 2 + (s + 1))
                    act.wait_ge(m_raw_ps, i * 2 + (s + 1))
                    for b in range(NB):
                        ch.step(A(ln_part[:, s, b], bank[4 + 2 * s + b], ACT.Abs, bias=bdt_s[:, b:b + 1]))
                    for b in range(NB):
                        last = A(pos_part[:, s, b], bank[4 + 2 * s + b], ACT.Relu, bias=bdt_s[:, b:b + 1])
                    last.then_inc(m_raw, 1)
                    ch.wait()
                    ch.link(A(ln_part[:, s], ln_part[:, s], ACT.Exp, scale=-1.0))
                    A(ln_part[:, s], ln_part[:, s], ACT.Ln, bias=one_c[:, 0:1]).then_inc(m_soft, 1)
            ch.end()

            act.wait_ge(m_du, NG)
            with act.Fori(0, NG) as g:
                for n in range(N):
                    s = n % 2
                    apart(act, c_h, g * N + (n + 1))
                    for b in range(NB):
                        d = delta[:, b, bass.ds(g * G, G)].rearrange("p (q t) -> p q t", q=GB)[:, :, 1:S]
                        o = decay_ps[:, s, b, :].rearrange("p (q t) -> p q t", q=GB)[:, :, 1:S]
                        last = A(o, d, ACT.Exp, scale=Aneg[:, b, n:n + 1])
                    last.then_inc(c_decay, 1)
                    act.wait_ge(c_C, g * N + (n + 1))
                    act.wait_ge(c_hC, g * N + (n + 1))
                    A(C_bc[:, s], bank[3], ACT.Copy).then_inc(c_C_sb, 1)

            with act.Fori(0, NG // 2) as i:
                for s in range(2):
                    if s == 0:
                        act.wait_ge(c_gated, NG + 1)
                    apart(act, p_xa, i * 2 + (s + 1))
                    A(ygs[:, s], xm[:, :, bass.ds(i * (2 * G) + s * G, G)], ACT.Copy).then_inc(p_yg, 1)
                    for q in range(GT):
                        j = i * (2 * GT) + (s * GT + q)
                        last = A(XA[:, bass.ds(j, 1), :], X[:, bass.ds(j, 1), :], ACT.Identity,
                                 scale=rs[:, bass.ds(j, 1)], bias=nmr[:, bass.ds(j, 1)])
                    last.then_inc(p_xl, 1)
            act.preload_act_table(ACT.Gelu_apprx_tanh)
            with act.Fori(0, NG) as g:
                for c in range(FFC):
                    act.wait_ge(d_h_ps, g * FFC + (c + 1))
                    A(hT[:, c], bank[2 + c], ACT.Gelu_apprx_tanh, bias=bff1_s[:, c:c + 1]).then_inc(d_h, 1)
            route_ffn(ffn[1])

        @block.vector
        def _(dve):
            V = nc.vector
            ch = Chain(dve, v_chain)
            def norm_factors(j0=0, j1=NT, twice=False):
                st, k = stats[:, j0:j1, :], 2 if twice else 1
                mean, var = mean2[:, j0:j1], var4[:, j0:j1]
                v, t, r, o = (x[:, 0:k, j0:j1] for x in (vv, t32, factor, offset))
                ch.step(V.tensor_tensor(mean, st[:, :, 1], st[:, :, 4], ALU.add))
                ch.step(V.tensor_tensor(var, st[:, :, 1], st[:, :, 4], ALU.subtract))
                ch.link(V.tensor_tensor(t[:, 0], st[:, :, 2], st[:, :, 5], ALU.add))
                ch.link(V.tensor_tensor(var, var, var, ALU.mult))
                ch.link(V.scalar_tensor_tensor(out=var, in0=t[:, 0], scalar=4.0 / D, in1=var, op0=ALU.mult,
                                               op1=ALU.add))
                if twice:
                    ch.step(V.tensor_scalar(v[:, 1], var, 0.25 * (1 + EPS), EPS * EPS, ALU.mult, ALU.add))
                ch.link(V.tensor_scalar(v[:, 0], var, 0.25, EPS, ALU.mult, ALU.add))
                ch.link(V.tensor_scalar(r.bitcast(I32), v.bitcast(I32), 1, None, ALU.logical_shift_right))
                ch.link(V.tensor_scalar(r.bitcast(I32), r.bitcast(I32), -1.0, float(0x5f3759df), ALU.mult, ALU.add))
                for _ in range(3):
                    ch.link(V.scalar_tensor_tensor(out=t, in0=r, scalar=-0.5, in1=r, op0=ALU.mult, op1=ALU.mult))
                    ch.link(V.tensor_tensor(t, t, v, ALU.mult))
                    ch.link(V.scalar_tensor_tensor(out=r, in0=t, scalar=1.5, in1=r, op0=ALU.add, op1=ALU.mult))
                ch.link(V.scalar_tensor_tensor(out=o, in0=col(mean).broadcast_to([P, k, j1 - j0]), scalar=-0.5,
                                               in1=r, op0=ALU.mult, op1=ALU.mult))

            def one(tile, j):
                return tile[:, bass.ds(j, 1), :].rearrange("p a d -> p (a d)")

            def tile_stats(tile, j):
                return V.bn_stats(one(stats, j), one(tile, j))

            def normed(dst, src, j, r, m):
                return V.tensor_scalar(dst, one(src, j), r[:, bass.ds(j, 1)], m[:, bass.ds(j, 1)], ALU.mult, ALU.add)

            for j in range(NT):
                if j % (NT // 4) == 0:
                    dve.wait_ge(s_x[j * 4 // NT], 16)
                ch.step(tile_stats(X, j))
            ch.wait()
            norm_factors()
            dve.wait_ge(s_first_const, 1)

            def attend(n, c=0):
                s = (n + c) % 2 if isinstance(n, int) else c % 2
                r = 1 - s

                def has(k):
                    return not isinstance(n, int) or 0 <= n + c + k < B

                if has(-1):
                    dve.wait_ge(a_pT_ps, n + c)
                    V.tensor_copy(pT_a[:, r], bank[6 + r][:, 0:384]).then_inc(a_pT, 1)
                if has(0):
                    apart(dve, a_sc_ps, n + (c + 1))
                    V.tensor_tensor_reduce(sc_a[:, s, 0:P], bank[4 + s][:, 0:P], mask[:, P:S], -1.0 / D ** 0.5,
                                           3e38, ALU.add, ALU.min, nmax[:, s, 0:1]).then_inc(a_max, 1)
                    V.tensor_tensor_reduce(sc_a[:, s, P:P + S], bank[4 + s][:, P:P + S], mask[:, :], -1.0 / D ** 0.5,
                                           3e38, ALU.add, ALU.min, nmax[:, s, 1:2]).then_inc(a_max, 1)
                if has(2):
                    dve.wait_ge(a_xT_ps, n + (c + 3))
                    V.tensor_copy(xT_a[:, s], bank[s][:, 0:S]).then_inc(a_xT, 1)
                if has(3):
                    for k in range(2):
                        last = normed(xn_a[:, r, k, :], X, n * 2 + (2 * (c + 3) + k), rs, nmr)
                    last.then_inc(a_xn, 1)
                if has(-1):
                    dve.wait_ge(a_exp, n + c)
                    ch.link(V.reciprocal(rinv[:, r], psum_e[:, r]))
                    dve.wait_ge(a_out_ps, n + c)
                    for k in range(2):
                        xt = one(X, n * 2 + (2 * (c - 1) + k))
                        last = V.scalar_tensor_tensor(out=xt, in0=bank[4 + r][:, k * P:(k + 1) * P],
                                                      scalar=rinv[:, r, k:k + 1], in1=xt, op0=ALU.mult, op1=ALU.add)
                        if k == 0:
                            ch.step(last)
                    last.then_inc(a_fin, 1)
                    apart(dve, a_fin, n + (c + 2))
                    for k in range(2):
                        ch.step(tile_stats(X, n * 2 + (2 * (c - 1) + k)))

            for n in range(-3, FIRST):
                attend(n)
            with dve.Fori(0, ATT_LOOP) as i:
                ch.loop(i, 2 * 4, ATT_LOOP)
                for c in range(2):
                    attend(i * 2, FIRST + c)
            ch.end()
            for n in range(FIRST + 2 * ATT_LOOP, B + 1):
                attend(n)
            ch.wait()
            dve.wait_ge(s_const, 1)

            def route_ffn(f):
                norm_factors()
                with dve.Fori(0, NG // 2) as i:
                    for s in range(2):
                        dve.wait_ge(f.copied, i * 2 + (s + 1))
                        apart(dve, f.turn.ps, i * 2 + (s + 1))
                        for q in range(GT):
                            last = normed(xs[:, s, q, :], X, i * (2 * GT) + (s * GT + q), rs, nmr)
                        last.then_inc(f.turn.xs, 1)
                logits = bank[2][:, 0:E * NT].rearrange("p (e j) -> p e j", e=E)
                dve.wait_ge(f.logits, NG + 2)
                ch.link(V.tensor_reduce(tl, by_tile(logits), AX, ALU.max))
                V.tensor_tensor(pe, logits, over_experts(tl), ALU.subtract).then_inc(f.shifted, 1)
                dve.wait_ge(f.exps, 1)
                ch.link(V.tensor_reduce(tl, by_tile(pe), AX, ALU.add))
                ch.link(V.reciprocal(tl, tl))
                V.tensor_tensor(prob, pe, over_experts(tl), ALU.mult).then_inc(f.to_turn, 1)
                ch.step(V.tensor_scalar(cand[:, :, :], digits[:, :, :], 2 * (DIGITS - 1), None,
                                        ALU.logical_shift_left))
                ch.step(V.memset(least_bits[:, :], 0))
                dve.wait_ge(f.turned, 1)
                ch.link(V.tensor_copy(probT, bank[4][:, 0:2 * P].rearrange("p (h t) -> p h t", h=2)))
                for k in range(DIGITS):
                    shift = 2 * (DIGITS - 1 - k)
                    with nc.allow_low_precision(reason="counts up to 128 are exact"):
                        for half in range(2):
                            for c in range(3):
                                last = V.tensor_scalar(reached[:, half, c], probT[:, half],
                                                       cand[:, half, c:c + 1].bitcast(F32), 0.0, ALU.is_ge, ALU.add,
                                                       accum_out=n_reached[:, half, c:c + 1])
                    last.then_inc(f.flags, 1)
                    dve.wait_ge(f.counts, k + 1)
                    ch.link(V.tensor_scalar(enough[:, :, :], bank[3][:, 0:6].rearrange("p (h c) -> p h c", h=2),
                                            CAP - 0.5, None, ALU.is_ge))
                    with nc.allow_low_precision(reason="0 to 3"):
                        ch.link(V.tensor_reduce(digit[:, :], enough[:, :, :], AX, ALU.add))
                    ch.link(V.scalar_tensor_tensor(out=least_bits[:, :], in0=digit[:, :], scalar=shift,
                                                   in1=least_bits[:, :], op0=ALU.logical_shift_left,
                                                   op1=ALU.bitwise_or))
                    if shift:
                        ch.link(V.scalar_tensor_tensor(out=cand[:, :, :], in0=digits[:, :, :], scalar=shift - 2,
                                                       in1=col(least_bits[:, :], 2).broadcast_to([P, 2, 3]),
                                                       op0=ALU.logical_shift_left, op1=ALU.bitwise_or))
                V.tensor_copy(thr_row, col(least_bits[:, :].bitcast(F32), 2).broadcast_to([P, 2, P])).then_inc(
                    f.to_turn, 1)
                dve.wait_ge(f.turned, 2)
                thr = bank[4][:, 0:E * NT].rearrange("p (e j) -> p e j", e=E)
                above, least, need = fA, fB, e8[:, 0]
                ch.link(V.tensor_tensor(above, prob, thr, ALU.is_gt))
                with nc.allow_low_precision(reason="counts up to 32 are exact"):
                    V.tensor_reduce(cnt_b[:, :], above, AX, ALU.add).then_inc(f.flags, 1)
                ch.step(V.tensor_tensor(least, prob, thr, ALU.is_equal))
                dve.wait_ge(f.counts, DIGITS + 1)
                ch.link(V.tensor_scalar(need, bank[3][:, 0:E], -1.0, float(CAP), ALU.mult, ALU.add))
                V.tensor_copy(flag_b[:, :, :], least).then_inc(f.flags, 1)

                def before(n, dst):
                    within = bank[0][:, 0:E * NT].rearrange("p (e j) -> p e j", e=E)
                    totals = bank[1][:, 0:E * NT]
                    dve.wait_ge(f.counts, n)
                    flat = incl.rearrange("p e j -> p (e j)")
                    ch.link(V.tensor_tensor_scan(flat, resets[:, :, :].rearrange("p e j -> p (e j)"), totals, 0.0,
                                                 ALU.mult, ALU.add))
                    ch.link(V.tensor_tensor(dst, incl, totals.rearrange("p (e j) -> p e j", e=E), ALU.subtract))
                    ch.link(V.tensor_tensor(dst, dst, within, ALU.add))

                before(DIGITS + 2, fC)
                ch.link(V.tensor_tensor(fC, fC, over_tiles(need), ALU.is_lt))
                ch.link(V.tensor_tensor(fC, fC, least, ALU.mult))
                ch.link(V.tensor_tensor(sel, fC, above, ALU.add))
                ch.link(V.tensor_reduce(tl, by_tile(sel), AX, ALU.max))
                ch.link(V.tensor_scalar(tl, tl, -1.0, 1.0, ALU.mult, ALU.add))
                ch.link(V.tensor_tensor(sel, sel, over_experts(tl), ALU.max))
                ch.link(V.tensor_tensor(fA, prob, sel, ALU.mult))
                ch.link(V.scalar_tensor_tensor(out=fA.rearrange("p e j -> p (e j)"),
                                               in0=sel.rearrange("p e j -> p (e j)"), scalar=-1.0,
                                               in1=fA.rearrange("p e j -> p (e j)"), op0=ALU.add, op1=ALU.add))
                ch.link(V.tensor_reduce(gate[:, :], by_tile(fA), AX, ALU.max))
                ch.link(V.tensor_tensor(fB, fA, over_experts(gate[:, :]), ALU.is_equal))
                ch.link(V.tensor_tensor(fB, fB, em8[:, :, :], ALU.mult))
                ch.link(V.tensor_reduce(tl, by_tile(fB), AX, ALU.min))
                ch.link(V.tensor_tensor(fA, em8[:, :, :], over_experts(tl), ALU.is_equal))
                V.tensor_copy(flag_b[:, :, :], fA).then_inc(f.flags, 1)
                before(DIGITS + 3, fC)
                ch.link(V.tensor_scalar(e8i[:, :], incl[:, :, NT - 1], float(P - 1), None, ALU.add))
                ch.link(V.tensor_scalar(e8i[:, :], e8i[:, :], P.bit_length() - 1, None, ALU.logical_shift_right))
                ch.step(V.memset(e8[:, 2], 1.0))
                ch.link(V.tensor_copy(e8[:, 1], e8i[:, :]))
                ch.link(V.tensor_tensor_scan(e8[:, 3], e8[:, 2], e8[:, 1], 0.0, ALU.mult, ALU.add))
                ch.link(V.tensor_tensor(e8[:, 4], e8[:, 3], e8[:, 1], ALU.subtract))
                ch.link(V.tensor_scalar(e8[:, 5], e8[:, 4], float(P), None, ALU.mult))
                ch.link(V.tensor_tensor(fC, fC, over_tiles(e8[:, 5]), ALU.add))
                ch.link(V.tensor_tensor(fC, fC, fA, ALU.mult))
                ch.link(V.tensor_reduce(pos_f[:, :], by_tile(fC), AX, ALU.add))
                ch.link(V.tensor_tensor(kcmp[:, :, :], col(e8[:, 3]).broadcast_to([P, RT, E]), kk[:, :, :], ALU.is_le))
                ch.link(V.tensor_reduce(ktab[:, :], kcmp[:, :, :], AX, ALU.add))
                ch.link(V.tensor_scalar(ktab[:, :], ktab[:, :], float(E - 1), None, ALU.min))
                three = ktab[:, :].rearrange("p (i s) -> p i s", s=3)
                ch.link(V.scalar_tensor_tensor(out=three[:, :, 1], in0=three[:, :, 2], scalar=float(E),
                                               in1=three[:, :, 1], op0=ALU.mult, op1=ALU.add))
                ch.link(V.scalar_tensor_tensor(out=etab[:, :], in0=three[:, :, 1], scalar=float(E),
                                               in1=three[:, :, 0], op0=ALU.mult, op1=ALU.add))
                V.tensor_copy(pos[:, :], pos_f[:, :]).then_inc(f.routed, 1)

                def turned_tiles(i):
                    dve.wait_ge(f.x_ps, i + 1)
                    V.tensor_copy(rxT, bank[6][:, 0:3 * P].rearrange("p (s t) -> p s t", s=3)).then_inc(f.x, 1)

                def tiles(i, more):
                    if more:
                        turned_tiles(i + 1)
                    for s in range(3):
                        dve.wait_ge(f.hT_ps, i * 3 + (s + 1))
                        V.tensor_copy(rhT[:, s], bank[3 + s][:, 0:F]).then_inc(f.hT, 1)
                    dve.wait_ge(f.stored, i * 16 + 16)
                    dve.wait_ge(f.y_ps, i + 1)
                    V.tensor_copy(ry, bank[7][:, 0:3 * P].rearrange("p (s d) -> p s d", s=3)).then_inc(f.y, 1)

                turned_tiles(0)
                with dve.Fori(0, RT // 3 - 1) as i:
                    tiles(i, True)
                tiles(RT // 3 - 1, False)

            def gathered_quarter(f, q):
                dve.wait_ge(f.gathered[q], 16 * NT // 4)
                for j in range(q * NT // 4, (q + 1) * NT // 4):
                    ch.step(V.scalar_tensor_tensor(out=X[:, j, :], in0=Y[:, j, :], scalar=gate[:, j:j + 1],
                                                   in1=X[:, j, :], op0=ALU.mult, op1=ALU.add))
                ch.wait()

            route_ffn(ffn[0])

            dve.wait_ge(s_weights, 16 * (N_WEIGHTS - 1))
            for k in range(TAPS):
                if k % 2 == 0:
                    dve.wait_ge(s_conv_ps, k // 2 + 1)
                V.tensor_tensor(wfold[:, k, :], win_s[:, 0:DI], bank[6 + k // 2][:, (k % 2) * DI:(k % 2 + 1) * DI],
                                ALU.mult).then_inc(s_weights_prep, 1)
            for b in range(NB):
                for c in range(3):
                    V.tensor_copy(wbc3[:, b, c * 2 * N:(c + 1) * 2 * N], wx_s[:, b, R:R + 2 * N]).then_inc(
                        s_weights_prep, 1)
                V.tensor_scalar(diagD[:, b, :], ident[:, :], Dp_s[:, b:b + 1], None, ALU.mult).then_inc(
                    s_weights_prep, 1)
            ch.link(V.memset(xaT[:, :, 0:PAD], 0.0))

            def normed_group(g):
                for q in range(GT):
                    last = normed(xs[:, 0, q, :], X, g * GT + q, rs2, nmr2)
                last.then_inc(m_turn.xs, 1)
                dve.wait_ge(m_turn.ps, g + 1)
                V.tensor_scalar(xaT[:, bass.ds(g * GB, GB), PAD:SP_], bank[0].rearrange("p (q t) -> p q t", q=GB),
                                g1[:, 0:1], b1[:, 0:1], ALU.mult, ALU.add).then_inc(m_turn.xT, 1)

            for q in range(4):
                gathered_quarter(ffn[0], q)
                j0, j1 = q * NT // 4, (q + 1) * NT // 4
                for j in range(j0, j1):
                    ch.step(tile_stats(X, j))
                ch.wait()
                norm_factors(j0, j1, twice=True)
                for g in range(q * NG // 4, (q + 1) * NG // 4):
                    normed_group(g)

            with dve.Fori(0, NG // 2) as i:
                ch.loop(i, 2 * 6, NG // 2)
                for s in range(2):
                    dve.wait_ge(m_dt_ps, i * 2 + (s + 1))
                    V.tensor_copy(dtT[0:R, s], bank[s][0:R, :]).then_inc(m_dt, 1)
                    dve.wait_ge(m_bc_ps, i * 2 + (s + 1))
                    at = bass.ds(i * (2 * G) + s * G, G)
                    bc, rest = bank[2 + s][0:BC3, :], bcr[0:BC3, 0]
                    ch.link(V.tensor_copy(bc_hi[:, :], bc))
                    ch.step(V.tensor_copy(bc_parts[0:2 * N, at], bc_hi[0:2 * N, :]))
                    ch.link(V.tensor_tensor(rest, bc, bc_hi[:, :], ALU.subtract))
                    ch.link(V.tensor_copy(bc_hi[:, :], rest))
                    ch.step(V.tensor_copy(bc_parts[2 * N:4 * N, at], bc_hi[2 * N:4 * N, :]))
                    ch.link(V.tensor_tensor(rest, rest, bc_hi[:, :], ALU.subtract))
                    V.tensor_copy(bc_parts[4 * N:6 * N, at], rest[4 * N:6 * N]).then_inc(m_bc, 1)
                    dve.wait_ge(m_bc, i * 2 + (s + 3))
            ch.end()

            dve.wait_ge(m_soft, NG)
            V.memset(decay_ps[:, :, :, 0:G:S], 0.0).then_inc(c_h, 1)
            dve.wait_ge(c_h, 1)
            dve.sem_inc(c_h, 1)
            dve.sem_inc(c_dBu, 1)
            dve.sem_inc(c_gated, 1)
            dve.wait_ge(m_du, NG)

            def times_B(g, n):
                m = g * N + n
                dve.wait_ge(c_h, m + 1)
                dve.wait_ge(c_B, m + 1)
                V.tensor_tensor(dBu[n % 2], du[:, :, tokens_of(g, n)], col(bank[2]).broadcast_to([P, NB, G]),
                                ALU.mult).then_inc(c_dBu, 1)

            def scan(g, n):
                m = g * N + n
                dve.wait_ge(c_dBu, m + 2)
                dve.wait_ge(c_decay, m + 1)
                dve.wait_ge(c_y, m + 1)
                V.tensor_tensor_scan(h[:, n % 4].rearrange("p b t -> p (b t)"),
                                     decay_ps[:, n % 2].rearrange("p b t -> p (b t)"),
                                     dBu[n % 2].rearrange("p b t -> p (b t)"), 0.0, ALU.mult, ALU.add).then_inc(c_h, 1)

            def gated(g):
                dve.wait_ge(c_y, g * N + (N + 4))
                at = tokens_of(g, 0)
                for b in range(NB):
                    last = V.tensor_tensor(xm[:, b, at], bank[b], zs[:, b, at], ALU.mult)
                last.then_inc(c_gated, 1)

            times_B(0, 0)
            for n in range(2):
                times_B(0, n + 1)
                scan(0, n)
            with dve.Fori(0, NG - 1) as g:
                for n in range(2, N + 2):
                    times_B(g, n + 1)
                    scan(g, n)
                gated(g)
            for n in range(2, N):
                if n + 1 < N:
                    times_B(NG - 1, n + 1)
                scan(NG - 1, n)
            gated(NG - 1)

            with dve.Fori(0, NG // 2) as i:
                ch.loop(i, 2 * GT, NG // 2)
                for s in range(2):
                    dve.wait_ge(p_xl, i * 2 + (s + 1))
                    dve.wait_ge(p_out_ps, i * 2 + (s + 1))
                    xa = XA[:, bass.ds(i * (2 * GT) + s * GT, GT), :]
                    V.tensor_tensor(xa, xa, bank[s].rearrange("p (q d) -> p q d", q=GT), ALU.add).then_inc(p_xa, 1)
                    apart(dve, p_xa, i * 2 + (s + 3))
                    for q in range(GT):
                        ch.step(tile_stats(XA, i * (2 * GT) + (s * GT + q)))
            ch.end()
            ch.wait()
            norm_factors()
            def normed_group(g):
                for q in range(GT):
                    last = normed(xs[:, 0, q, :], XA, g * GT + q, rs, nmr)
                last.then_inc(d_turn.xs, 1)

            def turned_group(g):
                dve.wait_ge(d_turn.ps, g + 1)
                V.tensor_scalar(xsT[:, 0], bank[0], g2[:, 0:1], b2[:, 0:1], ALU.mult, ALU.add).then_inc(
                    d_turn.xT, 1)

            def dense_out(g, more):
                if more:
                    normed_group(g + 1)
                xt, xa = X[:, bass.ds(g * GT, GT), :], XA[:, bass.ds(g * GT, GT), :]
                ch.step(V.tensor_tensor(xt, xt, xa, ALU.add))
                if more:
                    turned_group(g + 1)
                ch.wait()
                dve.wait_ge(d_y_ps, g + 1)
                V.tensor_tensor(xt, xt, bank[1].rearrange("p (q d) -> p q d", q=GT), ALU.add).then_inc(d_x, 1)
                apart(dve, d_x, g + 2)
                for q in range(GT):
                    ch.step(tile_stats(X, g * GT + q))

            normed_group(0)
            turned_group(0)
            with dve.Fori(0, NG - 1) as g:
                ch.loop(g, 1 + GT, NG - 1)
                dense_out(g, True)
            ch.end()
            dense_out(NG - 1, False)
            ch.wait()
            route_ffn(ffn[1])
            for q in range(4):
                gathered_quarter(ffn[1], q)
                dve.sem_inc(ffn[1].added, 1)

        @block.tensor
        def _(pe_):
            mm, tr = nc.tensor.matmul, nc.tensor.transpose
            pe_.wait_ge(s_first_const, 1)
            pe_.wait_ge(s_attn_w, 32)
            pe_.sem_inc(a_fin, 2)

            def attend(n, c=0):
                s = (n + c) % 2 if isinstance(n, int) else c % 2
                r = 1 - s

                def has(k):
                    return not isinstance(n, int) or 0 <= n + c + k < B

                if has(-1):
                    pe_.wait_ge(a_exp, n + c)
                    for k in range(3):
                        last = tr(bank[6 + r][:, k * P:(k + 1) * P], pr_a[:, r, k * P:(k + 1) * P], ident[:, :])
                    last.then_inc(a_pT_ps, 1)
                if has(2):
                    pe_.wait_ge(a_xn, n + (c + 3))
                    for k in range(2):
                        last = tr(bank[s][:, k * P:(k + 1) * P], xn_a[:, s, k, :], ident[:, :])
                    last.then_inc(a_xT_ps, 1)
                if has(0):
                    pe_.wait_ge(a_uv, n + (c + 1))
                    pe_.wait_ge(a_fin, n + (c + 1))
                    mm(bank[4 + s][:, 0:P], uv_a[:, s, 0:P], xT_a[:, s, 0:P], start=True, stop=True)
                    mm(bank[4 + s][:, P:P + S], uv_a[:, s, P:S], xT_a[:, s, :], start=True,
                       stop=True).then_inc(a_sc_ps, 1)
                if has(-1):
                    pe_.wait_ge(a_pT, n + c)
                    v = [uv_a[:, r, S + k * P:S + (k + 1) * P] for k in range(2)]
                    mm(bank[4 + r][:, 0:P], pT_a[:, r, 0:P], v[0], start=True, stop=True)
                    mm(bank[4 + r][:, P:S], pT_a[:, r, P:2 * P], v[0], start=True, stop=False)
                    mm(bank[4 + r][:, P:S], pT_a[:, r, 2 * P:3 * P], v[1], start=False,
                       stop=True).then_inc(a_out_ps, 1)
                if has(1):
                    pe_.wait_ge(a_xT, n + (c + 2))
                    mm(bank[2 + r][:, 0:S], qk_s[:, :], xT_a[:, r], start=True, stop=True)
                    for k in range(2):
                        last = mm(bank[2 + r][:, S + k * P:S + (k + 1) * P], xT_a[:, r, k * P:(k + 1) * P],
                                  ov_s[:, :], start=True, stop=True)
                    last.then_inc(a_uv_ps, 1)

            for n in range(-2, FIRST):
                attend(n)
            with pe_.Fori(0, ATT_LOOP) as i:
                for c in range(2):
                    attend(i * 2, FIRST + c)
            for n in range(FIRST + 2 * ATT_LOOP, B + 1):
                attend(n)
            pe_.wait_ge(s_const, 1)
            pe_.wait_ge(s_weights, 16 * (N_WEIGHTS - 1))

            def route_ffn(f, n):
                pe_.sem_inc(f.turn.ps, 2)
                with pe_.Fori(0, NG // 2) as i:
                    for s in range(2):
                        pe_.wait_ge(f.turn.xs, i * 2 + (s + 1))
                        for q in range(GT):
                            last = tr(bank[s][:, q * P:(q + 1) * P], xs[:, s, q, :], ident[:, :])
                        last.then_inc(f.turn.ps, 1)
                    for s in range(2):
                        pe_.wait_ge(f.turn.xT, i * 2 + (s + 1))
                        for q in range(GT):
                            j = i * (2 * GT) + (s * GT + q)
                            o = bank[2][:, 0:E * NT].rearrange("p (e j) -> p e j", e=E)[:, :, bass.ds(j, 1)]
                            last = mm(o.rearrange("p e a -> p (e a)"), xsT[:, s, q * P:(q + 1) * P], Wg_s[:, :],
                                      start=True, stop=True)
                        last.then_inc(f.logits, 1)

                def turn(x):
                    for half in range(2):
                        last = tr(bank[4][:, half * P:(half + 1) * P], x[:, half * P:(half + 1) * P], ident[:, :])
                    last.then_inc(f.turned, 1)

                pe_.wait_ge(f.to_turn, 1)
                turn(prob.rearrange("p e j -> p (e j)"))
                for k in range(DIGITS):
                    pe_.wait_ge(f.flags, k + 1)
                    mm(bank[3][:, 0:6], same_expert[:, :], n_reached[:, :, :].rearrange("p h c -> p (h c)"),
                       start=True, stop=True).then_inc(f.counts, 1)
                pe_.wait_ge(f.to_turn, 2)
                turn(thr_row.rearrange("p h t -> p (h t)"))
                pe_.wait_ge(f.flags, DIGITS + 1)
                mm(bank[3][:, 0:E], ones_b[:, :], cnt_b[:, :], start=True, stop=True).then_inc(f.counts, 1)
                flags = flag_b[:, :, :].rearrange("p e j -> p (e j)")
                for n_flags in (DIGITS + 2, DIGITS + 3):
                    pe_.wait_ge(f.flags, n_flags)
                    mm(bank[0][:, 0:E * NT], below_b[:, :], flags, start=True, stop=True)
                    mm(bank[1][:, 0:E * NT], ones_b[:, :], flags, start=True, stop=True).then_inc(f.counts, 1)
                pe_.wait_ge(f.routed, 1)
                pe_.wait_ge(s_experts[n], 16 * (1 + FC))
                pe_.sem_inc(f.y, 1)

                def turned_tiles(i):
                    pe_.wait_ge(f.loaded, i * 16 + 16)
                    for s in range(3):
                        last = tr(bank[6][:, s * P:(s + 1) * P], xin[:, s, :], ident[:, :])
                    last.then_inc(f.x_ps, 1)

                def tiles(i, more):
                    three = pe_.value_load(etab[0:1, bass.ds(i, 1)], min_val=0, max_val=E ** 3 - 1)
                    who = [three % E, three // E % E, three // (E * E)]
                    pe_.wait_ge(f.x, i + 1)
                    for s in range(3):
                        mm(bank[s][:, 0:F], rxT[:, s], W1s[:, bass.ds(who[s], 1), :].rearrange("p a f -> p (a f)"),
                           start=True, stop=True).then_inc(f.h_ps, 1)
                    if more:
                        turned_tiles(i + 1)
                    for s in range(3):
                        pe_.wait_ge(f.h, i * 3 + (s + 1))
                        for c in range(FC):
                            last = tr(bank[3 + s][:, c * P:(c + 1) * P], rh[:, s, c * P:(c + 1) * P], ident[:, :])
                        last.then_inc(f.hT_ps, 1)
                    pe_.wait_ge(f.y, i + 1)
                    for s in range(3):
                        pe_.wait_ge(f.hT, i * 3 + (s + 1))
                        for c in range(FC):
                            last = mm(bank[7][:, s * P:(s + 1) * P], rhT[:, s, c * P:(c + 1) * P],
                                      W2s[:, bass.ds(who[s], 1), c, :].rearrange("p a d -> p (a d)"),
                                      start=(c == 0), stop=(c == FC - 1))
                    last.then_inc(f.y_ps, 1)

                turned_tiles(0)
                with pe_.Fori(0, RT // 3 - 1) as i:
                    tiles(i, True)
                tiles(RT // 3 - 1, False)
                pe_.wait_ge(f.y, RT // 3 + 1)

            route_ffn(ffn[0], 0)

            for k in range(TAPS):
                last = mm(bank[6 + k // 2][:, (k % 2) * DI:(k % 2 + 1) * DI], ones_row[0:1, :], wconv_row[0:1, k, :],
                          start=True, stop=True)
                if k % 2:
                    last.then_inc(s_conv_ps, 1)
            pe_.wait_ge(s_weights_prep, TAPS + NB * 4)

            def turned_group(turn, g):
                pe_.wait_ge(turn.xs, g + 1)
                for q in range(GT):
                    last = tr(bank[0][:, q * P:(q + 1) * P], xs[:, 0, q, :], ident[:, :])
                last.then_inc(turn.ps, 1)

            pe_.sem_inc(m_xc, 1)
            pe_.sem_inc(m_z, 1)

            def in_proj(g, more):
                seqs = bass.ds(g * GB, GB)
                pe_.wait_ge(m_turn.xT, g + 1)
                pe_.wait_ge(m_xc, g + 1)
                for b in range(NB):
                    for k in range(TAPS):
                        last = mm(bank[2 + b], wfold[:, k, b * P:(b + 1) * P], xaT[:, seqs, k:k + S],
                                  start=(k == 0), stop=(k == TAPS - 1))
                last.then_inc(m_xc_ps, 1)
                if more:
                    turned_group(m_turn, g + 1)
                pe_.wait_ge(m_z, g + 1)
                for b in range(NB):
                    last = mm(bank[4 + b], win_s[:, DI + b * P:DI + (b + 1) * P], xaT[:, seqs, PAD:SP_],
                              start=True, stop=True)
                last.then_inc(m_z_ps, 1)

            turned_group(m_turn, 0)
            with pe_.Fori(0, NG - 1) as g:
                in_proj(g, True)
            in_proj(NG - 1, False)
            pe_.wait_ge(m_xc, NG + 1)

            pe_.sem_inc(m_bc, 2)
            pe_.sem_inc(m_raw, 2)
            with pe_.Fori(0, NG // 2) as i:
                def to_dt(s):
                    at = bass.ds(i * (2 * G) + s * G, G)
                    for b in range(NB):
                        last = mm(bank[s][0:R, :], wx_s[:, b, 0:R], xm[:, b, at], start=(b == 0), stop=(b == NB - 1))
                    last.then_inc(m_dt_ps, 1)

                def to_bc(s):
                    at = bass.ds(i * (2 * G) + s * G, G)
                    pe_.wait_ge(m_bc, i * 2 + (s + 1))
                    for b in range(NB):
                        last = mm(bank[2 + s][0:BC3, :], wbc3[:, b, :], xm[:, b, at], start=(b == 0),
                                  stop=(b == NB - 1))
                    last.then_inc(m_bc_ps, 1)

                def to_raw(s):
                    pe_.wait_ge(m_z, NG + 1)
                    pe_.wait_ge(m_dt, i * 2 + (s + 1))
                    pe_.wait_ge(m_raw, i * 2 + (s + 1))
                    for b in range(NB):
                        last = mm(bank[4 + 2 * s + b], wdt_s[:, b * P:(b + 1) * P], dtT[0:R, s], start=True,
                                  stop=True)
                    last.then_inc(m_raw_ps, 1)

                to_dt(0)
                to_bc(0)
                to_dt(1)
                to_raw(0)
                to_bc(1)
                to_raw(1)

            pe_.wait_ge(m_bc, NG + 2)
            pe_.sem_inc(c_y, 4)

            def pick_B(g, n):
                pe_.wait_ge(c_dBu, g * N + (n + 1))
                mm(bank[2], pick[:, n % N, :], bc_parts[:, tokens_of(g, n)], start=True, stop=True).then_inc(c_B, 1)

            def pick_C(g, n):
                if n > 0:
                    pe_.wait_ge(c_C_sb, g * N + n)
                mm(bank[3], pick[:, N + n % N, :], bc_parts[:, tokens_of(g, n)], start=True, stop=True).then_inc(
                    c_C, 1)

            def sum_state(g, n):
                if n == 0:
                    pe_.wait_ge(c_gated, g + 1)
                    for b in range(NB):
                        mm(bank[b], diagD[:, b, :], xm[:, b, tokens_of(g, 0)], start=True, stop=False)
                pe_.wait_ge(c_hC, g * N + (n + 3))
                for b in range(NB):
                    last = mm(bank[b], ident[:, :], h[:, n % 4, b, :], start=False, stop=(n == N - 1))
                last.then_inc(c_y, 1)

            pick_B(0, 0)
            pick_C(0, 0)
            pick_B(0, 1)
            for n in range(2):
                pick_B(0, n + 2)
                pick_C(0, n + 1)
            with pe_.Fori(0, NG - 1) as g:
                for n in range(2, N + 2):
                    sum_state(g, n - 2)
                    pick_B(g, n + 2)
                    pick_C(g, n + 1)
            for n in range(2, N + 2):
                sum_state(NG - 1, n - 2)
                if n + 2 < N:
                    pick_B(NG - 1, n + 2)
                if n + 1 < N:
                    pick_C(NG - 1, n + 1)

            for s in range(2):
                pe_.sem_inc(p_xa, 1)
            with pe_.Fori(0, NG // 2) as i:
                for s in range(2):
                    pe_.wait_ge(p_yg, i * 2 + (s + 1))
                    for q in range(GT):
                        for b in range(NB):
                            last = mm(bank[s][:, q * P:(q + 1) * P], ygs[:, s, b, q * P:(q + 1) * P], wout_s[:, b, :],
                                      start=(b == 0), stop=(b == NB - 1))
                    last.then_inc(p_out_ps, 1)

            pe_.sem_inc(d_x, 1)

            def dense(g, more):
                pe_.wait_ge(d_turn.xT, g + 1)
                for c in range(FFC):
                    mm(bank[2 + c], wff1_s[:, c * P:(c + 1) * P], xsT[:, 0], start=True,
                       stop=True).then_inc(d_h_ps, 1)
                if more:
                    turned_group(d_turn, g + 1)
                pe_.wait_ge(d_h, g * FFC + FFC)
                pe_.wait_ge(d_x, g + 1)
                for q in range(GT):
                    mm(bank[1][:, q * P:(q + 1) * P], ones_row[0:1, :], bff2_s[0:1, :], start=True, stop=False)
                    for c in range(FFC):
                        last = mm(bank[1][:, q * P:(q + 1) * P], hT[:, c, q * P:(q + 1) * P], wff2_s[:, c, :],
                                  start=False, stop=(c == FFC - 1))
                last.then_inc(d_y_ps, 1)

            turned_group(d_turn, 0)
            with pe_.Fori(0, NG - 1) as g:
                dense(g, True)
            dense(NG - 1, False)
            route_ffn(ffn[1], 1)


_INS = ["L0_attn_a_input_data", "L0_attn_a_qk", "L0_attn_a_ov", "L0_attn_b_ln1_g", "L0_attn_b_ln1_b",
        "L0_attn_b_w_in", "L0_attn_b_w_conv", "L0_attn_b_b_conv", "L0_attn_b_w_xproj", "L0_attn_b_w_dt",
        "L0_attn_b_b_dt", "L0_attn_b_A_log", "L0_attn_b_Dp", "L0_attn_b_w_out", "L0_attn_b_ln2_g",
        "L0_attn_b_ln2_b", "L0_attn_b_w_ff1", "L0_attn_b_b_ff1", "L0_attn_b_w_ff2", "L0_attn_b_b_ff2",
        "L0_ffn_Wg", "L0_ffn_W1", "L0_ffn_W2"]


def kernel(**inputs):
    import numpy as _np
    import concourse.bacc as _bacc
    from concourse import mybir as _mybir
    from concourse.bass_utils import run_bass_kernel_spmd as _run

    nc = _bacc.Bacc("TRN2", target_bir_lowering=False, num_devices=1)
    arrays, args = {}, []
    for name in _INS:
        a = _np.ascontiguousarray(inputs[name])
        arrays[f"in_{name}"] = a
        args.append(nc.dram_tensor(f"in_{name}", a.shape, _mybir.dt.from_np(a.dtype), kind="ExternalInput").ap())
    shape = inputs["L0_attn_a_input_data"].shape
    tokens, experts = shape[0] * shape[1], inputs["L0_ffn_Wg"].shape[1]
    rows = (tokens + experts * (P - 1)) // P * P
    args.append(nc.dram_tensor("out_0", shape, _mybir.dt.float32, kind="ExternalOutput").ap())
    for name in ("routed_in", "routed_out"):
        args.append(nc.dram_tensor(name, (rows, shape[2]), _mybir.dt.float32, kind="Internal").ap())
    hybrid_kernel(nc, *args)
    r = _run(nc, [arrays], core_ids=[0])
    return r.results[0]["out_0"]
```

```python
from contextlib import ExitStack

import concourse.bass as bass
from concourse import mybir

P = 128
ALU = mybir.AluOpType
ACT = mybir.ActivationFunctionType
AX = mybir.AxisListType.X
F32 = mybir.dt.float32
BF16 = mybir.dt.bfloat16
I32 = mybir.dt.int32
EPS = 1e-5
MASKED = -1e30
DIGITS = 15


class Chain:

    def __init__(self, eng, sem):
        self.eng, self.sem = eng, sem
        self.base, self.i, self.per, self.trips, self.k = 0, None, 0, 0, 0

    def loop(self, i, per, trips):
        self.base += self.k
        self.i, self.per, self.trips, self.k = i, per, trips, 0

    def end(self):
        assert self.k == self.per, (self.k, self.per)
        self.base += self.per * self.trips
        self.i, self.k = None, 0

    def step(self, ins):
        ins.then_inc(self.sem, 1)
        self.k += 1

    def wait(self):
        at = self.base + self.k
        self.eng.wait_ge(self.sem, at if self.i is None else self.i * self.per + at)

    def link(self, ins):
        self.step(ins)
        self.wait()


def hybrid_kernel(nc, x_in, qk, ov, ln1_g, ln1_b, w_in, w_conv, b_conv, w_xproj, w_dt, b_dt, A_log, Dp, w_out,
                  ln2_g, ln2_b, w_ff1, b_ff1, w_ff2, b_ff2, Wg, W1, W2, out, normed_rows, routed_out):
    B, S, D = x_in.shape
    T = B * S
    NT = T // P
    E = Wg.shape[1]
    F = W1.shape[2]
    FC = F // P
    CAP = max(1, T // E)
    RT = (T + E * (P - 1)) // P
    DI, TAPS = w_conv.shape
    NB = DI // P
    N = A_log.shape[1]
    R = w_dt.shape[0]
    FF = w_ff1.shape[1]
    FFC = FF // P
    G = 512
    NG = T // G
    GT = G // P
    GB = G // S
    PAD = TAPS - 1
    SP_ = S + PAD
    BC3 = 3 * 2 * N
    assert NT * E == 256 and RT % 6 == 3 and BC3 == 96 and S == 2 * P

    with ExitStack() as ctx:
        def sb(name, shape, dt=F32):
            return ctx.enter_context(nc.sbuf_tensor(name, shape, dt))

        def sem(name):
            return ctx.enter_context(nc.semaphore(name))

        bank = [ctx.enter_context(nc.psum_tensor(f"bank{k}", [P, 512], F32)) for k in range(4)]
        decay_ps = ctx.enter_context(nc.psum_tensor("decay_ps", [P, 2, NB, G], F32))
        bank += [decay_ps[:, s, b, :] for s in range(2) for b in range(NB)]
        bank = [b[:, :] for b in bank]

        X = sb("X", [P, NT, D])

        r_delta = sb("r_delta", [P, NB, T])
        r_du = sb("r_du", [P, NB, T])
        r_xm = sb("r_xm", [P, NB, T])
        r_zs = sb("r_zs", [P, NB, T])
        delta, du, xm, zs = r_delta, r_du, r_xm, r_zs
        W1s = r_du[:, 0, 0:E * F].rearrange("p (e f) -> p e f", e=E)
        W2s = r_du[:, 0, E * F:2 * E * F].rearrange("p (e c d) -> p e c d", e=E, c=FC)
        taps = r_du[:, 0, 0:TAPS * G].rearrange("p (k t) -> p k t", k=TAPS)
        conv_sum = r_du[:, 0, TAPS * G:(TAPS + 1) * G]
        XN = r_zs[:, 0, :].rearrange("p (j d) -> p j d", j=NT)
        hot_place = r_zs[:, 0, 0:NT * P // 2].bitcast(BF16).rearrange("p (j s) -> p j s", j=NT)
        hot_tile = r_zs[:, 0, NT * P // 2:(P + RT) * NT // 2].bitcast(BF16).rearrange("p (j k) -> p j k", j=NT)
        tile_ids = r_zs[:, 0, (P + RT) * NT // 2:(P + 3 * RT) * NT // 2].bitcast(BF16).rearrange(
            "p (j c k) -> p j c k", j=NT, c=2)
        Y = r_zs[:, 1, :].rearrange("p (j d) -> p j d", j=NT)
        XA = r_delta[:, 0, :].rearrange("p (j d) -> p j d", j=NT)

        early = r_delta[:, 1, :]
        mask, qk_s, ov_s = early[:, 0:S], early[:, S:S + D], early[:, S + D:S + 2 * D]
        wconv_row = early[0:1, 512:512 + TAPS * DI].rearrange("p (k c) -> p k c", k=TAPS)
        kcmp = early[:, 1536:1536 + RT * E].rearrange("p (k e) -> p k e", e=E)
        ktab = early[:, 1856:1856 + RT]
        e8 = early[:, 1984:2048].rearrange("p (k e) -> p k e", e=E)

        work = sb("work", [P, max(6144, 2048 + B * SP_)])

        def carve(at, *shape):
            n = 1
            for k in shape:
                n *= k
            names = " ".join("abcd"[:len(shape)])
            v = work[:, at:at + n]
            if len(shape) > 1:
                v = v.rearrange(f"p ({names}) -> p {names}", **dict(zip("abcd", shape)))
            return v

        xn_a = carve(0, 2, 2, P)
        xT_a = carve(512, 2, S)
        uv_a = carve(1024, 2, 512)
        sc_a = carve(2048, 2, 384)
        pr_a = carve(2816, 2, 384)
        pT_a = carve(3584, 2, 384)
        xs = carve(0, 2, GT, P)
        xsT = carve(1024, 2, G)
        pe = carve(2048, E, NT)
        prob = carve(2304, E, NT)
        fA = carve(2560, E, NT)
        fB = carve(2816, E, NT)
        fC = carve(3072, E, NT)
        incl = carve(3328, E, NT)
        sel = carve(3584, E, NT)
        tl = carve(3840, NT)
        probT = carve(4096, 2, P)
        thr_row = carve(4352, P)
        reached = carve(4480, 3, 2, P)
        xin = carve(4096, 2, 3, P)
        rxT = carve(4864, 3, P)
        place = carve(3872, NT).bitcast(I32)
        tile_no = carve(3904, NT).bitcast(I32)
        tile_f = carve(3936, NT)
        place_b = carve(3968, NT // 2).bitcast(BF16)
        W1x = carve(0, 3, F)
        rhT = carve(768, 3, F)
        ry = carve(1536, 3, P)
        dtT = carve(0, 2, G)
        bcr = carve(1024, 1, G)
        bc_hi = carve(1536, G // 2).bitcast(BF16)[R:R + 2 * N]
        bc_lo = carve(1792, G // 2).bitcast(BF16)[R:R + 2 * N]
        pos_part = [carve(4096, NB, G), carve(2048, NB, G)]
        ln_part = [carve(5120, NB, G), carve(3072, NB, G)]
        xaT = carve(2048, B, SP_)
        h = carve(0, 4, NB, G)
        dBu1 = carve(4096, NB, G)
        C_bc = carve(5120, 2, G)
        hT = carve(2048, FFC, G)
        ygs = carve(2048, 2, NB, G)

        ident = sb("ident", [P, P])
        ones_b = sb("ones_b", [P, P], BF16)
        not_before_b = sb("not_before_b", [P, P], BF16)
        flag_b = sb("flag_b", [P, E, NT], BF16)
        cnt_b = sb("cnt_b", [P, E], BF16)
        resets = sb("resets", [P, E, NT])
        em8 = sb("em8", [P, E, NT])
        kk = sb("kk", [P, RT, E])
        source = sb("source", [P, RT], I32)
        places = sb("places", [P, P], BF16)
        tiles_j = sb("tiles_j", [P, NT], BF16)
        rows_p = sb("rows_p", [P, 1])
        etab = sb("etab", [P, RT // 3], I32)
        same_expert = sb("same_expert", [P, P], BF16)
        digits = sb("digits", [P, 3], I32)
        least_bits = sb("least_bits", [P, 1], I32)
        cand = sb("cand", [P, 3], I32)
        n_reached = sb("n_reached", [P, 3], BF16)
        enough = sb("enough", [P, 3])
        digit = sb("digit", [P, 1], I32)
        e8i = sb("e8i", [P, E], I32)
        gate = sb("gate", [P, NT])
        pos = sb("pos", [P, NT], I32)
        one_c = sb("one_c", [P, 1])
        stats = sb("stats", [P, NT, 6])
        mean2 = sb("mean2", [P, NT])
        var4 = sb("var4", [P, NT])
        vv = sb("vv", [P, 2, NT])
        t32 = sb("t32", [P, 2, NT])
        factor = sb("factor", [P, 2, NT])
        offset = sb("offset", [P, 2, NT])
        rs, nmr, rs2, nmr2 = factor[:, 0], offset[:, 0], factor[:, 1], offset[:, 1]
        nmax = sb("nmax", [P, 2, 2])
        psum_e = sb("psum_e", [P, 2, 2])
        rinv = sb("rinv", [P, 2, 2])

        Wg_s = sb("Wg_s", [P, E])
        g1, b1 = sb("g1", [P, 1]), sb("b1", [P, 1])
        g2, b2 = sb("g2", [P, 1]), sb("b2", [P, 1])
        win_s = sb("win_s", [P, 2 * DI])
        wfold = sb("wfold", [P, TAPS, DI])
        dBu = [wfold[:, :, :].rearrange("p k c -> p (k c)").rearrange("p (b t) -> p b t", b=NB), dBu1]
        bconv_s = sb("bconv_s", [P, NB])
        wconv_s = sb("wconv_s", [P, TAPS])
        wx_s = sb("wx_s", [P, NB, R + 2 * N])
        wdt_s = sb("wdt_s", [R, DI])
        bdt_s = sb("bdt_s", [P, NB])
        Aneg = sb("Aneg", [P, NB, N])
        Dp_s = sb("Dp_s", [P, NB])
        diagD = sb("diagD", [P, NB, P])
        wout_s = sb("wout_s", [P, NB, D])
        wff1_s = sb("wff1_s", [P, FF])
        bff1_s = sb("bff1_s", [P, FFC])
        wff2_s = sb("wff2_s", [P, FFC, D])
        bff2_s = sb("bff2_s", [P, D])
        ones_row = sb("ones_row", [1, P])
        pick = sb("pick", [BC3, 2 * N, P], BF16)
        bc_parts = sb("bc_parts", [BC3, T], BF16)

        s_first_const = sem("s_first_const")
        s_const = sem("s_const")
        s_passed = sem("s_passed")
        s_x = [sem(f"s_x{q}") for q in range(4)]
        s_attn_w = sem("s_attn_w")
        s_weights = sem("s_weights")
        s_experts = [sem(f"s_experts{n}") for n in range(2)]
        v_chain, a_chain, g_chain = sem("v_chain"), sem("a_chain"), sem("g_chain")
        a_xn = sem("a_xn")
        a_xT_ps = sem("a_xT_ps")
        a_xT = sem("a_xT")
        a_uv_ps = sem("a_uv_ps")
        a_uv = sem("a_uv")
        a_sc_ps = sem("a_sc_ps")
        a_max = sem("a_max")
        a_exp = sem("a_exp")
        a_pT_ps = sem("a_pT_ps")
        a_pT = sem("a_pT")
        a_out_ps = sem("a_out_ps")
        a_fin = sem("a_fin")
        s_prepared = sem("s_prepared")
        s_conv_ps = sem("s_conv_ps")

        class Turn:
            def __init__(self, tag):
                self.xs = sem(f"{tag}_xs")
                self.ps = sem(f"{tag}_ps")
                self.xT = sem(f"{tag}_xT")

        class Ffn:
            def __init__(self, l):
                self.ahead = (2, 1)[l]
                self.turn = Turn(f"f{l}")
                self.copied = sem(f"f{l}_copied")
                self.logits = sem(f"f{l}_logits")
                self.shifted = sem(f"f{l}_shifted")
                self.exps = sem(f"f{l}_exps")
                self.to_turn = sem(f"f{l}_to_turn")
                self.turned = sem(f"f{l}_turned")
                self.flags = sem(f"f{l}_flags")
                self.counts = sem(f"f{l}_counts")
                self.routed = sem(f"f{l}_routed")
                self.kept = sem(f"f{l}_kept")
                self.hot_tile = sem(f"f{l}_hot_tile")
                self.tile_ids = sem(f"f{l}_tile_ids")
                self.hot_place = sem(f"f{l}_hot_place")
                self.source_ps = sem(f"f{l}_source_ps")
                self.source = sem(f"f{l}_source")
                self.loaded = [sem(f"f{l}_loaded{u}") for u in range(2)]
                self.x_ps = sem(f"f{l}_x_ps")
                self.x = sem(f"f{l}_x")
                self.h_ps = sem(f"f{l}_h_ps")
                self.h = sem(f"f{l}_h")
                self.y_ps = sem(f"f{l}_y_ps")
                self.y = sem(f"f{l}_y")
                self.stored = sem(f"f{l}_stored")
                self.gathered = [sem(f"f{l}_gathered{g}") for g in range(NG)]
                self.added = sem(f"f{l}_added")

        ffn = [Ffn(0), Ffn(1)]
        m_turn = Turn("m")
        m_xc_ps = sem("m_xc_ps")
        m_x1_ps = sem("m_x1_ps")
        m_taps = sem("m_taps")
        m_conv = sem("m_conv")
        m_x1 = sem("m_x1")
        m_xc = sem("m_xc")
        m_z_ps = sem("m_z_ps")
        m_z = sem("m_z")
        m_dt_ps = sem("m_dt_ps")
        m_dt = sem("m_dt")
        m_bc_read = sem("m_bc_read")
        m_bc = sem("m_bc")
        m_raw_ps = sem("m_raw_ps")
        m_raw = sem("m_raw")
        m_soft = sem("m_soft")
        m_delta = sem("m_delta")
        m_du = sem("m_du")
        c_B = sem("c_B")
        c_C = sem("c_C")
        c_dBu = sem("c_dBu")
        c_decay = sem("c_decay")
        c_h = sem("c_h")
        c_C_sb = sem("c_C_sb")
        c_hC = sem("c_hC")
        c_y = sem("c_y")
        c_gated = sem("c_gated")
        p_yg = sem("p_yg")
        p_xl = sem("p_xl")
        p_out_ps = sem("p_out_ps")
        p_xa = sem("p_xa")
        d_turn = Turn("d")
        d_h_ps = sem("d_h_ps")
        d_h = sem("d_h")
        d_y_ps = sem("d_y_ps")
        d_xa = sem("d_xa")
        d_x = sem("d_x")
        s_out = sem("s_out")

        x_tiles = x_in.rearrange("b (h p) d -> p (b h) d", p=P)
        out_tiles = out.rearrange("b (h p) d -> p (b h) d", p=P)

        def col(v, axis=1):
            return v.unsqueeze(axis)

        def over_tiles(v):
            return col(v, 2).broadcast_to([P, E, NT])

        def over_experts(v):
            return col(v, 1).broadcast_to([P, E, NT])

        def by_tile(v):
            return v.rearrange("p e j -> p j e")

        def tokens_of(g, n):
            return bass.ds(g * G + n // N * G, G)

        def rows(routed, i):
            return routed[bass.ds(i * (3 * P), 3 * P), :].rearrange("(k p) d -> p k d", p=P)

        def apart(eng, semaphore, value):
            eng.wait_ge(semaphore, value)
            eng.sem_inc(s_passed, 1)

        block = ctx.enter_context(nc.Block())

        N_WEIGHTS = 20
        FIRST = 1
        ATT_LOOP = (B - 4) // 2

        @block.sync
        def _(sp):
            for q in range(4):
                a, b = q * NT // 4, (q + 1) * NT // 4
                sp.dma_start(X[:, a:b, :], x_tiles[:, a:b, :]).then_inc(s_x[q], 16)
            sp.dma_start(qk_s[:, :], qk).then_inc(s_attn_w, 16)
            sp.dma_start(ov_s[:, :], ov).then_inc(s_attn_w, 16)

            def experts(n):
                sp.dma_start(W1s, W1.rearrange("e d f -> d e f")).then_inc(s_experts[n], 16)
                for c in range(FC):
                    sp.dma_start(W2s[:, :, c, :], W2[:, c * P:(c + 1) * P, :].rearrange("e p d -> p e d")).then_inc(
                        s_experts[n], 16)

            experts(0)

            def ld(dst, src):
                sp.dma_start(dst, src).then_inc(s_weights, 16)

            with nc.allow_non_contiguous_dma(reason="small weights"):
                ld(Wg_s[:, :], Wg)
                for v, w in ((g1, ln1_g), (b1, ln1_b), (g2, ln2_g), (b2, ln2_b)):
                    ld(v[:, :], w.rearrange("(p a) -> p a", a=1))
                ld(win_s[:, :], w_in)
                ld(wconv_row[0:1, :, :], w_conv.rearrange("(a c) k -> a k c", a=1))
                ld(wconv_s[:, :], w_conv[P:2 * P, :])
                ld(bconv_s[:, :], b_conv.rearrange("(b p) -> p b", p=P))
                ld(wx_s[:, :, :], w_xproj.rearrange("(b p) r -> p b r", p=P))
                ld(wdt_s[:, :], w_dt)
                ld(bdt_s[:, :], b_dt.rearrange("(b p) -> p b", p=P))
                ld(Aneg[:, :, :], A_log.rearrange("(b p) n -> p b n", p=P))
                ld(Dp_s[:, :], Dp.rearrange("(b p) -> p b", p=P))
                ld(wout_s[:, :, :], w_out.rearrange("(b p) d -> p b d", p=P))
                ld(wff1_s[:, :], w_ff1)
                ld(bff1_s[:, :], b_ff1.rearrange("(c p) -> p c", p=P))
                ld(wff2_s[:, :, :], w_ff2.rearrange("(c p) d -> p c d", p=P))
                ld(bff2_s[:, :], b_ff2.rearrange("(a d) -> a d", a=1).broadcast_to([P, D]))

            def keep_normed(f):
                sp.wait_ge(f.copied, NG + f.ahead)
                sp.dma_start(normed_rows.rearrange("(j p) d -> p j d", p=P), XN).then_inc(f.kept, 16)

            def routed_tiles(f):
                def store(i):
                    sp.wait_ge(f.y, i + 2)
                    sp.dma_start(rows(routed_out, i), ry).then_inc(f.stored, 16)

                sp.sem_inc(f.stored, 16)
                with sp.Fori(0, RT // 3) as i:
                    store(i)

            keep_normed(ffn[0])
            routed_tiles(ffn[0])
            sp.wait_ge(c_gated, NG + 1)
            experts(1)
            keep_normed(ffn[1])
            routed_tiles(ffn[1])
            for g in range(NG):
                a, b = g * GT, (g + 1) * GT
                sp.wait_ge(ffn[1].added, g + 1)
                sp.dma_start(out_tiles[:, a:b, :], X[:, a:b, :]).then_inc(s_out, 16)
            sp.wait_ge(s_out, 16 * NG)

        @block.gpsimd
        def _(pool):
            ch = Chain(pool, g_chain)
            ch.step(pool.memset(ident[:, :], 0.0))
            ch.link(pool.memset(mask[:, :], 0.0))
            ch.step(pool.affine_select(out=ident[:, :], in_=ident[:, :], compare_op=ALU.not_equal, fill=1.0, base=0,
                                       pattern=[[-1, P]], channel_multiplier=1))
            ch.link(pool.affine_select(out=mask[:, P:S], in_=mask[:, P:S], compare_op=ALU.is_ge, fill=MASKED, base=0,
                                       pattern=[[-1, P]], channel_multiplier=1))
            pool.sem_inc(s_first_const, 1)
            ch.step(pool.memset(not_before_b[:, :], -1.0))
            ch.step(pool.memset(resets[:, :, :], 1.0))
            ch.step(pool.memset(pick[:, :, :], 0.0))
            ch.step(pool.memset(ones_b[:, :], 1.0))
            ch.step(pool.memset(ones_row[:, :], 1.0))
            ch.step(pool.memset(one_c[:, :], 1.0))
            ch.step(pool.iota(em8[:, :, :], [[1, E], [0, NT]], base=-E, channel_multiplier=0,
                              allow_small_or_imprecise_dtypes=True))
            ch.step(pool.iota(places[:, :], [[1, P]], base=0, channel_multiplier=0,
                              allow_small_or_imprecise_dtypes=True))
            ch.step(pool.iota(tiles_j[:, :], [[1, NT]], base=0, channel_multiplier=0,
                              allow_small_or_imprecise_dtypes=True))
            ch.step(pool.iota(rows_p[:, :], [[0, 1]], base=0, channel_multiplier=1,
                              allow_small_or_imprecise_dtypes=True))
            ch.step(pool.memset(same_expert[:, :], 1.0))
            ch.step(pool.iota(digits[:, :], [[1, 3]], base=1, channel_multiplier=0))
            ch.link(pool.iota(kk[:, :, :], [[1, RT], [0, E]], base=0, channel_multiplier=0,
                              allow_small_or_imprecise_dtypes=True))
            ch.step(pool.affine_select(out=not_before_b[:, :], in_=not_before_b[:, :], compare_op=ALU.is_ge,
                                       fill=0.0, base=0, pattern=[[-1, P]], channel_multiplier=1))
            ch.step(pool.memset(resets[:, :, 0:1], 0.0))
            pairs = NT // 2
            blocks = same_expert[:, :].rearrange("p (e j) -> p e j", j=pairs)
            ch.step(pool.affine_select(out=blocks, in_=blocks, compare_op=ALU.is_ge, fill=0.0, base=0,
                                       pattern=[[-pairs, P // pairs], [0, pairs]], channel_multiplier=1))
            ch.wait()
            ch.step(pool.affine_select(out=blocks, in_=blocks, compare_op=ALU.is_ge, fill=0.0, base=pairs - 1,
                                       pattern=[[pairs, P // pairs], [0, pairs]], channel_multiplier=-1))
            for part in range(3):
                ch.link(pool.affine_select(out=pick[:, :, :], in_=pick[:, :, :], compare_op=ALU.not_equal, fill=1.0,
                                           base=-2 * N * part, pattern=[[-1, 2 * N], [0, P]], channel_multiplier=1))
            pool.sem_inc(s_const, 1)
            pool.sem_inc(c_hC, 2)

            def convolve(g):
                pool.wait_ge(m_taps, g + 3)
                ch.link(pool.tensor_tensor(taps[:, 3], taps[:, 3], taps[:, 0], ALU.add))
                ch.link(pool.tensor_tensor(taps[:, 3], taps[:, 3], taps[:, 1], ALU.add))
                pool.tensor_tensor(conv_sum, taps[:, 3], taps[:, 2], ALU.add).then_inc(m_conv, 1)

            def routed(f, between=None):
                pool.wait_ge(f.hot_tile, 1)
                pool.tensor_tensor(tile_ids[:, :, 1, :], hot_tile, col(tiles_j[:, :], 2).broadcast_to([P, NT, RT]),
                                   ALU.mult).then_inc(f.tile_ids, 1)
                pool.wait_ge(f.source, 1)
                pool.wait_ge(f.kept, 16)
                for i in range(RT // 3):
                    if i > 1:
                        pool.wait_ge(f.x_ps, i - 1)
                    for s in range(3):
                        k = i * 3 + s
                        pool.indirect_dma_start(out=xin[:, i % 2, s, :], out_offset=None, in_=normed_rows,
                                                in_offset=bass.IndirectOffsetOnAxis(ap=source[:, k:k + 1], axis=0),
                                                bounds_check=T - 1).then_inc(f.loaded[i % 2], 16)
                pool.wait_ge(f.stored, 16 * (RT // 3 + 1))
                for j in range(NT):
                    pool.indirect_dma_start(out=Y[:, j, :], out_offset=None, in_=routed_out,
                                            in_offset=bass.IndirectOffsetOnAxis(ap=pos[:, j:j + 1], axis=0),
                                            bounds_check=RT * P - 1).then_inc(f.gathered[j // GT], 16)
                    if between is not None and j % GT == GT - 1 and j // GT >= CONV_LAG:
                        between(j // GT - CONV_LAG)

            CONV_LAG = 4
            routed(ffn[0], convolve)
            with pool.Fori(0, CONV_LAG) as i:
                ch.loop(i, 2, CONV_LAG)
                convolve(i + (NG - CONV_LAG))
            ch.end()

            def softplus(i, s, last):
                at = bass.ds(i * (2 * G) + s * G, G)
                pool.wait_ge(m_soft, i * 2 + (s + 1))
                pool.tensor_tensor(delta[:, :, at], pos_part[s], ln_part[s], ALU.add).then_inc(m_delta, 1)
                if not last:
                    pool.wait_ge(m_delta, i * 2 + (s + 3))
                    pool.tensor_tensor(du[:, :, at], delta[:, :, at], xm[:, :, at], ALU.mult).then_inc(m_du, 1)

            with pool.Fori(0, NG // 2 - 1) as i:
                for s in range(2):
                    softplus(i, s, False)
            for s in range(2):
                softplus(NG // 2 - 1, s, True)

            with pool.Fori(0, NG) as g:
                for n in range(N):
                    s = n % 2
                    pool.wait_ge(c_h, g * N + (n + 3))
                    pool.wait_ge(c_C_sb, g * N + (n + 1))
                    pool.tensor_tensor(h[:, n % 4], h[:, n % 4], col(C_bc[:, s]).broadcast_to([P, NB, G]),
                                       ALU.mult).then_inc(c_hC, 1)

            pool.wait_ge(p_xa, NG + 2)
            with pool.Fori(0, NG) as g:
                xt, xa = X[:, bass.ds(g * GT, GT), :], XA[:, bass.ds(g * GT, GT), :]
                pool.tensor_tensor(xt, xt, xa, ALU.add).then_inc(d_xa, 1)
                apart(pool, d_xa, g * 2 + 1)
                pool.tensor_tensor(xt, xt, col(bff2_s[:, :]).broadcast_to([P, GT, D]), ALU.add).then_inc(d_xa, 1)

            routed(ffn[1])

        @block.scalar
        def _(act):
            ch = Chain(act, a_chain)
            A = nc.scalar.activation
            act.preload_act_table(ACT.Exp)

            def attend(n, c=0):
                s = (n + c) % 2 if isinstance(n, int) else c % 2

                def has(k):
                    return not isinstance(n, int) or 0 <= n + c + k < B

                if has(0):
                    act.wait_ge(a_max, (n * 2) + (2 * c + 2))
                    A(pr_a[:, s, 0:P], sc_a[:, s, 0:P], ACT.Exp, scale=-1.0, bias=nmax[:, s, 0:1],
                      accum_out=psum_e[:, s, 0:1])
                    A(pr_a[:, s, P:P + S], sc_a[:, s, P:P + S], ACT.Exp, scale=-1.0, bias=nmax[:, s, 1:2],
                      accum_out=psum_e[:, s, 1:2]).then_inc(a_exp, 1)
                if has(1):
                    act.wait_ge(a_uv_ps, n + (c + 2))
                    A(uv_a[:, 1 - s, 0:S], bank[3 - s][:, 0:S], ACT.Copy).then_inc(a_uv, 1)
                    A(uv_a[:, 1 - s, S:2 * S], bank[3 - s][:, S:2 * S], ACT.Copy)

            for n in range(-1, FIRST):
                attend(n)
            with act.Fori(0, ATT_LOOP) as i:
                for c in range(2):
                    attend(i * 2, FIRST + c)
            for n in range(FIRST + 2 * ATT_LOOP, B):
                attend(n)

            def normed_tokens(f):
                act.sem_inc(f.copied, 2)
                act.sem_inc(f.logits, 2)
                with act.Fori(0, NG // 2) as i:
                    for s in range(2):
                        apart(act, f.turn.xs, i * 2 + (s + 1))
                        A(XN[:, bass.ds(i * (2 * GT) + s * GT, GT), :], xs[:, s], ACT.Copy).then_inc(f.copied, 1)
                    for s in range(2):
                        act.wait_ge(f.logits, i * 2 + (s + 1))
                        act.wait_ge(f.turn.ps, i * 2 + (s + 3))
                        A(xsT[:, s], bank[s], ACT.Copy).then_inc(f.turn.xT, 1)

            def route_ffn(f):
                act.wait_ge(f.shifted, 1)
                A(pe, pe, ACT.Exp).then_inc(f.exps, 1)
                act.wait_ge(f.hot_tile, 1)
                A(tile_ids[:, :, 0, :], hot_tile, ACT.Copy, scale=rows_p[:, 0:1]).then_inc(f.tile_ids, 1)
                act.preload_act_table(ACT.Gelu)

                def tiles(i):
                    for s in range(3):
                        act.wait_ge(f.h_ps, i * 3 + (s + 1))
                        A(rhT[:, s], bank[s][:, 0:F], ACT.Gelu).then_inc(f.h, 1)

                with act.Fori(0, RT // 3) as i:
                    tiles(i)

            normed_tokens(ffn[0])
            route_ffn(ffn[0])

            act.wait_ge(s_weights, 16 * (N_WEIGHTS - 1))
            ch.link(A(Aneg[:, :, :], Aneg[:, :, :], ACT.Exp))
            ch.link(A(Aneg[:, :, :], Aneg[:, :, :], ACT.Copy, scale=-1.0))
            act.preload_act_table(ACT.Silu)
            act.wait_ge(m_taps, 1)
            act.sem_inc(m_taps, 1)

            def second_block(g):
                apart(act, m_conv, g + 1)
                A(xm[:, 1, bass.ds(g * G, G)], conv_sum, ACT.Silu, bias=bconv_s[:, 1:2]).then_inc(m_x1, 1)

            def inner(g, first=False):
                at = bass.ds(g * G, G)
                if not first:
                    second_block(g - 1)
                act.wait_ge(m_x1_ps, g + 1)
                for k in range(TAPS):
                    late = PAD - k
                    last = A(taps[:, k].rearrange("p (q t) -> p q t", q=GB)[:, :, late:S],
                             bank[3].rearrange("p (q t) -> p q t", q=GB)[:, :, 0:S - late], ACT.Copy,
                             scale=wconv_s[:, k:k + 1])
                last.then_inc(m_taps, 1)
                apart(act, m_xc_ps, g + 1)
                A(xm[:, 0, at], bank[2], ACT.Silu, bias=bconv_s[:, 0:1]).then_inc(m_xc, 1)
                apart(act, m_z_ps, g + 1)
                for b in range(NB):
                    last = A(zs[:, b, at], bank[4 + b], ACT.Silu)
                last.then_inc(m_z, 1)

            inner(0, first=True)
            with act.Fori(1, NG) as g:
                inner(g)
            second_block(NG - 1)
            act.preload_act_table_set("natural_log_exp_and_others")
            act.sem_inc(m_delta, 2)
            with act.Fori(0, NG // 2) as i:
                ch.loop(i, 2 * (NB + 1), NG // 2)
                for s in range(2):
                    apart(act, m_delta, i * 2 + (s + 1))
                    act.wait_ge(m_raw_ps, i * 2 + (s + 1))
                    for b in range(NB):
                        ch.step(A(ln_part[s][:, b], bank[4 + 2 * s + b], ACT.Abs, bias=bdt_s[:, b:b + 1]))
                    for b in range(NB):
                        last = A(pos_part[s][:, b], bank[4 + 2 * s + b], ACT.Relu, bias=bdt_s[:, b:b + 1])
                    last.then_inc(m_raw, 1)
                    ch.wait()
                    ch.link(A(ln_part[s], ln_part[s], ACT.Exp, scale=-1.0))
                    A(ln_part[s], ln_part[s], ACT.Ln, bias=one_c[:, 0:1]).then_inc(m_soft, 1)
            ch.end()

            act.wait_ge(m_delta, NG + 1)
            with act.Fori(0, NG) as g:
                for n in range(N):
                    s = n % 2
                    apart(act, c_h, g * N + (n + 1))
                    for b in range(NB):
                        d = delta[:, b, bass.ds(g * G, G)].rearrange("p (q t) -> p q t", q=GB)[:, :, 1:S]
                        o = decay_ps[:, s, b, :].rearrange("p (q t) -> p q t", q=GB)[:, :, 1:S]
                        last = A(o, d, ACT.Exp, scale=Aneg[:, b, n:n + 1])
                    last.then_inc(c_decay, 1)
                    act.wait_ge(c_C, g * N + (n + 1))
                    act.wait_ge(c_hC, g * N + (n + 1))
                    A(C_bc[:, s], bank[3], ACT.Copy).then_inc(c_C_sb, 1)

            with act.Fori(0, NG // 2) as i:
                for s in range(2):
                    if s == 0:
                        act.wait_ge(c_gated, NG + 1)
                    apart(act, p_xa, i * 2 + (s + 1))
                    A(ygs[:, s], xm[:, :, bass.ds(i * (2 * G) + s * G, G)], ACT.Copy).then_inc(p_yg, 1)
                    for q in range(GT):
                        j = i * (2 * GT) + (s * GT + q)
                        last = A(XA[:, bass.ds(j, 1), :], X[:, bass.ds(j, 1), :], ACT.Identity,
                                 scale=rs[:, bass.ds(j, 1)], bias=nmr[:, bass.ds(j, 1)])
                    last.then_inc(p_xl, 1)
            act.preload_act_table(ACT.Gelu_apprx_tanh)
            f = ffn[1]

            def hidden(g):
                for c in range(FFC):
                    act.wait_ge(d_h_ps, g * FFC + (c + 1))
                    A(hT[:, c], bank[2 + c], ACT.Gelu_apprx_tanh, bias=bff1_s[:, c:c + 1]).then_inc(d_h, 1)

            def normed_group(g):
                apart(act, f.turn.xs, g + 1)
                A(XN[:, bass.ds(g * GT, GT), :], xs[:, 1], ACT.Copy).then_inc(f.copied, 1)
                act.wait_ge(f.logits, g + 1)
                act.wait_ge(f.turn.ps, g + 2)
                A(xsT[:, 1], bank[6], ACT.Copy).then_inc(f.turn.xT, 1)

            act.sem_inc(f.copied, 1)
            act.sem_inc(f.logits, 1)
            hidden(0)
            with act.Fori(0, NG - 1) as g:
                hidden(g + 1)
                normed_group(g)
            normed_group(NG - 1)
            route_ffn(ffn[1])

        @block.vector
        def _(dve):
            V = nc.vector
            ch = Chain(dve, v_chain)
            FACTOR_STEPS = 18

            def norm_factors(at=slice(0, NT), n=NT, twice=False):
                st, k = stats[:, at, :], 2 if twice else 1
                mean, var = mean2[:, at], var4[:, at]
                v, t, r, o = (x[:, 0:k, at] for x in (vv, t32, factor, offset))
                ch.step(V.tensor_tensor(mean, st[:, :, 1], st[:, :, 4], ALU.add))
                ch.step(V.tensor_tensor(var, st[:, :, 1], st[:, :, 4], ALU.subtract))
                ch.link(V.tensor_tensor(t[:, 0], st[:, :, 2], st[:, :, 5], ALU.add))
                ch.link(V.tensor_tensor(var, var, var, ALU.mult))
                ch.link(V.scalar_tensor_tensor(out=var, in0=t[:, 0], scalar=4.0 / D, in1=var, op0=ALU.mult,
                                               op1=ALU.add))
                if twice:
                    ch.step(V.tensor_scalar(v[:, 1], var, 0.25 * (1 + EPS), EPS * EPS, ALU.mult, ALU.add))
                ch.link(V.tensor_scalar(v[:, 0], var, 0.25, EPS, ALU.mult, ALU.add))
                ch.link(V.tensor_scalar(r.bitcast(I32), v.bitcast(I32), 1, None, ALU.logical_shift_right))
                ch.link(V.tensor_scalar(r.bitcast(I32), r.bitcast(I32), -1.0, float(0x5f3759df), ALU.mult, ALU.add))
                for _ in range(3):
                    ch.link(V.scalar_tensor_tensor(out=t, in0=r, scalar=-0.5, in1=r, op0=ALU.mult, op1=ALU.mult))
                    ch.link(V.tensor_tensor(t, t, v, ALU.mult))
                    ch.link(V.scalar_tensor_tensor(out=r, in0=t, scalar=1.5, in1=r, op0=ALU.add, op1=ALU.mult))
                ch.link(V.scalar_tensor_tensor(out=o, in0=col(mean).broadcast_to([P, k, n]), scalar=-0.5,
                                               in1=r, op0=ALU.mult, op1=ALU.mult))

            def one(tile, j):
                return tile[:, bass.ds(j, 1), :].rearrange("p a d -> p (a d)")

            def tile_stats(tile, j):
                return V.bn_stats(one(stats, j), one(tile, j))

            def normed(dst, src, j, r, m):
                return V.tensor_scalar(dst, one(src, j), r[:, bass.ds(j, 1)], m[:, bass.ds(j, 1)], ALU.mult, ALU.add)

            for j in range(NT):
                if j % (NT // 4) == 0:
                    dve.wait_ge(s_x[j * 4 // NT], 16)
                ch.step(tile_stats(X, j))
            ch.wait()
            norm_factors()
            dve.wait_ge(s_first_const, 1)

            def attend(n, c=0):
                s = (n + c) % 2 if isinstance(n, int) else c % 2
                r = 1 - s

                def has(k):
                    return not isinstance(n, int) or 0 <= n + c + k < B

                if has(-1):
                    dve.wait_ge(a_pT_ps, n + c)
                    V.tensor_copy(pT_a[:, r], bank[6 + r][:, 0:384]).then_inc(a_pT, 1)
                if has(0):
                    apart(dve, a_sc_ps, n + (c + 1))
                    V.tensor_tensor_reduce(sc_a[:, s, 0:P], bank[4 + s][:, 0:P], mask[:, P:S], -1.0 / D ** 0.5,
                                           3e38, ALU.add, ALU.min, nmax[:, s, 0:1]).then_inc(a_max, 1)
                    V.tensor_tensor_reduce(sc_a[:, s, P:P + S], bank[4 + s][:, P:P + S], mask[:, :], -1.0 / D ** 0.5,
                                           3e38, ALU.add, ALU.min, nmax[:, s, 1:2]).then_inc(a_max, 1)
                if has(2):
                    dve.wait_ge(a_xT_ps, n + (c + 3))
                    V.tensor_copy(xT_a[:, s], bank[s][:, 0:S]).then_inc(a_xT, 1)
                if has(3):
                    for k in range(2):
                        last = normed(xn_a[:, r, k, :], X, n * 2 + (2 * (c + 3) + k), rs, nmr)
                    last.then_inc(a_xn, 1)
                if has(-1):
                    dve.wait_ge(a_exp, n + c)
                    ch.link(V.reciprocal(rinv[:, r], psum_e[:, r]))
                    dve.wait_ge(a_out_ps, n + c)
                    for k in range(2):
                        xt = one(X, n * 2 + (2 * (c - 1) + k))
                        last = V.scalar_tensor_tensor(out=xt, in0=bank[4 + r][:, k * P:(k + 1) * P],
                                                      scalar=rinv[:, r, k:k + 1], in1=xt, op0=ALU.mult, op1=ALU.add)
                        if k == 0:
                            ch.step(last)
                    last.then_inc(a_fin, 1)
                    apart(dve, a_fin, n + (c + 2))
                    for k in range(2):
                        ch.step(tile_stats(X, n * 2 + (2 * (c - 1) + k)))

            for n in range(-3, FIRST):
                attend(n)
            with dve.Fori(0, ATT_LOOP) as i:
                ch.loop(i, 2 * 4, ATT_LOOP)
                for c in range(2):
                    attend(i * 2, FIRST + c)
            ch.end()
            for n in range(FIRST + 2 * ATT_LOOP, B + 1):
                attend(n)
            ch.wait()
            dve.wait_ge(s_const, 1)

            def normed_tokens(f):
                norm_factors()
                with dve.Fori(0, NG // 2) as i:
                    for s in range(2):
                        dve.wait_ge(f.copied, i * 2 + (s + 1))
                        apart(dve, f.turn.ps, i * 2 + (s + 1))
                        for q in range(GT):
                            last = normed(xs[:, s, q, :], X, i * (2 * GT) + (s * GT + q), rs, nmr)
                        last.then_inc(f.turn.xs, 1)

            def route_ffn(f, n):
                logits = bank[7][:, 0:E * NT].rearrange("p (e j) -> p e j", e=E)
                dve.wait_ge(f.logits, NG + f.ahead)
                ch.link(V.tensor_reduce(tl, by_tile(logits), AX, ALU.max))
                V.tensor_tensor(pe, logits, over_experts(tl), ALU.subtract).then_inc(f.shifted, 1)
                dve.wait_ge(f.exps, 1)
                ch.link(V.tensor_reduce(tl, by_tile(pe), AX, ALU.add))
                ch.link(V.reciprocal(tl, tl))
                V.tensor_tensor(prob, pe, over_experts(tl), ALU.mult).then_inc(f.to_turn, 1)
                ch.step(V.tensor_scalar(cand[:, :], digits[:, :], 2 * (DIGITS - 1), None, ALU.logical_shift_left))
                ch.step(V.memset(least_bits[:, :], 0))
                dve.wait_ge(f.turned, 1)
                ch.link(V.tensor_copy(probT, bank[4][:, 0:2 * P].rearrange("p (h t) -> p h t", h=2)))
                for k in range(DIGITS):
                    shift = 2 * (DIGITS - 1 - k)
                    with nc.allow_low_precision(reason="counts up to 256 are exact"):
                        for c in range(3):
                            last = V.tensor_scalar(reached[:, c], probT, cand[:, c:c + 1].bitcast(F32), 0.0,
                                                   ALU.is_ge, ALU.add, accum_out=n_reached[:, c:c + 1])
                        last.then_inc(f.flags, 1)
                        dve.wait_ge(f.counts, k + 1)
                        ch.link(V.tensor_scalar(enough[:, :], bank[3][:, 0:3], CAP - 0.5, None, ALU.is_ge))
                        ch.link(V.tensor_reduce(digit[:, :], enough[:, :], AX, ALU.add))
                    ch.link(V.scalar_tensor_tensor(out=least_bits[:, :], in0=digit[:, :], scalar=shift,
                                                   in1=least_bits[:, :], op0=ALU.logical_shift_left,
                                                   op1=ALU.bitwise_or))
                    if shift:
                        ch.link(V.scalar_tensor_tensor(out=cand[:, :], in0=digits[:, :], scalar=shift - 2,
                                                       in1=least_bits[:, :].broadcast_to([P, 3]),
                                                       op0=ALU.logical_shift_left, op1=ALU.bitwise_or))
                V.tensor_copy(thr_row, least_bits[:, :].bitcast(F32).broadcast_to([P, P])).then_inc(f.to_turn, 1)
                dve.wait_ge(f.turned, 2)
                thr = over_tiles(bank[4][:, 0:P].rearrange("p (e j) -> p e j", e=E)[:, :, 0])
                above, need = fA, e8[:, 0]
                ch.link(V.tensor_tensor(above, prob, thr, ALU.is_gt))
                with nc.allow_low_precision(reason="counts up to 32 are exact"):
                    V.tensor_reduce(cnt_b[:, :], above, AX, ALU.add).then_inc(f.flags, 1)
                least = flag_b[:, :, :]
                V.tensor_tensor(least, prob, thr, ALU.is_equal).then_inc(f.flags, 1)
                dve.wait_ge(f.counts, DIGITS + 1)
                ch.link(V.tensor_scalar(need, bank[3][:, 0:E], -1.0, float(CAP), ALU.mult, ALU.add))

                def before(n, dst):
                    within = bank[0][:, 0:E * NT].rearrange("p (e j) -> p e j", e=E)
                    totals = bank[1][:, 0:E * NT]
                    dve.wait_ge(f.counts, n)
                    flat = incl.rearrange("p e j -> p (e j)")
                    ch.link(V.tensor_tensor_scan(flat, resets[:, :, :].rearrange("p e j -> p (e j)"), totals, 0.0,
                                                 ALU.mult, ALU.add))
                    ch.link(V.tensor_tensor(dst, incl, within, ALU.add))

                before(DIGITS + 2, fC)
                ch.link(V.tensor_tensor(fC, fC, over_tiles(need), ALU.is_lt))
                ch.link(V.tensor_tensor(fC, fC, least, ALU.mult))
                ch.link(V.tensor_tensor(sel, fC, above, ALU.add))
                ch.link(V.tensor_reduce(tl, by_tile(sel), AX, ALU.max))
                ch.link(V.tensor_scalar(tl, tl, -3.0, 2.0, ALU.mult, ALU.add))
                ch.link(V.scalar_tensor_tensor(out=sel, in0=sel, scalar=3.0, in1=over_experts(tl), op0=ALU.mult,
                                               op1=ALU.add))
                ch.link(V.tensor_tensor(fA, prob, sel, ALU.min))
                ch.link(V.tensor_reduce(gate[:, :], by_tile(fA), AX, ALU.max))
                ch.link(V.tensor_tensor(fB, fA, over_experts(gate[:, :]), ALU.is_equal))
                ch.link(V.tensor_tensor(fB, fB, em8[:, :, :], ALU.mult))
                ch.link(V.tensor_reduce(tl, by_tile(fB), AX, ALU.min))
                mine = flag_b[:, :, :]
                V.tensor_tensor(mine, em8[:, :, :], over_experts(tl), ALU.is_equal).then_inc(f.flags, 1)
                before(DIGITS + 3, fC)
                ch.link(V.tensor_scalar(e8i[:, :], incl[:, :, NT - 1], float(P - 1), None, ALU.add))
                ch.link(V.tensor_scalar(e8i[:, :], e8i[:, :], P.bit_length() - 1, None, ALU.logical_shift_right))
                ch.step(V.memset(e8[:, 2], 1.0))
                ch.link(V.tensor_copy(e8[:, 1], e8i[:, :]))
                ch.link(V.tensor_tensor_scan(e8[:, 3], e8[:, 2], e8[:, 1], 0.0, ALU.mult, ALU.add))
                ch.link(V.tensor_tensor(e8[:, 4], e8[:, 3], e8[:, 1], ALU.subtract))
                ch.link(V.tensor_scalar(e8[:, 5], e8[:, 4], float(P), None, ALU.mult))
                ch.link(V.tensor_tensor(fC, fC, over_tiles(e8[:, 5]), ALU.add))
                ch.link(V.tensor_tensor(fC, fC, mine, ALU.mult))
                with nc.allow_low_precision(reason="whole numbers"):
                    V.tensor_reduce(pos[:, :], by_tile(fC), AX, ALU.add).then_inc(f.routed, 1)
                dve.wait_ge(f.routed, 1)
                ch.step(V.tensor_scalar(place, pos[:, :], P - 1, None, ALU.bitwise_and))
                ch.link(V.tensor_scalar(tile_no, pos[:, :], P.bit_length() - 1, None, ALU.logical_shift_right))
                ch.step(V.tensor_copy(place_b, place))
                ch.link(V.tensor_copy(tile_f, tile_no))
                dve.wait_ge(f.kept, 16)
                V.tensor_tensor(hot_tile, col(kk[:, :, 0]).broadcast_to([P, NT, RT]),
                                col(tile_f, 2).broadcast_to([P, NT, RT]), ALU.is_equal).then_inc(f.hot_tile, 1)
                for q in range(4):
                    at = slice(q * NT // 4, (q + 1) * NT // 4)
                    V.tensor_tensor(hot_place[:, at], col(places[:, :]).broadcast_to([P, NT // 4, P]),
                                    col(place_b[:, at], 2).broadcast_to([P, NT // 4, P]),
                                    ALU.is_equal).then_inc(f.hot_place, 1)
                dve.wait_ge(f.source_ps, 1)
                ch.link(V.tensor_scalar(ktab[:, :], bank[2][:, RT:2 * RT], float(P), None, ALU.mult))
                V.tensor_tensor(source[:, :], ktab[:, :], bank[2][:, 0:RT], ALU.add).then_inc(f.source, 1)
                ch.link(V.tensor_tensor(kcmp[:, :, :], col(e8[:, 3]).broadcast_to([P, RT, E]), kk[:, :, :], ALU.is_le))
                ch.link(V.tensor_reduce(ktab[:, :], kcmp[:, :, :], AX, ALU.add))
                ch.link(V.tensor_scalar(ktab[:, :], ktab[:, :], float(E - 1), None, ALU.min))
                three = ktab[:, :].rearrange("p (i s) -> p i s", s=3)
                ch.link(V.scalar_tensor_tensor(out=three[:, :, 1], in0=three[:, :, 2], scalar=float(E),
                                               in1=three[:, :, 1], op0=ALU.mult, op1=ALU.add))
                V.scalar_tensor_tensor(out=etab[:, :], in0=three[:, :, 1], scalar=float(E), in1=three[:, :, 0],
                                       op0=ALU.mult, op1=ALU.add).then_inc(f.routed, 1)

                def turned_tiles(i):
                    three = dve.value_load(etab[0:1, bass.ds(i, 1)], min_val=0, max_val=E ** 3 - 1)
                    who = [three % E, three // E % E, three // (E * E)]
                    dve.wait_ge(f.x_ps, i + 1)
                    V.tensor_copy(rxT, bank[6][:, 0:3 * P].rearrange("p (s t) -> p s t", s=3))
                    for s in range(3):
                        last = V.tensor_copy(W1x[:, s:s + 1], W1s[:, bass.ds(who[s], 1), :])
                    last.then_inc(f.x, 1)

                def tiles(i, more):
                    if more:
                        turned_tiles(i + 1)
                    dve.wait_ge(f.stored, i * 16 + 16)
                    dve.wait_ge(f.y_ps, i + 1)
                    V.tensor_copy(ry, bank[7][:, 0:3 * P].rearrange("p (s d) -> p s d", s=3)).then_inc(f.y, 1)

                dve.wait_ge(f.routed, 2)
                dve.wait_ge(s_experts[n], 16 * (1 + FC))
                turned_tiles(0)
                with dve.Fori(0, RT // 3 - 1) as i:
                    tiles(i, True)
                tiles(RT // 3 - 1, False)

            def gathered_group(f, g):
                dve.wait_ge(f.gathered[g], 16 * GT)
                for j in range(g * GT, (g + 1) * GT):
                    ch.step(V.scalar_tensor_tensor(out=X[:, j, :], in0=Y[:, j, :], scalar=gate[:, j:j + 1],
                                                   in1=X[:, j, :], op0=ALU.mult, op1=ALU.add))
                ch.wait()

            normed_tokens(ffn[0])
            route_ffn(ffn[0], 0)

            dve.wait_ge(s_weights, 16 * (N_WEIGHTS - 1))
            dve.wait_ge(s_conv_ps, 1)
            V.tensor_tensor(wfold[:, :, 0:P], col(win_s[:, 0:P]).broadcast_to([P, TAPS, P]),
                            bank[6].rearrange("p (k c) -> p k c", k=TAPS), ALU.mult).then_inc(s_prepared, 1)
            V.memset(taps, 0.0).then_inc(m_taps, 1)
            for b in range(NB):
                V.tensor_scalar(diagD[:, b, :], ident[:, :], Dp_s[:, b:b + 1], None, ALU.mult).then_inc(
                    s_prepared, 1)
            ch.link(V.memset(xaT[:, :, 0:PAD], 0.0))

            def joined(g):
                gathered_group(ffn[0], g)
                for j in range(g * GT, (g + 1) * GT):
                    ch.step(tile_stats(X, j))
                ch.wait()

            def factors(g, n):
                norm_factors(slice(g * GT, (g + n) * GT), n * GT, twice=True)

            def normed_group(g):
                for q in range(GT):
                    last = normed(xs[:, 0, q, :], X, g * GT + q, rs2, nmr2)
                last.then_inc(m_turn.xs, 1)

            def turned_group(g):
                dve.wait_ge(m_turn.ps, g + 1)
                V.tensor_scalar(xaT[:, g * GB:(g + 1) * GB, PAD:SP_], bank[0].rearrange("p (q t) -> p q t", q=GB),
                                g1[:, 0:1], b1[:, 0:1], ALU.mult, ALU.add).then_inc(m_turn.xT, 1)

            for g in range(2):
                joined(g)
                factors(g, 1)
                normed_group(g)
                if g == 0:
                    turned_group(0)
            for g in range(2, NG, 2):
                joined(g)
                joined(g + 1)
                turned_group(g - 1)
                factors(g, 2)
                normed_group(g)
                turned_group(g)
                normed_group(g + 1)
            turned_group(NG - 1)

            def inner(i, s):
                dve.wait_ge(m_dt_ps, i * 2 + (s + 1))
                V.tensor_copy(dtT[0:R, s], bank[s][0:R, :]).then_inc(m_dt, 1)
                at = bass.ds(i * (2 * G) + s * G, G)
                bc, rest = bank[s][R:R + 2 * N, :], bcr[R:R + 2 * N, 0]
                ch.link(V.tensor_copy(bc_hi[:, :], bc))
                ch.step(V.tensor_copy(bc_parts[0:2 * N, at], bc_hi[:, :]))
                V.tensor_tensor(rest, bc, bc_hi[:, :], ALU.subtract).then_inc(m_bc_read, 1)
                dve.wait_ge(m_bc_read, i * 2 + (s + 3))
                ch.link(V.tensor_copy(bc_lo[:, :], rest))
                ch.step(V.tensor_copy(bc_parts[2 * N:4 * N, at], bc_lo[:, :]))
                V.tensor_tensor(bc_parts[4 * N:6 * N, at], rest, bc_lo[:, :], ALU.subtract).then_inc(m_bc, 1)
                dve.wait_ge(m_bc, i * 2 + (s + 1))

            def delta_x(g):
                at = bass.ds(g * G, G)
                dve.wait_ge(m_delta, g + 3)
                V.tensor_tensor(du[:, :, at], delta[:, :, at], xm[:, :, at], ALU.mult).then_inc(m_du, 1)

            with dve.Fori(0, NG // 2) as i:
                ch.loop(i, 2 * 4, NG // 2)
                for s in range(2):
                    inner(i, s)
            ch.end()
            dve.wait_ge(m_raw, NG + 2)
            V.memset(decay_ps[:, :, :, 0:G:S], 0.0).then_inc(c_h, 1)
            dve.wait_ge(c_h, 1)
            dve.sem_inc(c_h, 1)
            dve.sem_inc(c_dBu, 1)
            dve.sem_inc(c_gated, 1)

            def times_B(g, n):
                m = g * N + n
                dve.wait_ge(c_h, m + 1)
                dve.wait_ge(c_B, m + 1)
                V.tensor_tensor(dBu[n % 2], du[:, :, tokens_of(g, n)], col(bank[2]).broadcast_to([P, NB, G]),
                                ALU.mult).then_inc(c_dBu, 1)

            def scan(g, n):
                m = g * N + n
                dve.wait_ge(c_dBu, m + 2)
                dve.wait_ge(c_decay, m + 1)
                dve.wait_ge(c_y, m + 1)
                V.tensor_tensor_scan(h[:, n % 4].rearrange("p b t -> p (b t)"),
                                     decay_ps[:, n % 2].rearrange("p b t -> p (b t)"),
                                     dBu[n % 2].rearrange("p b t -> p (b t)"), 0.0, ALU.mult, ALU.add).then_inc(c_h, 1)

            def gated(g):
                dve.wait_ge(c_y, g * N + (N + 4))
                at = tokens_of(g, 0)
                for b in range(NB):
                    last = V.tensor_tensor(xm[:, b, at], bank[b], zs[:, b, at], ALU.mult)
                last.then_inc(c_gated, 1)

            dve.wait_ge(m_du, NG - 2)
            times_B(0, 0)
            delta_x(NG - 2)
            for n in range(2):
                times_B(0, n + 1)
                scan(0, n)
                if n == 0:
                    delta_x(NG - 1)
            dve.wait_ge(m_du, NG)
            with dve.Fori(0, NG - 1) as g:
                for n in range(2, N + 2):
                    times_B(g, n + 1)
                    scan(g, n)
                gated(g)
            for n in range(2, N):
                if n + 1 < N:
                    times_B(NG - 1, n + 1)
                scan(NG - 1, n)
            gated(NG - 1)

            with dve.Fori(0, NG // 2) as i:
                ch.loop(i, 2 * GT, NG // 2)
                for s in range(2):
                    dve.wait_ge(p_xl, i * 2 + (s + 1))
                    dve.wait_ge(p_out_ps, i * 2 + (s + 1))
                    xa = XA[:, bass.ds(i * (2 * GT) + s * GT, GT), :]
                    V.tensor_tensor(xa, xa, bank[s].rearrange("p (q d) -> p q d", q=GT), ALU.add).then_inc(p_xa, 1)
                    apart(dve, p_xa, i * 2 + (s + 3))
                    for q in range(GT):
                        ch.step(tile_stats(XA, i * (2 * GT) + (s * GT + q)))
            ch.end()
            ch.wait()
            norm_factors()

            def normed_group(g):
                for q in range(GT):
                    last = normed(xs[:, 0, q, :], XA, g * GT + q, rs, nmr)
                last.then_inc(d_turn.xs, 1)

            def turned_group(g):
                dve.wait_ge(d_turn.ps, g + 1)
                V.tensor_scalar(xsT[:, 0], bank[0], g2[:, 0:1], b2[:, 0:1], ALU.mult, ALU.add).then_inc(
                    d_turn.xT, 1)

            f = ffn[1]

            def dense_out(g, more):
                if more:
                    turned_group(g + 1)
                xt = X[:, bass.ds(g * GT, GT), :]
                dve.wait_ge(d_xa, g * 2 + 2)
                dve.wait_ge(d_y_ps, g + 1)
                V.tensor_tensor(xt, xt, bank[1].rearrange("p (q d) -> p q d", q=GT), ALU.add).then_inc(d_x, 1)
                apart(dve, d_x, g + 2)
                for q in range(GT):
                    ch.step(tile_stats(X, g * GT + q))
                if more > 1:
                    normed_group(g + 2)
                ch.wait()
                dve.sem_inc(s_passed, 1)
                norm_factors(bass.ds(g * GT, GT), GT)
                dve.wait_ge(f.copied, g + 1)
                apart(dve, f.turn.ps, g + 1)
                for q in range(GT):
                    last = normed(xs[:, 1, q, :], X, g * GT + q, rs, nmr)
                last.then_inc(f.turn.xs, 1)

            normed_group(0)
            turned_group(0)
            normed_group(1)
            with dve.Fori(0, NG - 2) as g:
                ch.loop(g, GT + FACTOR_STEPS, NG - 2)
                dense_out(g, 2)
            ch.end()
            dense_out(NG - 2, 1)
            dense_out(NG - 1, 0)
            route_ffn(ffn[1], 1)
            for g in range(NG):
                gathered_group(ffn[1], g)
                dve.sem_inc(ffn[1].added, 1)

        @block.tensor
        def _(pe_):
            mm, tr = nc.tensor.matmul, nc.tensor.transpose
            pe_.wait_ge(s_first_const, 1)
            pe_.wait_ge(s_attn_w, 32)
            pe_.sem_inc(a_fin, 2)

            def attend(n, c=0):
                s = (n + c) % 2 if isinstance(n, int) else c % 2
                r = 1 - s

                def has(k):
                    return not isinstance(n, int) or 0 <= n + c + k < B

                if has(-1):
                    pe_.wait_ge(a_exp, n + c)
                    for k in range(3):
                        last = tr(bank[6 + r][:, k * P:(k + 1) * P], pr_a[:, r, k * P:(k + 1) * P], ident[:, :])
                    last.then_inc(a_pT_ps, 1)
                if has(2):
                    pe_.wait_ge(a_xn, n + (c + 3))
                    for k in range(2):
                        last = tr(bank[s][:, k * P:(k + 1) * P], xn_a[:, s, k, :], ident[:, :])
                    last.then_inc(a_xT_ps, 1)
                if has(0):
                    pe_.wait_ge(a_uv, n + (c + 1))
                    pe_.wait_ge(a_fin, n + (c + 1))
                    mm(bank[4 + s][:, 0:P], uv_a[:, s, 0:P], xT_a[:, s, 0:P], start=True, stop=True)
                    mm(bank[4 + s][:, P:P + S], uv_a[:, s, P:S], xT_a[:, s, :], start=True,
                       stop=True).then_inc(a_sc_ps, 1)
                if has(-1):
                    pe_.wait_ge(a_pT, n + c)
                    v = [uv_a[:, r, S + k * P:S + (k + 1) * P] for k in range(2)]
                    mm(bank[4 + r][:, 0:P], pT_a[:, r, 0:P], v[0], start=True, stop=True)
                    mm(bank[4 + r][:, P:S], pT_a[:, r, P:2 * P], v[0], start=True, stop=False)
                    mm(bank[4 + r][:, P:S], pT_a[:, r, 2 * P:3 * P], v[1], start=False,
                       stop=True).then_inc(a_out_ps, 1)
                if has(1):
                    pe_.wait_ge(a_xT, n + (c + 2))
                    mm(bank[2 + r][:, 0:S], qk_s[:, :], xT_a[:, r], start=True, stop=True)
                    for k in range(2):
                        last = mm(bank[2 + r][:, S + k * P:S + (k + 1) * P], xT_a[:, r, k * P:(k + 1) * P],
                                  ov_s[:, :], start=True, stop=True)
                    last.then_inc(a_uv_ps, 1)

            for n in range(-2, FIRST):
                attend(n)
            with pe_.Fori(0, ATT_LOOP) as i:
                for c in range(2):
                    attend(i * 2, FIRST + c)
            for n in range(FIRST + 2 * ATT_LOOP, B + 1):
                attend(n)
            pe_.wait_ge(s_const, 1)
            pe_.wait_ge(s_weights, 16 * (N_WEIGHTS - 1))

            def logits_of(j, xT):
                o = bank[7][:, 0:E * NT].rearrange("p (e j) -> p e j", e=E)[:, :, bass.ds(j, 1)]
                return mm(o.rearrange("p e a -> p (e a)"), xT, Wg_s[:, :], start=True, stop=True)

            def normed_tokens(f):
                pe_.sem_inc(f.turn.ps, 2)

                def turned_group(i, s):
                    pe_.wait_ge(f.turn.xs, i * 2 + (s + 1))
                    for q in range(GT):
                        last = tr(bank[s][:, q * P:(q + 1) * P], xs[:, s, q, :], ident[:, :])
                    last.then_inc(f.turn.ps, 1)

                def logits(i, s):
                    for q in range(GT):
                        last = logits_of(i * (2 * GT) + (s * GT + q), xsT[:, s, q * P:(q + 1) * P])
                    last.then_inc(f.logits, 1)

                for s in range(2):
                    turned_group(0, s)
                with pe_.Fori(0, NG // 2 - 1) as i:
                    for s in range(2):
                        pe_.wait_ge(f.turn.xT, i * 2 + (s + 1))
                        turned_group(i + 1, s)
                        logits(i, s)
                for s in range(2):
                    pe_.wait_ge(f.turn.xT, NG - 2 + (s + 1))
                    logits(NG // 2 - 1, s)

            def route_ffn(f, n):
                pe_.wait_ge(f.to_turn, 1)
                for h in range(2):
                    last = tr(bank[4][:, h * P:(h + 1) * P],
                              prob.rearrange("p e (j h) -> p h (e j)", h=2)[:, h], ident[:, :])
                last.then_inc(f.turned, 1)
                for k in range(DIGITS):
                    pe_.wait_ge(f.flags, k + 1)
                    mm(bank[3][:, 0:3], same_expert[:, :], n_reached[:, :], start=True, stop=True).then_inc(
                        f.counts, 1)
                pe_.wait_ge(f.to_turn, 2)
                tr(bank[4][:, 0:P], thr_row, ident[:, :]).then_inc(f.turned, 1)
                pe_.wait_ge(f.flags, DIGITS + 1)
                mm(bank[3][:, 0:E], ones_b[:, :], cnt_b[:, :], start=True, stop=True).then_inc(f.counts, 1)
                flags = flag_b[:, :, :].rearrange("p e j -> p (e j)")
                for n_flags in (DIGITS + 2, DIGITS + 3):
                    pe_.wait_ge(f.flags, n_flags)
                    mm(bank[0][:, 0:E * NT], not_before_b[:, :], flags, start=True, stop=True)
                    mm(bank[1][:, 0:E * NT], ones_b[:, :], flags, start=True, stop=True).then_inc(f.counts, 1)
                pe_.wait_ge(f.tile_ids, 2)
                for j in range(NT):
                    if j % (NT // 4) == 0:
                        pe_.wait_ge(f.hot_place, j * 4 // NT + 1)
                    last = mm(bank[2][:, 0:2 * RT], hot_place[:, j, :], tile_ids[:, j].rearrange("p c k -> p (c k)"),
                              start=(j == 0), stop=(j == NT - 1))
                last.then_inc(f.source_ps, 1)
                pe_.wait_ge(f.routed, 2)
                pe_.wait_ge(s_experts[n], 16 * (1 + FC))
                pe_.sem_inc(f.y, 1)

                def turned_tiles(m, u):
                    pe_.wait_ge(f.loaded[u], m * 48 + 48)
                    for s in range(3):
                        last = tr(bank[6][:, s * P:(s + 1) * P], xin[:, u, s, :], ident[:, :])
                    last.then_inc(f.x_ps, 1)

                def tiles(m, u, more=True):
                    i = m * 2 + u
                    pe_.wait_ge(f.x, i + 1)
                    for s in range(3):
                        for c in range(FC):
                            last = mm(bank[s][:, c * P:(c + 1) * P], W1x[:, s, c * P:(c + 1) * P], rxT[:, s],
                                      start=True, stop=True)
                        last.then_inc(f.h_ps, 1)
                    if more:
                        turned_tiles(m + u, 1 - u)
                    three = pe_.value_load(etab[0:1, bass.ds(i, 1)], min_val=0, max_val=E ** 3 - 1)
                    who = [three % E, three // E % E, three // (E * E)]
                    pe_.wait_ge(f.y, i + 1)
                    for s in range(3):
                        pe_.wait_ge(f.h, i * 3 + (s + 1))
                        for c in range(FC):
                            last = mm(bank[7][:, s * P:(s + 1) * P], rhT[:, s, c * P:(c + 1) * P],
                                      W2s[:, bass.ds(who[s], 1), c, :].rearrange("p a d -> p (a d)"),
                                      start=(c == 0), stop=(c == FC - 1))
                    last.then_inc(f.y_ps, 1)

                turned_tiles(0, 0)
                with pe_.Fori(0, RT // 6) as m:
                    for u in range(2):
                        tiles(m, u)
                tiles(RT // 6, 0, more=False)
                pe_.wait_ge(f.y, RT // 3 + 1)

            normed_tokens(ffn[0])
            route_ffn(ffn[0], 0)

            for k in range(TAPS):
                last = mm(bank[6][:, k * P:(k + 1) * P], ones_row[0:1, :], wconv_row[0:1, k, 0:P], start=True,
                          stop=True)
            last.then_inc(s_conv_ps, 1)
            pe_.wait_ge(s_prepared, 1 + NB)

            def turned_group(turn, g):
                pe_.wait_ge(turn.xs, g + 1)
                for q in range(GT):
                    last = tr(bank[0][:, q * P:(q + 1) * P], xs[:, 0, q, :], ident[:, :])
                last.then_inc(turn.ps, 1)

            pe_.sem_inc(m_xc, 1)
            pe_.sem_inc(m_z, 1)

            def in_proj(g, more):
                seqs = bass.ds(g * GB, GB)
                pe_.wait_ge(m_turn.xT, g + 1)
                pe_.wait_ge(m_taps, g + 2)
                mm(bank[3], win_s[:, P:2 * P], xaT[:, seqs, PAD:SP_], start=True, stop=True).then_inc(m_x1_ps, 1)
                pe_.wait_ge(m_xc, g + 1)
                for k in range(TAPS):
                    last = mm(bank[2], wfold[:, k, 0:P], xaT[:, seqs, k:k + S], start=(k == 0), stop=(k == TAPS - 1))
                last.then_inc(m_xc_ps, 1)
                if more:
                    turned_group(m_turn, g + 1)
                pe_.wait_ge(m_z, g + 1)
                for b in range(NB):
                    last = mm(bank[4 + b], win_s[:, DI + b * P:DI + (b + 1) * P], xaT[:, seqs, PAD:SP_],
                              start=True, stop=True)
                last.then_inc(m_z_ps, 1)

            turned_group(m_turn, 0)
            with pe_.Fori(0, NG - 1) as g:
                in_proj(g, True)
            in_proj(NG - 1, False)
            pe_.wait_ge(m_xc, NG + 1)
            pe_.wait_ge(m_taps, NG + 2)

            pe_.sem_inc(m_bc_read, 2)
            pe_.sem_inc(m_raw, 2)

            def project(i, s):
                at = bass.ds(i * (2 * G) + s * G, G)
                pe_.wait_ge(m_x1, i * 2 + (s + 1))
                pe_.wait_ge(m_bc_read, i * 2 + (s + 1))
                for b in range(NB):
                    last = mm(bank[s][0:R + 2 * N, :], wx_s[:, b, :], xm[:, b, at], start=(b == 0),
                              stop=(b == NB - 1))
                last.then_inc(m_dt_ps, 1)

            def to_raw(i, s):
                pe_.wait_ge(m_z, NG + 1)
                pe_.wait_ge(m_dt, i * 2 + (s + 1))
                pe_.wait_ge(m_raw, i * 2 + (s + 1))
                for b in range(NB):
                    last = mm(bank[4 + 2 * s + b], wdt_s[:, b * P:(b + 1) * P], dtT[0:R, s], start=True, stop=True)
                last.then_inc(m_raw_ps, 1)

            def projections(i, more):
                project(i, 1)
                to_raw(i, 0)
                if more:
                    project(i + 1, 0)
                to_raw(i, 1)

            project(0, 0)
            with pe_.Fori(0, NG // 2 - 1) as i:
                projections(i, True)
            projections(NG // 2 - 1, False)
            pe_.wait_ge(m_bc, NG)
            pe_.wait_ge(m_bc_read, NG + 2)
            pe_.sem_inc(c_y, 4)

            def pick_B(g, n):
                pe_.wait_ge(c_dBu, g * N + (n + 1))
                mm(bank[2], pick[:, n % N, :], bc_parts[:, tokens_of(g, n)], start=True, stop=True).then_inc(c_B, 1)

            def pick_C(g, n):
                if n > 0:
                    pe_.wait_ge(c_C_sb, g * N + n)
                mm(bank[3], pick[:, N + n % N, :], bc_parts[:, tokens_of(g, n)], start=True, stop=True).then_inc(
                    c_C, 1)

            def start_sum(g):
                pe_.wait_ge(c_gated, g + 1)
                for b in range(NB):
                    mm(bank[b], diagD[:, b, :], xm[:, b, tokens_of(g, 0)], start=True, stop=False)

            def sum_state(g, n):
                pe_.wait_ge(c_hC, g * N + (n + 3))
                for b in range(NB):
                    last = mm(bank[b], ident[:, :], h[:, n % 4, b, :], start=False, stop=(n == N - 1))
                last.then_inc(c_y, 1)

            LATE = N // 2 + 2

            def states(g, n, picked):
                if n == 2:
                    start_sum(g)
                first = 2 <= n < LATE
                if not first and n >= 2:
                    sum_state(g, n - 2)
                if n + 2 < picked:
                    pick_B(g, n + 2)
                if n + 1 < picked:
                    pick_C(g, n + 1)
                if first:
                    sum_state(g, n - 2)

            pick_B(0, 0)
            pick_C(0, 0)
            pick_B(0, 1)
            for n in range(2):
                states(0, n, N)
            with pe_.Fori(0, NG - 1) as g:
                for n in range(2, N + 2):
                    states(g, n, 2 * N)
            for n in range(2, N + 2):
                states(NG - 1, n, N)

            for s in range(2):
                pe_.sem_inc(p_xa, 1)
            with pe_.Fori(0, NG // 2) as i:
                for s in range(2):
                    pe_.wait_ge(p_yg, i * 2 + (s + 1))
                    for q in range(GT):
                        for b in range(NB):
                            last = mm(bank[s][:, q * P:(q + 1) * P], ygs[:, s, b, q * P:(q + 1) * P], wout_s[:, b, :],
                                      start=(b == 0), stop=(b == NB - 1))
                    last.then_inc(p_out_ps, 1)

            pe_.sem_inc(d_x, 1)

            def dense(g, more, behind):
                pe_.wait_ge(d_turn.xT, g + 1)
                for c in range(FFC):
                    mm(bank[2 + c], wff1_s[:, c * P:(c + 1) * P], xsT[:, 0], start=True,
                       stop=True).then_inc(d_h_ps, 1)
                    if c == 0 and behind > 1:
                        logits(g - 2)
                if more:
                    turned_group(d_turn, g + 1)
                pe_.wait_ge(d_x, g + 1)
                for q in range(GT):
                    for c in range(FFC):
                        if q == 0:
                            pe_.wait_ge(d_h, g * FFC + (c + 1))
                        last = mm(bank[1][:, q * P:(q + 1) * P], hT[:, c, q * P:(q + 1) * P], wff2_s[:, c, :],
                                  start=(c == 0), stop=(c == FFC - 1))
                last.then_inc(d_y_ps, 1)
                if behind > 0:
                    normed_group(g - 1)

            def normed_group(g):
                pe_.wait_ge(ffn[1].turn.xs, g + 1)
                for q in range(GT):
                    last = tr(bank[6][:, q * P:(q + 1) * P], xs[:, 1, q, :], ident[:, :])
                last.then_inc(ffn[1].turn.ps, 1)

            def logits(g):
                pe_.wait_ge(ffn[1].turn.xT, g + 1)
                for q in range(GT):
                    last = logits_of(g * GT + q, xsT[:, 1, q * P:(q + 1) * P])
                last.then_inc(ffn[1].logits, 1)

            pe_.sem_inc(ffn[1].turn.ps, 1)
            turned_group(d_turn, 0)
            dense(0, True, 0)
            dense(1, True, 1)
            with pe_.Fori(2, NG - 1) as g:
                dense(g, True, 2)
            dense(NG - 1, False, 2)
            logits(NG - 2)
            normed_group(NG - 1)
            logits(NG - 1)
            route_ffn(ffn[1], 1)


_INS = ["L0_attn_a_input_data", "L0_attn_a_qk", "L0_attn_a_ov", "L0_attn_b_ln1_g", "L0_attn_b_ln1_b",
        "L0_attn_b_w_in", "L0_attn_b_w_conv", "L0_attn_b_b_conv", "L0_attn_b_w_xproj", "L0_attn_b_w_dt",
        "L0_attn_b_b_dt", "L0_attn_b_A_log", "L0_attn_b_Dp", "L0_attn_b_w_out", "L0_attn_b_ln2_g",
        "L0_attn_b_ln2_b", "L0_attn_b_w_ff1", "L0_attn_b_b_ff1", "L0_attn_b_w_ff2", "L0_attn_b_b_ff2",
        "L0_ffn_Wg", "L0_ffn_W1", "L0_ffn_W2"]


def kernel(**inputs):
    import numpy as _np
    import concourse.bacc as _bacc
    from concourse import mybir as _mybir
    from concourse.bass_utils import run_bass_kernel_spmd as _run

    nc = _bacc.Bacc("TRN2", target_bir_lowering=False, num_devices=1)
    arrays, args = {}, []
    for name in _INS:
        a = _np.ascontiguousarray(inputs[name])
        arrays[f"in_{name}"] = a
        args.append(nc.dram_tensor(f"in_{name}", a.shape, _mybir.dt.from_np(a.dtype), kind="ExternalInput").ap())
    shape = inputs["L0_attn_a_input_data"].shape
    tokens, experts = shape[0] * shape[1], inputs["L0_ffn_Wg"].shape[1]
    rows = (tokens + experts * (P - 1)) // P * P
    args.append(nc.dram_tensor("out_0", shape, _mybir.dt.float32, kind="ExternalOutput").ap())
    for name, n in (("normed_rows", tokens), ("routed_out", rows)):
        args.append(nc.dram_tensor(name, (n, shape[2]), _mybir.dt.float32, kind="Internal").ap())
    hybrid_kernel(nc, *args)
    r = _run(nc, [arrays], core_ids=[0])
    return r.results[0]["out_0"]
```
